# Optimizing a Trainium2 kernel written in Bass

```python
import numpy as np
import jax
import jax.numpy as jnp

def _softmax(x, axis=-1):
    return jax.nn.softmax(x, axis=axis)

def _gelu(x):
    return jax.nn.gelu(x, approximate=True)

def _silu(x):
    return jax.nn.silu(x)

def _sigmoid(x):
    return jax.nn.sigmoid(x)

def _layernorm(x, axis=-1, eps=1e-05):
    m = jnp.mean(x, axis=axis, keepdims=True)
    v = jnp.var(x, axis=axis, keepdims=True)
    return (x - m) / jnp.sqrt(v + eps)

def _scatter_add(tgt, idx, src, axis=0):
    return tgt.at[idx].add(src)

def _segment_sum(src, seg, n):
    return jax.ops.segment_sum(src, seg, n)
kernel_name = 'mk_hybrid_d1_jaxref_r8_65cbdb'

def setup_inputs(seed: int=0):
    np.random.seed(seed)
    _w = jnp.asarray

    def _L0_attn_a_setup():
        import jax, jax.numpy as jnp
        import numpy as np
        from math import sqrt
        HEADS = 16
        DIM_HEAD = 64
        BETA = 1.0 / sqrt(DIM_HEAD)
        key = jax.random.key(seed)
        k1, k2, k3 = jax.random.split(key, 3)
        b, n, dim = (2, 256, 128)
        inner = HEADS * DIM_HEAD
        x = jax.random.normal(k1, (b, n, dim), dtype=jnp.float32)
        W_qk = jax.random.normal(k2, (dim, 2 * inner), dtype=jnp.float32) * 0.02
        W_out = jax.random.normal(k3, (inner, dim), dtype=jnp.float32) * 0.02
        return {'x': x, 'W_qk': W_qk, 'W_out': W_out}
    _L0_attn_a_in = _L0_attn_a_setup()

    def _L0_attn_b_setup():
        import jax, jax.numpy as jnp
        import numpy as np
        D_MODEL = 128
        EXPAND = 2
        INNER = D_MODEL * EXPAND
        D_STATE = 64
        K = 3
        BSZ = 2
        SEQ = 512
        key = jax.random.key(seed)
        ks = jax.random.split(key, 12)
        s = 0.02

        def w(k, shape):
            return jax.random.normal(k, shape, jnp.float32) * s
        return {'x': jax.random.normal(ks[0], (BSZ, SEQ, D_MODEL), jnp.float32), 'W_in': w(ks[1], (D_MODEL, 2 * INNER)), 'b_in': jnp.zeros((2 * INNER,), jnp.float32), 'conv_w': w(ks[2], (INNER, K)), 'conv_b': jnp.zeros((INNER,), jnp.float32), 'W_dt': w(ks[3], (INNER, D_STATE)), 'b_dt': jnp.zeros((D_STATE,), jnp.float32), 'W_B': w(ks[4], (INNER, D_STATE)), 'b_B': jnp.zeros((D_STATE,), jnp.float32), 'W_C': w(ks[5], (INNER, D_STATE)), 'b_C': jnp.zeros((D_STATE,), jnp.float32), 'W_si': w(ks[6], (D_STATE, INNER)), 'b_si': jnp.zeros((INNER,), jnp.float32), 'D': jnp.ones((INNER,), jnp.float32), 'W_out': w(ks[7], (INNER, D_MODEL)), 'b_out': jnp.zeros((D_MODEL,), jnp.float32)}
    _L0_attn_b_in = _L0_attn_b_setup()

    def _L0_ffn_setup():
        import jax, jax.numpy as jnp
        import numpy as np
        B, S, D = (2, 256, 128)
        I = 64
        E = 16
        TOP_K = 2

        def _mlp(x, wg, wu, wd):
            return jnp.einsum('bsi,id->bsd', jax.nn.silu(x @ wg) * (x @ wu), wd)
        key = jax.random.key(seed)
        ks = jax.random.split(key, 10)
        sc_d = 1.0 / np.sqrt(D)
        sc_i = 1.0 / np.sqrt(I)
        return {'x': jax.random.normal(ks[0], (B, S, D), dtype=jnp.float32), 'gate_w': jax.random.normal(ks[1], (D, E), dtype=jnp.float32) * sc_d, 'gate_b': jnp.zeros((E,), dtype=jnp.float32), 'shared_wg': jax.random.normal(ks[2], (D, I), dtype=jnp.float32) * sc_d, 'shared_wu': jax.random.normal(ks[3], (D, I), dtype=jnp.float32) * sc_d, 'shared_wd': jax.random.normal(ks[4], (I, D), dtype=jnp.float32) * sc_i, 'experts_wg': jax.random.normal(ks[5], (E, D, I), dtype=jnp.float32) * sc_d, 'experts_wu': jax.random.normal(ks[6], (E, D, I), dtype=jnp.float32) * sc_d, 'experts_wd': jax.random.normal(ks[7], (E, I, D), dtype=jnp.float32) * sc_i}
    _L0_ffn_in = _L0_ffn_setup()
    _d = {'L0_attn_a_x': _L0_attn_a_in['x'], 'L0_attn_a_W_qk': _L0_attn_a_in['W_qk'], 'L0_attn_a_W_out': _L0_attn_a_in['W_out'], 'L0_attn_b_W_in': _L0_attn_b_in['W_in'], 'L0_attn_b_b_in': _L0_attn_b_in['b_in'], 'L0_attn_b_conv_w': _L0_attn_b_in['conv_w'], 'L0_attn_b_conv_b': _L0_attn_b_in['conv_b'], 'L0_attn_b_W_dt': _L0_attn_b_in['W_dt'], 'L0_attn_b_b_dt': _L0_attn_b_in['b_dt'], 'L0_attn_b_W_B': _L0_attn_b_in['W_B'], 'L0_attn_b_b_B': _L0_attn_b_in['b_B'], 'L0_attn_b_W_C': _L0_attn_b_in['W_C'], 'L0_attn_b_b_C': _L0_attn_b_in['b_C'], 'L0_attn_b_W_si': _L0_attn_b_in['W_si'], 'L0_attn_b_b_si': _L0_attn_b_in['b_si'], 'L0_attn_b_D': _L0_attn_b_in['D'], 'L0_attn_b_W_out': _L0_attn_b_in['W_out'], 'L0_attn_b_b_out': _L0_attn_b_in['b_out'], 'L0_ffn_gate_w': _L0_ffn_in['gate_w'], 'L0_ffn_gate_b': _L0_ffn_in['gate_b'], 'L0_ffn_shared_wg': _L0_ffn_in['shared_wg'], 'L0_ffn_shared_wu': _L0_ffn_in['shared_wu'], 'L0_ffn_shared_wd': _L0_ffn_in['shared_wd'], 'L0_ffn_experts_wg': _L0_ffn_in['experts_wg'], 'L0_ffn_experts_wu': _L0_ffn_in['experts_wu'], 'L0_ffn_experts_wd': _L0_ffn_in['experts_wd']}
    _x0 = _d['L0_attn_a_x']
    _d['L0_attn_a_x'] = jax.random.normal(jax.random.fold_in(jax.random.key(seed), 1), (2, 1024, 128), dtype=_x0.dtype)
    del _x0
    return _d

def reference(L0_attn_a_x, L0_attn_a_W_qk, L0_attn_a_W_out, L0_attn_b_W_in, L0_attn_b_b_in, L0_attn_b_conv_w, L0_attn_b_conv_b, L0_attn_b_W_dt, L0_attn_b_b_dt, L0_attn_b_W_B, L0_attn_b_b_B, L0_attn_b_W_C, L0_attn_b_b_C, L0_attn_b_W_si, L0_attn_b_b_si, L0_attn_b_D, L0_attn_b_W_out, L0_attn_b_b_out, L0_ffn_gate_w, L0_ffn_gate_b, L0_ffn_shared_wg, L0_ffn_shared_wu, L0_ffn_shared_wd, L0_ffn_experts_wg, L0_ffn_experts_wu, L0_ffn_experts_wd):

    def _L0_attn_a_ref(x, W_qk, W_out):
        import jax, jax.numpy as jnp
        import numpy as np
        from math import sqrt
        HEADS = 16
        DIM_HEAD = 64
        BETA = 1.0 / sqrt(DIM_HEAD)
        b, n, _ = x.shape
        qk = x @ W_qk
        q, k = jnp.split(qk, 2, axis=-1)
        q = q.reshape(b, n, HEADS, DIM_HEAD).transpose(0, 2, 1, 3)
        k = k.reshape(b, n, HEADS, DIM_HEAD).transpose(0, 2, 1, 3)
        scores = jnp.einsum('bhid,bhjd->bhij', q * BETA, k)
        mask_value = -jnp.finfo(scores.dtype).max
        causal_mask = jnp.triu(jnp.ones((n, n), dtype=bool), k=1)
        scores = jnp.where(causal_mask, mask_value, scores)
        attn = jax.nn.softmax(scores, axis=-1)
        out = jnp.einsum('bhij,bhjd->bhid', attn, k)
        out = out.transpose(0, 2, 1, 3).reshape(b, n, HEADS * DIM_HEAD)
        return out @ W_out

    def _L0_attn_b_ref(x, W_in, b_in, conv_w, conv_b, W_dt, b_dt, W_B, b_B, W_C, b_C, W_si, b_si, D, W_out, b_out):
        import jax, jax.numpy as jnp
        import numpy as np
        D_MODEL = 128
        EXPAND = 2
        INNER = D_MODEL * EXPAND
        D_STATE = 64
        K = 3
        BSZ = 2
        SEQ = 512
        bsz, seq_len, _ = x.shape
        inner = W_in.shape[1] // 2
        k = conv_w.shape[1]
        xz = x @ W_in + b_in
        x_main, gate = (xz[..., :inner], xz[..., inner:])
        lhs = jnp.transpose(x_main, (0, 2, 1))
        rhs = conv_w[:, None, :]
        conv = jax.lax.conv_general_dilated(lhs, rhs, window_strides=(1,), padding=[(k - 1, 0)], dimension_numbers=('NCH', 'OIH', 'NCH'), feature_group_count=inner)
        x_main = jnp.transpose(conv, (0, 2, 1)) + conv_b
        x_main = jax.nn.silu(x_main)
        dt = jax.nn.sigmoid(x_main @ W_dt + b_dt)
        Bm = x_main @ W_B + b_B
        Cm = x_main @ W_C + b_C

        def step(state, inp):
            dt_t, B_t, C_t = inp
            state = (1.0 - dt_t) * state + dt_t * B_t
            return (state, C_t * state)
        xs = (jnp.moveaxis(dt, 1, 0), jnp.moveaxis(Bm, 1, 0), jnp.moveaxis(Cm, 1, 0))
        state0 = jnp.zeros((bsz, dt.shape[-1]), x.dtype)
        _, y = jax.lax.scan(step, state0, xs)
        y = jnp.moveaxis(y, 0, 1)
        mu = jnp.mean(y, axis=-1, keepdims=True)
        var = jnp.var(y, axis=-1, keepdims=True)
        y = (y - mu) * jax.lax.rsqrt(var + 1e-05)
        y = y @ W_si + b_si
        y = y + D * x_main
        y = y * jax.nn.sigmoid(gate)
        return y @ W_out + b_out

    def _L0_ffn_ref(x, gate_w, gate_b, shared_wg, shared_wu, shared_wd, experts_wg, experts_wu, experts_wd):
        import jax, jax.numpy as jnp
        import numpy as np
        B, S, D = (2, 256, 128)
        I = 64
        E = 16
        TOP_K = 2

        def _mlp(x, wg, wu, wd):
            return jnp.einsum('bsi,id->bsd', jax.nn.silu(x @ wg) * (x @ wu), wd)
        router_logits = jax.nn.sigmoid(x @ gate_w + gate_b)
        expert_values, expert_indices = jax.lax.top_k(router_logits, k=TOP_K)
        expert_values = expert_values / jnp.sum(expert_values, axis=-1, keepdims=True)
        hg = jnp.einsum('bsd,edi->bsei', x, experts_wg)
        hu = jnp.einsum('bsd,edi->bsei', x, experts_wu)
        all_outputs = jnp.einsum('bsei,eid->bsed', jax.nn.silu(hg) * hu, experts_wd)
        selected = jnp.take_along_axis(all_outputs, expert_indices[..., None], axis=2)
        expert_weighted = jnp.sum(expert_values[..., None] * selected, axis=2)
        return x + _mlp(x, shared_wg, shared_wu, shared_wd) + expert_weighted
    x = L0_attn_a_x
    x = x + _L0_attn_a_ref(_layernorm(x, axis=-1), L0_attn_a_W_qk, L0_attn_a_W_out)
    x = x + _L0_ffn_ref(_layernorm(x, axis=-1), L0_ffn_gate_w, L0_ffn_gate_b, L0_ffn_shared_wg, L0_ffn_shared_wu, L0_ffn_shared_wd, L0_ffn_experts_wg, L0_ffn_experts_wu, L0_ffn_experts_wd)
    x = x + _L0_attn_b_ref(_layernorm(x, axis=-1), L0_attn_b_W_in, L0_attn_b_b_in, L0_attn_b_conv_w, L0_attn_b_conv_b, L0_attn_b_W_dt, L0_attn_b_b_dt, L0_attn_b_W_B, L0_attn_b_b_B, L0_attn_b_W_C, L0_attn_b_b_C, L0_attn_b_W_si, L0_attn_b_b_si, L0_attn_b_D, L0_attn_b_W_out, L0_attn_b_b_out)
    x = x + _L0_ffn_ref(_layernorm(x, axis=-1), L0_ffn_gate_w, L0_ffn_gate_b, L0_ffn_shared_wg, L0_ffn_shared_wu, L0_ffn_shared_wd, L0_ffn_experts_wg, L0_ffn_experts_wu, L0_ffn_experts_wd)
    return x

_drawn_inputs = setup_inputs


def setup_inputs(seed=0):
    import zlib

    import numpy as np

    out = dict(_drawn_inputs(seed))
    spreads = {'L0_attn_b_b_in': (0.0, 0.8),
     'L0_attn_b_conv_b': (0.0, 0.592),
     'L0_attn_b_b_dt': (0.0, 2.0),
     'L0_attn_b_b_B': (0.0, 0.996),
     'L0_attn_b_b_C': (0.0, 1.556),
     'L0_attn_b_b_si': (0.0, 0.449),
     'L0_attn_b_D': (1.0, 0.6),
     'L0_attn_b_b_out': (0.0, 0.1),
     'L0_ffn_gate_b': (0.0, 0.1)}
    factors = {'L0_attn_b_W_in': 8.0,
     'L0_attn_b_conv_w': 8.0,
     'L0_attn_b_W_dt': 30.704,
     'L0_attn_b_W_B': 8.0,
     'L0_attn_b_W_C': 8.0,
     'L0_attn_b_W_si': 2.975}
    for name, (base, spread) in spreads.items():
        noise = np.random.default_rng([zlib.crc32(name.encode()), seed]).standard_normal(out[name].shape)
        drawn = base * np.exp(spread * noise) if base else spread * noise
        out[name] = jnp.asarray(drawn.astype(out[name].dtype))
    for name, factor in factors.items():
        out[name] = (out[name] * factor).astype(out[name].dtype)
    return out
```

```python
from contextlib import ExitStack

import concourse.bass as bass
from concourse import mybir

FP32 = mybir.dt.float32
F32R = mybir.dt.float32r
BF16 = mybir.dt.bfloat16
I32 = mybir.dt.int32
ALU = mybir.AluOpType
ACT = mybir.ActivationFunctionType
AX = mybir.AxisListType

P = 128
BATCH, SEQ, D = 2, 1024, 128
TOKENS = BATCH * SEQ
TILES = TOKENS // P
BANK = 512
GROUPS = TOKENS // BANK
PER = BANK // P
EPS = 1e-5

HEADS, DH = 16, 64
PAIRS = HEADS // 2
QT = SEQ // P
BETA = DH ** -0.5
MASKED = -3.0e38

EXPERTS, INTER = 16, 64
STEPS = EXPERTS // 2 + 1

INNER, STATE, TAPS = 256, 64, 3


def wait(eng, sem, value):
    if not isinstance(value, int) or value > 0:
        eng.wait_ge(sem, value)


def bcast(ap, n):
    return ap.unsqueeze(2).to_broadcast([ap.shape[0], ap.shape[1], n])


class Scope:

    def __init__(self, nc, tag):
        self.nc, self.tag, self.stack = nc, tag, ExitStack()

    def __enter__(self):
        self.stack.__enter__()
        return self

    def __exit__(self, *a):
        return self.stack.__exit__(*a)

    def sb(self, name, shape, dt=FP32):
        return self.stack.enter_context(self.nc.sbuf_tensor(f"{self.tag}_{name}", shape, dt))

    def ps(self, name, n=1):
        banks = [self.stack.enter_context(self.nc.psum_tensor(f"{self.tag}_{name}{i}", [P, BANK], FP32))
                 for i in range(n)]
        return banks if n > 1 else banks[0]

    def sem(self, name):
        return self.stack.enter_context(self.nc.semaphore(f"{self.tag}_{name}"))


def layernorm_transposed(nc, tag, k, residual=None, load=None):
    with Scope(nc, tag) as s:
        tp = s.ps("tp", GROUPS)
        sq = s.sb("sq", [P, TILES, D])
        tot = s.sb("tot", [P, TILES])
        mean = s.sb("mean", [P, TILES])
        var = s.sb("var", [P, TILES])
        sd = s.sb("sd", [P, TILES])
        rstd = s.sb("rstd", [P, TILES])
        x_loaded = [s.sem(f"x_loaded{n}") for n in range(GROUPS)]
        summed, centred, squared = s.sem("summed"), s.sem("centred"), s.sem("squared")
        meaned, varied, rooted = s.sem("meaned"), s.sem("varied"), s.sem("rooted")
        inverted, normed = s.sem("inverted"), s.sem("normed")
        transposed, high, low = s.sem("transposed"), s.sem("high"), s.sem("low")

        def grp(t, n):
            return t[:, n * PER:(n + 1) * PER, :]

        def cols(t, n):
            return t[:, n * PER:(n + 1) * PER]

        with nc.Block() as block:
            if load:
                @block.sync
                def _(sp):
                    load(sp, x_loaded)

            @block.vector
            def _(dve):
                for n in range(GROUPS):
                    if load:
                        dve.wait_ge(x_loaded[n], 16)
                    dve.reduce_sum(cols(tot, n), grp(k.x, n), AX.X).then_inc(summed, 1)
                dve.wait_ge(summed, GROUPS)
                dve.tensor_scalar(mean[:, :], tot[:, :], 1.0 / D, None, ALU.mult).then_inc(meaned, 1)
                dve.wait_ge(meaned, 1)
                for n in range(GROUPS):
                    dve.tensor_tensor(grp(k.xn, n), grp(k.x, n), bcast(cols(mean, n), D),
                                      ALU.subtract).then_inc(centred, 1)
                for n in range(GROUPS):
                    dve.wait_ge(squared, n + 1)
                    dve.reduce_sum(cols(tot, n), grp(sq, n), AX.X).then_inc(summed, 1)
                dve.wait_ge(summed, 2 * GROUPS)
                dve.tensor_scalar(var[:, :], tot[:, :], 1.0 / D, EPS, ALU.mult, ALU.add).then_inc(varied, 1)
                dve.wait_ge(rooted, 1)
                dve.reciprocal(rstd[:, :], sd[:, :]).then_inc(inverted, 1)
                dve.wait_ge(inverted, 1)
                for n in range(GROUPS):
                    dve.tensor_tensor(grp(k.xn, n), grp(k.xn, n), bcast(cols(rstd, n), D),
                                      ALU.mult).then_inc(normed, 1)
                for n in range(GROUPS):
                    dve.wait_ge(high, n + 1)
                    c = slice(n * BANK, (n + 1) * BANK)
                    dve.tensor_tensor(k.xlo[:, c], tp[n][:, :], k.xhi[:, c].bitcast(FP32),
                                      ALU.subtract).then_inc(low, 1)
                if residual is not None:
                    dve.wait_ge(normed, GROUPS)
                    dve.tensor_tensor(residual[:, :, :], k.x[:, :, :], k.xn[:, :, :], ALU.add)

            @block.scalar
            def _(act):
                for n in range(GROUPS):
                    act.wait_ge(centred, n + 1)
                    act.activation(grp(sq, n), grp(k.xn, n), ACT.Square).then_inc(squared, 1)
                act.wait_ge(varied, 1)
                act.activation(sd[:, :], var[:, :], ACT.Sqrt).then_inc(rooted, 1)
                for n in range(GROUPS):
                    act.wait_ge(transposed, n + 1)
                    act.activation(k.xhi[:, n * BANK:(n + 1) * BANK], tp[n][:, :], ACT.Copy).then_inc(high, 1)

            @block.tensor
            def _(pe):
                for n in range(GROUPS):
                    pe.wait_ge(normed, n + 1)
                    for j in range(PER):
                        last = pe.transpose(tp[n][:, j * P:(j + 1) * P], k.xn[:, n * PER + j, :], k.ident[:, :])
                    last.then_inc(transposed, 1)


HALF = QT // 2
SCORE_CHUNKS = [(j, j, HALF) for j in range(HALF)] + [(j, max(j, HALF), QT) for j in range(QT)]
NCHUNK = len(SCORE_CHUNKS)
CHUNK_AT = [P * sum(b - a for _, a, b in SCORE_CHUNKS[:c]) for c in range(NCHUNK + 1)]
DIAGONAL = [c for c, (j, a, _) in enumerate(SCORE_CHUNKS) if a == j]
FIRST_HALF_STEPS = HALF
MAX_CHUNKS = [(i, 0, i + 1) for i in range(HALF)]
for _i in range(HALF, QT):
    MAX_CHUNKS += [(_i, 0, HALF), (_i, HALF, _i + 1)]
NMAX = len(MAX_CHUNKS)
MAX_PER_STEP = [2, 2, 2, 1, 1, 1, 1, 1, 1, 0, 0, 0]
MAX_FIRST = [sum(MAX_PER_STEP[:c]) for c in range(NCHUNK)]
PROJ_STEPS = [0, 2, 4, 6]
KNAT_STEPS = [2, 5]
MROW_STEP = 10
PROLOGUE_FILLS = 7
BODY_FILLS = [5, 3, 5, 3]


def attention(nc, k, w_qk):
    with Scope(nc, "at") as s:
        def four(name):
            return [[s.sb(f"{name}{u}{l}", [P, SEQ], F32R) for l in range(2)] for u in range(2)]
        qs, ks, q2, k2 = four("qs"), four("ks"), four("q2"), four("k2")
        probs = s.sb("probs", [P, CHUNK_AT[-1]])
        k_nat = [s.sb(f"k_nat{u}", [P, QT, 3, DH]) for u in range(2)]
        k_t = s.sb("k_t", [P, SEQ])
        w_raw = s.sb("w_raw", [P, 2, P])
        w_hi = s.sb("w_hi", [P, 2, P], F32R)
        w_lo = s.sb("w_lo", [P, 2, P], F32R)
        inv = s.sb("inv", [P, 2, BANK])
        row_max = s.sb("row_max", [P, 2, QT])
        half_max = s.sb("half_max", [P, 2, QT - HALF, 2])
        neg_block = s.sb("neg_block", [QT, QT, P])
        maskb = s.sb("maskb", [P, P], BF16)
        identb = s.sb("identb", [P, P], BF16)
        max_ps, sc_ps, out_ps, misc = s.ps("max", 2), s.ps("sc", 2), s.ps("out", 2), s.ps("misc", 2)

        consts, rows_set, pool_turns = s.sem("consts"), s.sem("rows_set"), s.sem("pool_turns")
        w_loaded, w_split = s.sem("w_loaded"), s.sem("w_split")
        proj_ready, knat_ps_ready = s.sem("proj_ready"), s.sem("knat_ps_ready")
        hi_done, lo_done, dup_done = s.sem("hi_done"), s.sem("lo_done"), s.sem("dup_done")
        kt_done, knat_done = s.sem("kt_done"), s.sem("knat_done")
        max_ready, max_taken = s.sem("max_ready"), s.sem("max_taken")
        row_max_done, row_max_t, mrow_done = s.sem("row_max_done"), s.sem("row_max_t"), s.sem("mrow_done")
        scores_ready, exp_done, masked = s.sem("scores_ready"), s.sem("exp_done"), s.sem("masked")
        av_done, ln_done = s.sem("av_done"), s.sem("ln_done")
        inv_done, out_used = s.sem("inv_done"), s.sem("out_used")

        wq_view = w_qk.rearrange("d (a c) -> d a c", a=2)

        def rows(l):
            return slice(DH * l, DH * l + DH)

        def fill_no(slot, i):
            return i if slot < 0 else PROLOGUE_FILLS + sum(BODY_FILLS[:slot]) + i

        def bank_of(slot, i):
            return fill_no(slot, i) % 2

        def fills(p):
            def unit_proj(slot, unit):
                return [(slot, i, lo_done, 8 * unit + 2 * i + 2) for i in range(4)]

            def unit_knat(slot, first, unit):
                return [(slot, first + i, knat_done, 2 * unit + i + 1) for i in range(2)]
            if p is None:
                return unit_proj(-1, 0) + unit_knat(-1, 4, 0) + [(-1, 6, mrow_done, 1)]
            found = unit_proj(0, 2 * p + 1) + [(0, 4, mrow_done, 4 * p + 2)]
            found += unit_knat(1, 0, 2 * p + 1) + [(1, 2, mrow_done, 4 * p + 3)]
            more = not is_last(p)
            found += (unit_proj(2, 2 * p + 2) if more else []) + [(2, 4, mrow_done, 4 * p + 4)]
            return found + (unit_knat(3, 0, 2 * p + 2) + [(3, 2, mrow_done, 4 * p + 5)] if more else [])

        def wait_fill_free(eng, p, slot, i):
            first = isinstance(p, int) and p == 0
            before = [] if slot < 0 else fills(None) if first else fills(p - 1)
            own = fills(None) if slot < 0 else fills(p)
            own = own[:[f[:2] for f in own].index((slot, i))]
            bank = bank_of(slot, i)
            for s_, i_, sem, value in reversed(before + own):
                if bank_of(s_, i_) == bank:
                    eng.wait_ge(sem, value)
                    break
            return bank

        def slots(emit, eng):
            for kk in range(4):
                emit(0, kk)
            with eng.Fori(1, PAIRS - 1) as p:
                for kk in range(4):
                    emit(p, kk)
            for kk in range(4):
                emit(PAIRS - 1, kk)

        def is_last(p, kk=3):
            return isinstance(p, int) and p == PAIRS - 1 and kk >= 3

        def next_unit(p, kk):
            return 2 * p + (1 if kk < 2 else 2)

        def no_prep(p, kk):
            return isinstance(p, int) and p == PAIRS - 1 and kk >= 2

        with nc.Block() as block:
            @block.sync
            def _(sp):
                def load_w(p):
                    wait(sp, w_split, 2 * p)
                    sp.dma_start(w_raw[:, :, :], wq_view[:, :, bass.ds(p * P, P)]).then_inc(w_loaded, 16)

                def duplicate(u, unit):
                    sp.wait_ge(hi_done, unit * 8 + 4)
                    for l in range(2):
                        sp.dma_start(q2[u][l][rows(l), :].bitcast(FP32),
                                     qs[u][l][rows(l), :].bitcast(FP32)).then_inc(dup_done, 16)
                    sp.wait_ge(hi_done, unit * 8 + 8)
                    for l in range(2):
                        sp.dma_start(ks[u][l][rows(1 - l), :].bitcast(FP32),
                                     ks[u][l][rows(l), :].bitcast(FP32)).then_inc(dup_done, 16)

                load_w(0)
                duplicate(0, 0)

                def body(p):
                    duplicate(1, 2 * p + 1)
                    if not is_last(p):
                        load_w(p + 1)
                        duplicate(0, 2 * p + 2)
                body(0)
                with sp.Fori(1, PAIRS - 1) as p:
                    body(p)
                body(PAIRS - 1)
                sp.wait_ge(dup_done, 64 * 2 * PAIRS)

            @block.gpsimd
            def _(pool):
                pool.memset(maskb[:, :], 0.0).then_inc(consts, 1)
                pool.memset(identb[:, :], 0.0).then_inc(consts, 1)
                pool.memset(neg_block[:, :, :], 0.0).then_inc(consts, 1)
                for u in range(2):
                    pool.memset(k_nat[u][:, :, 1, :], 1.0).then_inc(consts, 1)
                pool.wait_ge(consts, 5)
                pool.affine_select(out=maskb[:, :], in_=maskb[:, :], compare_op=ALU.is_ge, fill=MASKED,
                                   base=0, pattern=[[-1, P]], channel_multiplier=1).then_inc(consts, 1)
                pool.affine_select(out=identb[:, :], in_=identb[:, :], compare_op=ALU.not_equal, fill=1.0,
                                   base=0, pattern=[[-1, P]], channel_multiplier=1).then_inc(consts, 1)
                pool.affine_select(out=neg_block[:, :, :], in_=neg_block[:, :, :], compare_op=ALU.not_equal,
                                   fill=-1.0, base=0, pattern=[[-1, QT], [0, P]],
                                   channel_multiplier=1).then_inc(consts, 1)

                def split_w(p):
                    pool.wait_ge(w_loaded, 16 * (p + 1))
                    wait(pool, proj_ready, 8 * p)
                    pool.sem_inc(pool_turns, 1)
                    pool.tensor_copy(w_hi[:, :, :], w_raw[:, :, :]).then_inc(w_split, 1)
                    pool.wait_ge(w_split, 2 * p + 1)
                    pool.sem_inc(pool_turns, 1)
                    pool.tensor_tensor(w_lo[:, :, :], w_raw[:, :, :], w_hi[:, :, :].bitcast(FP32),
                                       ALU.subtract).then_inc(w_split, 1)

                split_w(0)

                def slot(p, kk):
                    h = 4 * p + kk
                    if kk == 1 and not is_last(p):
                        split_w(p + 1)
                    for c in DIAGONAL:
                        pool.wait_ge(exp_done, NCHUNK * h + c + 1)
                        pool.sem_inc(pool_turns, 1)
                        v = probs[:, CHUNK_AT[c]:CHUNK_AT[c] + P]
                        pool.affine_select(out=v, in_=v, compare_op=ALU.is_ge, fill=0.0, base=0,
                                           pattern=[[1, P]], channel_multiplier=-1).then_inc(masked, 1)
                slots(slot, pool)

            @block.scalar
            def _(act):
                def proj_half(p, slot_no, u, unit, i):
                    bank = bank_of(slot_no, i)
                    act.wait_ge(proj_ready, 4 * unit + i + 1)
                    c = slice((i % 2) * BANK, (i % 2 + 1) * BANK)
                    if i >= 2:
                        act.activation(k_t[:, c], misc[bank][:, :], ACT.Copy).then_inc(kt_done, 1)
                    dst = qs if i < 2 else ks
                    for l in range(2):
                        act.activation(dst[u][l][rows(l), c], misc[bank][rows(l), :], ACT.Copy)\
                           .then_inc(hi_done, 1)

                def knat_half(p, slot_no, u, unit, i):
                    bank = bank_of(slot_no, i)
                    act.wait_ge(knat_ps_ready, 2 * unit + (i % 4) + 1)
                    act.activation(k_nat[u][:, HALF * (i % 4):HALF * (i % 4 + 1), 0::2, :],
                                   misc[bank][:, :].rearrange("p (t l d) -> p t l d", t=HALF, l=2),
                                   ACT.Copy).then_inc(knat_done, 1)

                def invert(g, l, half):
                    act.wait_ge(av_done, NCHUNK * g + (NCHUNK if half else FIRST_HALF_STEPS))
                    act.activation(inv[rows(l), half, :], out_ps[half][rows(1 - l), :], ACT.Ln).then_inc(ln_done, 1)
                    act.wait_ge(ln_done, 2 * g + half + 1)
                    act.activation(inv[rows(l), half, :], inv[rows(l), half, :], ACT.Exp, scale=-1.0)\
                       .then_inc(inv_done, 1)

                act.preload_act_table_set("natural_log_exp_and_others")
                for i in range(4):
                    proj_half(0, -1, 0, 0, i)
                for i in range(2):
                    bank = bank_of(-1, 4 + i)
                    act.wait_ge(knat_ps_ready, i + 1)
                    act.activation(k_nat[0][:, HALF * i:HALF * (i + 1), 0::2, :],
                                   misc[bank][:, :].rearrange("p (t l d) -> p t l d", t=HALF, l=2),
                                   ACT.Copy).then_inc(knat_done, 1)

                def slot(p, kk):
                    h = 4 * p + kk
                    zero = isinstance(p, int) and p == 0
                    for c in range(NCHUNK):
                        act.wait_ge(scores_ready, NCHUNK * h + c + 1)
                        if not (zero and kk == 0):
                            act.wait_ge(av_done, NCHUNK * (h - 1) + c + 1)
                        a, b = CHUNK_AT[c], CHUNK_AT[c + 1]
                        bank = (NCHUNK * kk + c) % 2
                        act.activation(probs[:, a:b], sc_ps[bank][:, 0:b - a], ACT.Exp, scale=BETA)\
                           .then_inc(exp_done, 1)
                        if c == 0 and not (zero and kk < 2):
                            invert(h - 2, kk % 2, 1)
                        if c == FIRST_HALF_STEPS and not (zero and kk == 0):
                            invert(h - 1, (kk + 1) % 2, 0)
                        if not no_prep(p, kk):
                            unit, u = next_unit(p, kk), (kk // 2 + 1) % 2
                            if kk % 2 == 0 and c - 1 in PROJ_STEPS:
                                proj_half(p, kk, u, unit, PROJ_STEPS.index(c - 1))
                            if kk % 2 == 1 and c - 1 in KNAT_STEPS:
                                knat_half(p, kk, u, unit, KNAT_STEPS.index(c - 1))
                slots(slot, act)
                invert(4 * PAIRS - 2, 0, 1)
                invert(4 * PAIRS - 1, 1, 0)
                invert(4 * PAIRS - 1, 1, 1)

            @block.vector
            def _(dve):
                for u in range(2):
                    for l in range(2):
                        o = DH * (1 - l)
                        dve.memset(q2[u][l][o:o + DH, :].bitcast(FP32), 0.0).then_inc(rows_set, 1)
                        dve.memset(k2[u][l][o:o + DH, :].bitcast(FP32), 0.0).then_inc(rows_set, 1)
                dve.wait_ge(rows_set, 8)
                for u in range(2):
                    for l in range(2):
                        o = DH * (1 - l)
                        dve.memset(k2[u][l][o:o + QT, :].bitcast(FP32), 1.0).then_inc(rows_set, 1)

                def low_half(p, slot_no, u, unit, i):
                    bank = bank_of(slot_no, i)
                    c = slice((i % 2) * BANK, (i % 2 + 1) * BANK)
                    for l in range(2):
                        dve.wait_ge(hi_done, 8 * unit + 2 * i + l + 1)
                        if i < 2:
                            dst, hi = qs[u][l][rows(1 - l), c], qs[u][l][rows(l), c]
                        else:
                            dst, hi = k2[u][l][rows(l), c], ks[u][l][rows(l), c]
                        dve.tensor_tensor(dst, misc[bank][rows(l), :], hi.bitcast(FP32), ALU.subtract)\
                           .then_inc(lo_done, 1)

                def maxima(h, kk, c):
                    i, a, b = MAX_CHUNKS[c]
                    dst = row_max[:, kk % 2, i:i + 1] if i < HALF else half_max[:, kk % 2, i - HALF, (a > 0):(a > 0) + 1]
                    dve.wait_ge(max_ready, NMAX * h + c + 1)
                    dve.reduce_max(dst, max_ps[(NMAX * kk + c) % 2][:, 0:(b - a) * P], AX.X).then_inc(max_taken, 1)

                def join_maxima(h, kk):
                    dve.wait_ge(max_taken, NMAX * (h + 1))
                    dve.reduce_max(row_max[:, kk % 2, HALF:QT], half_max[:, kk % 2, :, :], AX.X)\
                       .then_inc(row_max_done, 1)

                def max_row(h, p, slot_no, i, u, l):
                    bank = bank_of(slot_no, i)
                    dve.wait_ge(row_max_t, h + 1)
                    o = DH * (1 - l)
                    mt = misc[bank][0:QT, 0:P].unsqueeze(1).to_broadcast([QT, QT, P])
                    dve.tensor_tensor(q2[u][l][o:o + QT, :].rearrange("r (i q) -> r i q", i=QT), mt,
                                      neg_block[:, :, :], ALU.mult)\
                       .then_inc(mrow_done, 1)

                def scale_out(g, p, kk, half):
                    l = kk % 2
                    dve.wait_ge(inv_done, 2 * g + half + 1)
                    at = p * (BATCH * SEQ) + (kk // 2) * SEQ + half * BANK
                    dve.tensor_tensor(k.attn_t[rows(l), bass.ds(at, BANK)], out_ps[half][rows(l), :],
                                      inv[rows(l), half, :], ALU.mult).then_inc(out_used, 1)

                for i in range(4):
                    low_half(0, -1, 0, 0, i)
                for c in range(NMAX):
                    maxima(0, 0, c)
                join_maxima(0, 0)
                dve.wait_ge(consts, 8)
                dve.wait_ge(rows_set, 12)
                max_row(0, 0, -1, 6, 0, 0)

                def slot(p, kk):
                    h = 4 * p + kk
                    zero = isinstance(p, int) and p == 0
                    nk = (kk + 1) % 4
                    for c in range(NCHUNK):
                        if not is_last(p, kk):
                            for m in range(MAX_FIRST[c], MAX_FIRST[c] + MAX_PER_STEP[c]):
                                maxima(h + 1, nk, m)
                        if c == 2 and not (zero and kk < 2):
                            scale_out(h - 2, p if kk >= 2 else p - 1, (kk + 2) % 4, 1)
                        if c == FIRST_HALF_STEPS + 1 and not (zero and kk == 0):
                            scale_out(h - 1, p if kk >= 1 else p - 1, (kk + 3) % 4, 0)
                        if kk % 2 == 0 and not no_prep(p, kk) and c - 2 in PROJ_STEPS:
                            low_half(p, kk, (kk // 2 + 1) % 2, next_unit(p, kk), PROJ_STEPS.index(c - 2))
                        if c == MROW_STEP - 1 and not is_last(p, kk):
                            join_maxima(h + 1, nk)
                    if not is_last(p, kk):
                        max_row(h + 1, p, kk, BODY_FILLS[kk] - 1, nk // 2, nk % 2)
                slots(slot, dve)
                last = PAIRS - 1
                scale_out(4 * PAIRS - 2, last, 2, 1)
                scale_out(4 * PAIRS - 1, last, 3, 0)
                scale_out(4 * PAIRS - 1, last, 3, 1)

            @block.tensor
            def _(pe):
                def project(p, slot_no, b, unit, i):
                    bank = wait_fill_free(pe, p, slot_no, i)
                    a = i // 2
                    c = slice(b * SEQ + (i % 2) * BANK, b * SEQ + (i % 2 + 1) * BANK)
                    pe.matmul(misc[bank][:, :], w_hi[:, a, :], k.xhi[:, c], start=True, stop=False)
                    pe.matmul(misc[bank][:, :], w_hi[:, a, :], k.xlo[:, c], start=False, stop=False)
                    pe.matmul(misc[bank][:, :], w_lo[:, a, :], k.xhi[:, c], start=False, stop=True)\
                      .then_inc(proj_ready, 1)

                def turn_k(p, slot_no, first, unit, i):
                    bank = wait_fill_free(pe, p, slot_no, first + i)
                    pe.wait_ge(kt_done, 2 * unit + i + 1)
                    for t in range(HALF):
                        j = HALF * i + t
                        last = pe.transpose(misc[bank][:, t * P:(t + 1) * P], k_t[:, j * P:(j + 1) * P],
                                            k.ident[:, :])
                    last.then_inc(knat_ps_ready, 1)

                def max_scores(h, kk, c):
                    i, a, b = MAX_CHUNKS[c]
                    u, l = kk // 2, kk % 2
                    n = (NMAX * kk + c) % 2
                    wait(pe, max_taken, NMAX * h + c - 1)
                    diag = b == i + 1
                    pe_last = pe.matmul(max_ps[n][:, 0:(b - a) * P], qs[u][l][:, i * P:(i + 1) * P],
                                        ks[u][l][:, a * P:b * P], start=True, stop=not diag)
                    if diag:
                        o = (i - a) * P
                        pe_last = pe.matmul(max_ps[n][:, o:o + P], identb[:, :], maskb[:, :], start=False, stop=True)
                    pe_last.then_inc(max_ready, 1)

                def wait_unit(unit):
                    pe.wait_ge(hi_done, 8 * (unit + 1))
                    pe.wait_ge(lo_done, 8 * (unit + 1))
                    pe.wait_ge(dup_done, 64 * (unit + 1))

                def turn_max(h, kk, p, slot_no, i):
                    bank = wait_fill_free(pe, p, slot_no, i)
                    pe.wait_ge(row_max_done, h + 1)
                    pe.transpose(misc[bank][0:QT, 0:P], row_max[:, kk % 2, :], k.ident[:, :])\
                      .then_inc(row_max_t, 1)

                def scores(h, kk, c):
                    j, a, b = SCORE_CHUNKS[c]
                    u, l = kk // 2, kk % 2
                    n = (NCHUNK * kk + c) % 2
                    if c == 0:
                        pe.wait_ge(mrow_done, h + 1)
                    wait(pe, exp_done, NCHUNK * h + c - 1)
                    o = sc_ps[n][:, 0:(b - a) * P]
                    pe.matmul(o, ks[u][l][:, j * P:(j + 1) * P], qs[u][l][:, a * P:b * P], start=True, stop=False)
                    pe.matmul(o, k2[u][l][:, j * P:(j + 1) * P], q2[u][l][:, a * P:b * P], start=False, stop=True)\
                      .then_inc(scores_ready, 1)

                def outputs(g, kk, c):
                    j, a, b = SCORE_CHUNKS[c]
                    u, l = kk // 2, kk % 2
                    half = int(c >= FIRST_HALF_STEPS)
                    pe.wait_ge(exp_done, NCHUNK * g + c + 1)
                    if c in DIAGONAL:
                        pe.wait_ge(masked, len(DIAGONAL) * g + DIAGONAL.index(c) + 1)
                    if c in (0, FIRST_HALF_STEPS):
                        wait(pe, out_used, 2 * g + half - 1)
                    o = (a - half * HALF) * P
                    kn = k_nat[u][:, j, l:l + 2, :].rearrange("p l d -> p (l d)")
                    pe.matmul(out_ps[half][:, o:o + (b - a) * P], kn, probs[:, CHUNK_AT[c]:CHUNK_AT[c + 1]],
                              start=(j == 0), stop=(c in (FIRST_HALF_STEPS - 1, NCHUNK - 1)))\
                      .then_inc(av_done, 1)

                pe.wait_ge(w_split, 2)
                for i in range(4):
                    project(0, -1, 0, 0, i)
                for i in range(2):
                    turn_k(0, -1, 4, 0, i)
                wait_unit(0)
                pe.wait_ge(consts, 8)
                pe.wait_ge(rows_set, 12)
                for c in range(NMAX):
                    max_scores(0, 0, c)
                turn_max(0, 0, 0, -1, 6)

                def slot(p, kk):
                    h = 4 * p + kk
                    zero = isinstance(p, int) and p == 0
                    nk = (kk + 1) % 4
                    for c in range(NCHUNK):
                        if not (zero and kk == 0):
                            if c == 0 and kk % 2 == 1:
                                pe.wait_ge(knat_done, 2 * (2 * p + kk // 2 + 1))
                            outputs(h - 1, (kk + 3) % 4, c)
                        scores(h, kk, c)
                        if not is_last(p, kk):
                            if c == 0 and kk % 2 == 1:
                                wait_unit(next_unit(p, kk))
                            for m in range(MAX_FIRST[c], MAX_FIRST[c] + MAX_PER_STEP[c]):
                                max_scores(h + 1, nk, m)
                        if not no_prep(p, kk):
                            unit = next_unit(p, kk)
                            if kk % 2 == 0 and c in PROJ_STEPS:
                                if kk == 2 and c == PROJ_STEPS[0]:
                                    pe.wait_ge(w_split, 2 * (p + 2))
                                project(p, kk, (kk // 2 + 1) % 2, unit, PROJ_STEPS.index(c))
                            if kk % 2 == 1 and c in KNAT_STEPS:
                                turn_k(p, kk, 0, unit, KNAT_STEPS.index(c))
                        if c == MROW_STEP and not is_last(p, kk):
                            turn_max(h + 1, nk, p, kk, BODY_FILLS[kk] - 1)
                slots(slot, pe)
                for c in range(NCHUNK):
                    outputs(4 * PAIRS - 1, 3, c)


def project_out(nc, k, w_out):
    with Scope(nc, "po") as s:
        w = s.sb("w", [P, PAIRS, D])
        acc = s.ps("acc", GROUPS)
        loaded, done, added = s.sem("loaded"), s.sem("done"), s.sem("added")
        with nc.Block() as block:
            @block.sync
            def _(sp):
                sp.dma_start(w[:, :, :], w_out.rearrange("(p r) n -> r p n", r=P)).then_inc(loaded, 16)

            @block.tensor
            def _(pe):
                pe.wait_ge(loaded, 16)
                for n in range(GROUPS):
                    for j in range(PER):
                        for p in range(PAIRS):
                            at = p * TOKENS + (n * PER + j) * P
                            last = pe.matmul(acc[n][:, j * P:(j + 1) * P], k.attn_t[:, at:at + P], w[:, p, :],
                                             start=(p == 0), stop=(p == PAIRS - 1))
                    last.then_inc(done, 1)

            @block.vector
            def _(dve):
                for n in range(GROUPS):
                    dve.wait_ge(done, n + 1)
                    v = k.x[:, n * PER:(n + 1) * PER, :]
                    dve.tensor_tensor(v, v, acc[n][:, :].rearrange("p (t d) -> p t d", t=PER), ALU.add)\
                       .then_inc(added, 1)


def moe_weights(nc, f, ins):
    with Scope(nc, "mw") as s:
        raw = {n: s.sb(f"raw_{n}", [P, EXPERTS + 2, INTER]) for n in ("wg", "wu")}
        gate_raw = s.sb("gate_raw", [P, EXPERTS])
        sel = s.sb("sel", [P, EXPERTS // 2, P])
        iota_i = s.sb("iota_i", [P, TILES, EXPERTS], I32)
        loaded, split, made, sel_ready = s.sem("loaded"), s.sem("split"), s.sem("made"), s.sem("sel_ready")
        padded = s.sem("padded")
        with nc.Block() as block:
            @block.sync
            def _(sp):
                for n in ("wg", "wu"):
                    sp.dma_start(raw[n][:, 0:EXPERTS, :], ins[f"experts_{n}"].rearrange("e d i -> d e i"))\
                      .then_inc(loaded, 16)
                    sp.dma_start(raw[n][:, EXPERTS, :], ins[f"shared_{n}"]).then_inc(loaded, 16)
                sp.dma_start(gate_raw[:, :], ins["gate_w"]).then_inc(loaded, 16)
                sp.dma_start(f.gate_b[:, :], ins["gate_b"].rearrange("(e a) -> e a", a=1)).then_inc(loaded, 16)
                sp.dma_start(f.wd[:, 0:EXPERTS // 2, :], ins["experts_wd"].rearrange("(p e) i d -> (e i) p d", e=2))\
                  .then_inc(loaded, 16)
                sp.dma_start(f.wd[0:INTER, EXPERTS // 2, :], ins["shared_wd"]).then_inc(loaded, 16)
                sp.wait_ge(loaded, 16 * 8)

            @block.scalar
            def _(act):
                act.wait_ge(loaded, 16 * 8)
                act.wait_ge(padded, 3)
                act.activation(f.wg_hi[:, :, :], raw["wg"][:, :, :], ACT.Copy).then_inc(split, 1)
                act.activation(f.wu_hi[:, :, :], raw["wu"][:, :, :], ACT.Copy).then_inc(split, 1)
                act.activation(f.gate_hi[:, :], gate_raw[:, :], ACT.Copy).then_inc(split, 1)
                act.wait_ge(sel_ready, 5)
                act.activation(f.sel[:, :, :], sel[:, :, :], ACT.Copy)

            @block.vector
            def _(dve):
                for n in ("wg", "wu"):
                    dve.memset(raw[n][:, EXPERTS + 1, :], 0.0).then_inc(padded, 1)
                dve.memset(f.wd[INTER:P, EXPERTS // 2, :], 0.0).then_inc(padded, 1)
                dve.wait_ge(split, 1)
                dve.tensor_tensor(f.wg_lo[:, :, :], raw["wg"][:, :, :], f.wg_hi[:, :, :].bitcast(FP32), ALU.subtract)
                dve.wait_ge(split, 2)
                dve.tensor_tensor(f.wu_lo[:, :, :], raw["wu"][:, :, :], f.wu_hi[:, :, :].bitcast(FP32), ALU.subtract)
                dve.wait_ge(split, 3)
                dve.tensor_tensor(f.gate_lo[:, :], gate_raw[:, :], f.gate_hi[:, :].bitcast(FP32), ALU.subtract)
                dve.wait_ge(made, 1)
                dve.tensor_copy(f.iota[:, :, :], iota_i[:, :, :])

            @block.gpsimd
            def _(pool):
                pool.iota(iota_i[:, :, :], pattern=[[0, TILES], [1, EXPERTS]], base=0, channel_multiplier=0)\
                    .then_inc(made, 1)
                pool.memset(sel[:, :, :], 0.0).then_inc(sel_ready, 1)
                for half in range(2):
                    for top in (0, 32):
                        pool.wait_ge(sel_ready, 2 * half + top // 32 + 1)
                        v = sel[top:top + EXPERTS, :, half * INTER:(half + 1) * INTER]
                        i = pool.affine_select(out=v, in_=v, compare_op=ALU.not_equal, fill=1.0, base=-half,
                                               pattern=[[-2, EXPERTS // 2], [0, INTER]], channel_multiplier=1)
                        i.then_inc(sel_ready, 1)


def route(nc, tag, k, f):
    with Scope(nc, tag) as s:
        logits, nat, wt_ps = s.ps("logits", 2), s.ps("nat"), s.ps("wt", GROUPS)
        score_t = s.sb("score_t", [EXPERTS, TOKENS])
        full = [P, TILES, EXPERTS]
        sc, eq, key, one1, one2, sc2, w1, w = [s.sb(n, full) for n in ("sc", "eq", "key", "one1", "one2", "sc2", "w1", "w")]
        v1, v2, i1, i2, den, rec, g1, g2 = [s.sb(n, [P, TILES]) for n in ("v1", "v2", "i1", "i2", "den", "rec", "g1", "g2")]
        logit_ready, scored, nat_ready = s.sem("logit_ready"), s.sem("scored"), s.sem("nat_ready")
        step, w_ready, wt_ready, hi_done = s.sem("step"), s.sem("w_ready"), s.sem("wt_ready"), s.sem("hi_done")
        zeroed = s.sem("zeroed")
        with nc.Block() as block:
            @block.tensor
            def _(pe):
                for n in range(GROUPS):
                    wait(pe, scored, n - 1)
                    o = logits[n % 2][0:EXPERTS, :]
                    c = slice(n * BANK, (n + 1) * BANK)
                    pe.matmul(o, f.gate_hi[:, :], k.xhi[:, c], start=True, stop=False)
                    pe.matmul(o, f.gate_hi[:, :], k.xlo[:, c], start=False, stop=False)
                    pe.matmul(o, f.gate_lo[:, :], k.xhi[:, c], start=False, stop=True).then_inc(logit_ready, 1)
                pe.wait_ge(scored, GROUPS)
                for t in range(TILES):
                    last = pe.transpose(nat[:, t * EXPERTS:(t + 1) * EXPERTS], score_t[:, t * P:(t + 1) * P],
                                        k.ident[0:EXPERTS, 0:EXPERTS])
                last.then_inc(nat_ready, 1)
                pe.wait_ge(w_ready, 1)
                for t in range(TILES):
                    last = pe.transpose(wt_ps[t // PER][0:EXPERTS, (t % PER) * P:(t % PER + 1) * P], w[:, t, :],
                                        k.ident[:, :])
                    if t % PER == PER - 1:
                        last.then_inc(wt_ready, 1)

            @block.scalar
            def _(act):
                for n in range(GROUPS):
                    act.wait_ge(logit_ready, n + 1)
                    act.activation(score_t[:, n * BANK:(n + 1) * BANK], logits[n % 2][0:EXPERTS, :], ACT.Sigmoid,
                                   bias=f.gate_b[:, :]).then_inc(scored, 1)
                act.wait_ge(zeroed, 1)
                for n in range(GROUPS):
                    act.wait_ge(wt_ready, n + 1)
                    act.activation(f.wt[0:EXPERTS, n * BANK:(n + 1) * BANK], wt_ps[n][0:EXPERTS, :], ACT.Copy)\
                       .then_inc(hi_done, 1)

            @block.vector
            def _(dve):
                count = [0]

                def then(ins):
                    count[0] += 1
                    ins.then_inc(step, 1)
                    dve.wait_ge(step, count[0])

                dve.memset(f.wt[:, :].bitcast(FP32), 0.0).then_inc(zeroed, 1)
                dve.wait_ge(nat_ready, 1)
                then(dve.tensor_copy(sc[:, :, :], nat[:, 0:TILES * EXPERTS].rearrange("p (t e) -> p t e", t=TILES)))

                def largest(x, v, i, one):
                    then(dve.reduce_max(v[:, :], x[:, :, :], AX.X))
                    then(dve.tensor_tensor(eq[:, :, :], x[:, :, :], bcast(v[:, :], EXPERTS), ALU.is_equal))
                    then(dve.scalar_tensor_tensor(out=key[:, :, :], in0=eq[:, :, :], scalar=-100.0,
                                                  in1=f.iota[:, :, :], op0=ALU.mult, op1=ALU.add))
                    then(dve.tensor_reduce(i[:, :], key[:, :, :], AX.X, ALU.min))
                    then(dve.tensor_tensor(one[:, :, :], key[:, :, :], bcast(i[:, :], EXPERTS), ALU.is_equal))

                largest(sc, v1, i1, one1)
                then(dve.scalar_tensor_tensor(out=sc2[:, :, :], in0=one1[:, :, :], scalar=-4.0, in1=sc[:, :, :],
                                              op0=ALU.mult, op1=ALU.add))
                largest(sc2, v2, i2, one2)
                then(dve.tensor_tensor(den[:, :], v1[:, :], v2[:, :], ALU.add))
                then(dve.reciprocal(rec[:, :], den[:, :]))
                then(dve.tensor_tensor(g1[:, :], v1[:, :], rec[:, :], ALU.mult))
                then(dve.tensor_tensor(g2[:, :], v2[:, :], rec[:, :], ALU.mult))
                then(dve.tensor_tensor(w1[:, :, :], one1[:, :, :], bcast(g1[:, :], EXPERTS), ALU.mult))
                then(dve.tensor_tensor(w[:, :, :], one2[:, :, :], bcast(g2[:, :], EXPERTS), ALU.mult))
                dve.tensor_tensor(w[:, :, :], w[:, :, :], w1[:, :, :], ALU.add).then_inc(w_ready, 1)
                for n in range(GROUPS):
                    dve.wait_ge(hi_done, n + 1)
                    c = slice(n * BANK, (n + 1) * BANK)
                    dve.tensor_tensor(f.wt[32:32 + EXPERTS, c], wt_ps[n][0:EXPERTS, :],
                                      f.wt[0:EXPERTS, c].bitcast(FP32), ALU.subtract)


def experts(nc, tag, k, f, store=None):
    RING = 3
    with Scope(nc, tag) as s:
        g_ps, u_ps, wb_ps, acc = s.ps("g", RING), s.ps("u", RING), s.ps("wb"), s.ps("acc")
        gate = [s.sb(f"gate{r}", [P, BANK]) for r in range(RING)]
        prod = [s.sb(f"prod{r}", [P, BANK]) for r in range(RING)]
        hid = [s.sb(f"hid{r}", [P, BANK]) for r in range(RING)]
        g_ready, u_ready, wb_ready = s.sem("g_ready"), s.sem("u_ready"), s.sem("wb_ready")
        gated, multiplied = s.sem("gated"), s.sem("multiplied")
        hid_ready, down_done = s.sem("hid_ready"), s.sem("down_done")
        acc_used, stored = s.sem("acc_used"), s.sem("stored")
        LAST = STEPS - 1

        def turns(emit, eng):
            emit(0)
            with eng.Fori(1, GROUPS) as n:
                emit(n)

        with nc.Block() as block:
            @block.tensor
            def _(pe):
                def up(out, hi, lo, st, n):
                    x = bass.ds(n * BANK, BANK)
                    wh = hi[:, 2 * st:2 * st + 2, :].rearrange("p e i -> p (e i)")
                    wl = lo[:, 2 * st:2 * st + 2, :].rearrange("p e i -> p (e i)")
                    pe.matmul(out[:, :], wh, k.xhi[:, x], start=True, stop=False)
                    pe.matmul(out[:, :], wh, k.xlo[:, x], start=False, stop=False)
                    return pe.matmul(out[:, :], wl, k.xhi[:, x], start=False, stop=True)

                def down(n, st):
                    if st < LAST:
                        pe.wait_ge(hid_ready, LAST * n + st + 1)
                    else:
                        pe.wait_ge(multiplied, STEPS * (n + 1))
                    if st == 0:
                        wait(pe, acc_used, n)
                    for t in range(PER):
                        last = pe.matmul(acc[:, t * P:(t + 1) * P], hid[st % RING][:, t * P:(t + 1) * P],
                                         f.wd[:, st, :], start=(st == 0 and t == 0), stop=(st == LAST),
                                         skip_group_check=True)
                    last.then_inc(down_done, 1)

                def turn(n):
                    zero = isinstance(n, int)
                    for st in range(STEPS):
                        g, r = STEPS * n + st, st % RING
                        if not zero or st >= RING:
                            pe.wait_ge(gated, g - RING + 1)
                        up(g_ps[r], f.wg_hi, f.wg_lo, st, n).then_inc(g_ready, 1)
                        if not zero or st >= RING:
                            pe.wait_ge(multiplied, g - RING + 1)
                        up(u_ps[r], f.wu_hi, f.wu_lo, st, n).then_inc(u_ready, 1)
                        if st > 0:
                            down(n, st - 1)
                        elif not zero:
                            down(n - 1, LAST)
                        if st < LAST:
                            wait(pe, hid_ready, LAST * n + st)
                            pe.matmul(wb_ps[:, :], f.sel[:, st, :], f.wt[:, bass.ds(n * BANK, BANK)],
                                      start=True, stop=True).then_inc(wb_ready, 1)
                turns(turn, pe)
                down(GROUPS - 1, LAST)

            @block.scalar
            def _(act):
                def turn(n):
                    zero = isinstance(n, int)
                    for st in range(STEPS):
                        g, r = STEPS * n + st, st % RING
                        act.wait_ge(g_ready, g + 1)
                        if not zero or st >= RING:
                            act.wait_ge(multiplied, g - RING + 1)
                        act.activation(gate[r][:, :], g_ps[r][:, :], ACT.Silu).then_inc(gated, 1)
                turns(turn, act)

            @block.vector
            def _(dve):
                def add_up(n):
                    dve.wait_ge(down_done, STEPS * (n + 1))
                    at = bass.ds(n * PER, PER)
                    dve.tensor_tensor(k.x[:, at, :], k.xr[:, at, :],
                                      acc[:, :].rearrange("p (t d) -> p t d", t=PER), ALU.add).then_inc(acc_used, 1)

                def turn(n):
                    zero = isinstance(n, int)
                    for st in range(STEPS):
                        g, r = STEPS * n + st, st % RING
                        dve.wait_ge(gated, g + 1)
                        dve.wait_ge(u_ready, g + 1)
                        if not zero or st >= RING:
                            dve.wait_ge(down_done, g - RING + 1)
                        dst = prod[r] if st < LAST else hid[r]
                        i = dve.tensor_tensor(dst[:, :], gate[r][:, :], u_ps[r][:, :], ALU.mult)
                        i.then_inc(multiplied, 1)
                        if st < LAST:
                            dve.wait_ge(multiplied, g + 1)
                            dve.wait_ge(wb_ready, LAST * n + st + 1)
                            dve.tensor_tensor(hid[r][:, :], prod[r][:, :], wb_ps[:, :], ALU.mult)\
                               .then_inc(hid_ready, 1)
                        if st == 0 and not zero:
                            add_up(n - 1)
                turns(turn, dve)
                add_up(GROUPS - 1)

            if store is not None:
                @block.sync
                def _(sp):
                    for n in range(GROUPS):
                        sp.wait_ge(acc_used, n + 1)
                        sp.dma_start(store[:, n * PER:(n + 1) * PER, :], k.x[:, n * PER:(n + 1) * PER, :])\
                          .then_inc(stored, 16)
                    sp.wait_ge(stored, 16 * GROUPS)


def mixture(nc, tag, k, f, store=None):
    layernorm_transposed(nc, tag + "n", k, residual=k.xr)
    route(nc, tag + "r", k, f)
    experts(nc, tag + "e", k, f, store)


def state_space(nc, k, ins):
    KT = INNER // P
    PAD = TAPS - 1
    with Scope(nc, "ss") as s:
        ps = s.ps("ps", 8)
        w_in = s.sb("w_in", [P, 2 * INNER])
        w_in_hi, w_in_lo = s.sb("w_in_hi", [P, 2 * INNER], F32R), s.sb("w_in_lo", [P, 2 * INNER], F32R)
        b_in = s.sb("b_in", [P, 2 * KT])
        conv_w, conv_b, skip = s.sb("conv_w", [P, KT, TAPS]), s.sb("conv_b", [P, KT]), s.sb("skip", [P, KT])
        w_s = {n: s.sb(f"w_{n}", [P, KT, STATE]) for n in ("dt", "B", "C")}
        b_s = {n: s.sb(f"b_{n}", [P, 1]) for n in ("dt", "B", "C")}
        w_si, b_si = s.sb("w_si", [P, INNER]), s.sb("b_si", [P, KT])
        w_out, b_out = s.sb("w_out", [P, KT, D]), s.sb("b_out", [P, D])
        xm = [s.sb(f"xm{c}", [P, BATCH, SEQ + PAD]) for c in range(KT)]
        sg = [s.sb(f"sg{c}", [P, TOKENS]) for c in range(KT)]
        cv = s.sb("cv", [P, 2, SEQ])
        xs = [s.sb(f"xs{c}", [P, TOKENS]) for c in range(KT)]
        dt_t, decay, drive, state, y = [s.sb(n, [P, SEQ]) for n in ("dt_t", "decay", "drive", "state", "y")]
        y_nat = s.sb("y_nat", [P, QT * BATCH, STATE])
        y_c, y_sq = s.sb("y_c", [P, QT * BATCH, STATE]), s.sb("y_sq", [P, QT * BATCH, STATE])
        yt = s.sb("yt", [P, SEQ])
        z = [s.sb(f"z{c}", [P, TOKENS]) for c in range(KT)]
        st1, mean, var, sd, rstd = [s.sb(n, [P, QT * BATCH]) for n in ("st1", "mean", "var", "sd", "rstd")]

        loaded, split, w_ready = s.sem("loaded"), s.sem("split"), s.sem("w_ready")
        in_ready, in_used = s.sem("in_ready"), s.sem("in_used")
        xm_done, conv_done, conv_used, link = s.sem("xm_done"), s.sem("conv_done"), s.sem("conv_used"), s.sem("link")
        ssm_ready, dt_done, ssm_used = s.sem("ssm_ready"), s.sem("dt_done"), s.sem("ssm_used")
        y_done, nat_ready, centred, squared = s.sem("y_done"), s.sem("nat_ready"), s.sem("centred"), s.sem("squared")
        varied, rooted, normed, yt_ready, yt_done = s.sem("varied"), s.sem("rooted"), s.sem("normed"), s.sem("yt_ready"), s.sem("yt_done")
        si_ready, si_used, z_done = s.sem("si_ready"), s.sem("si_used"), s.sem("z_done")
        out_ready, padded = s.sem("out_ready"), s.sem("padded")
        N_IN = 2 * KT * GROUPS
        LOADS = 19

        def col(v):
            return v.rearrange("(c p) -> p c", p=P)

        with nc.Block() as block:
            @block.sync
            def _(sp):
                def load(dst, src):
                    slow = src.ap[-1][0] != 1
                    sp.dma_start(dst, src, allow_slow_non_contiguous=slow).then_inc(loaded, 16)
                load(w_in[:, :], ins["W_in"])
                load(b_in[:, :], col(ins["b_in"]))
                load(conv_w[:, :, :], ins["conv_w"].rearrange("(c p) t -> p c t", p=P))
                load(conv_b[:, :], col(ins["conv_b"]))
                load(skip[:, :], col(ins["D"]))
                for n in ("dt", "B", "C"):
                    load(w_s[n][:, :, :], ins[f"W_{n}"].rearrange("(c p) n -> p c n", p=P))
                    for b in range(BATCH):
                        load(b_s[n][b * STATE:(b + 1) * STATE, :], ins[f"b_{n}"].rearrange("(p a) -> p a", a=1))
                for b in range(BATCH):
                    load(w_si[b * STATE:(b + 1) * STATE, :], ins["W_si"])
                load(b_si[:, :], col(ins["b_si"]))
                load(w_out[:, :, :], ins["W_out"].rearrange("(c p) n -> p c n", p=P))
                load(b_out[:, :], ins["b_out"].partition_broadcast(P))
                sp.wait_ge(loaded, 16 * LOADS)

            @block.gpsimd
            def _(pool):
                for c in range(KT):
                    pool.memset(xm[c][:, :, 0:PAD], 0.0).then_inc(padded, 1)

            @block.tensor
            def _(pe):
                pe.wait_ge(w_ready, 1)
                for m in range(2 * KT):
                    for n in range(GROUPS):
                        i = m * GROUPS + n
                        wait(pe, in_used, i - 7)
                        o, c, r = ps[i % 8][:, :], slice(m * P, (m + 1) * P), slice(n * BANK, (n + 1) * BANK)
                        pe.matmul(o, w_in_hi[:, c], k.xhi[:, r], start=True, stop=False)
                        pe.matmul(o, w_in_hi[:, c], k.xlo[:, r], start=False, stop=False)
                        pe.matmul(o, w_in_lo[:, c], k.xhi[:, r], start=False, stop=True).then_inc(in_ready, 1)
                pe.wait_ge(in_used, N_IN)
                for b in range(BATCH):
                    pe.wait_ge(conv_used, KT * (b + 1))
                    for q, name in enumerate(("dt", "B", "C")):
                        for h in range(2):
                            o = ps[2 * q + h][b * STATE:(b + 1) * STATE, :]
                            for c in range(KT):
                                at = b * SEQ + h * BANK
                                last = pe.matmul(o, w_s[name][:, c, :], xs[c][:, at:at + BANK],
                                                 start=(c == 0), stop=(c == KT - 1))
                            last.then_inc(ssm_ready, 1)
                for h in range(2):
                    pe.wait_ge(y_done, h + 1)
                    for t in range(PER):
                        at = (h * PER + t) * P
                        last = pe.transpose(ps[6 + h][:, t * P:(t + 1) * P], y[:, at:at + P], k.ident[:, :])
                    last.then_inc(nat_ready, 1)
                pe.wait_ge(normed, 1)
                for h in range(2):
                    for t in range(PER):
                        j = h * PER + t
                        last = pe.transpose(ps[h][:, t * P:(t + 1) * P],
                                            y_c[:, 2 * j:2 * j + 2, :].rearrange("p b s -> p (b s)"), k.ident[:, :])
                    last.then_inc(yt_ready, 1)
                for b in range(BATCH):
                    for h in range(2):
                        if b == 0:
                            pe.wait_ge(yt_done, h + 1)
                        for c in range(KT):
                            i = (b * 2 + h) * KT + c
                            wait(pe, si_used, i - 3)
                            pe.matmul(ps[2 + i % 4][:, :], w_si[b * STATE:(b + 1) * STATE, c * P:(c + 1) * P],
                                      yt[b * STATE:(b + 1) * STATE, h * BANK:(h + 1) * BANK],
                                      start=True, stop=True).then_inc(si_ready, 1)
                for n in range(GROUPS):
                    pe.wait_ge(z_done, KT * (n + 1))
                    bank = (6, 7, 0, 1)[n]
                    for t in range(PER):
                        at = (n * PER + t) * P
                        for c in range(KT):
                            last = pe.matmul(ps[bank][:, t * P:(t + 1) * P], z[c][:, at:at + P], w_out[:, c, :],
                                             start=(c == 0), stop=(c == KT - 1))
                    last.then_inc(out_ready, 1)

            @block.scalar
            def _(act):
                act.wait_ge(loaded, 16 * LOADS)
                act.activation(w_in_hi[:, :], w_in[:, :], ACT.Copy).then_inc(split, 1)
                for m in range(2 * KT):
                    for n in range(GROUPS):
                        i = m * GROUPS + n
                        act.wait_ge(in_ready, i + 1)
                        b, h = n // 2, n % 2
                        if m < KT:
                            act.activation(xm[m][:, b, PAD + h * BANK:PAD + (h + 1) * BANK], ps[i % 8][:, :],
                                           ACT.Identity, bias=b_in[:, m:m + 1]).then_inc(in_used, 1)
                        else:
                            act.activation(sg[m - KT][:, n * BANK:(n + 1) * BANK], ps[i % 8][:, :],
                                           ACT.Sigmoid, bias=b_in[:, m:m + 1]).then_inc(in_used, 1)
                for b in range(BATCH):
                    for c in range(KT):
                        act.wait_ge(conv_done, b * KT + c + 1)
                        act.activation(xs[c][:, b * SEQ:(b + 1) * SEQ], cv[:, c, :], ACT.Silu, bias=conv_b[:, c:c + 1])\
                           .then_inc(conv_used, 1)
                act.wait_ge(ssm_ready, 12)
                for h in range(2):
                    act.activation(dt_t[:, h * BANK:(h + 1) * BANK], ps[h][:, :], ACT.Sigmoid, bias=b_s["dt"][:, :])\
                       .then_inc(dt_done, 1)
                act.wait_ge(centred, 1)
                act.activation(y_sq[:, :, :], y_c[:, :, :], ACT.Square).then_inc(squared, 1)
                act.wait_ge(varied, 1)
                act.activation(sd[:, :], var[:, :], ACT.Sqrt).then_inc(rooted, 1)
                for h in range(2):
                    act.wait_ge(yt_ready, h + 1)
                    act.activation(yt[:, h * BANK:(h + 1) * BANK], ps[h][:, :], ACT.Copy).then_inc(yt_done, 1)

            @block.vector
            def _(dve):
                count = [0]

                def then(ins):
                    count[0] += 1
                    ins.then_inc(link, 1)
                    dve.wait_ge(link, count[0])

                dve.wait_ge(split, 1)
                dve.tensor_tensor(w_in_lo[:, :], w_in[:, :], w_in_hi[:, :].bitcast(FP32), ALU.subtract)\
                   .then_inc(w_ready, 1)
                v = b_out[:, :].unsqueeze(1).to_broadcast([P, TILES, D])
                then(dve.tensor_tensor(k.x[:, :, :], k.x[:, :, :], v, ALU.add))
                dve.wait_ge(padded, KT)
                for b in range(BATCH):
                    for c in range(KT):
                        dve.wait_ge(in_used, (c * GROUPS) + 2 * (b + 1))
                        wait(dve, conv_used, (b - 1) * KT + c + 1)
                        o = cv[:, c, :]
                        then(dve.tensor_scalar(o, xm[c][:, b, 0:SEQ], conv_w[:, c, 0:1], None, ALU.mult))
                        then(dve.scalar_tensor_tensor(out=o, in0=xm[c][:, b, 1:SEQ + 1], scalar=conv_w[:, c, 1:2],
                                                      in1=o, op0=ALU.mult, op1=ALU.add))
                        dve.scalar_tensor_tensor(out=o, in0=xm[c][:, b, 2:SEQ + 2], scalar=conv_w[:, c, 2:3],
                                                 in1=o, op0=ALU.mult, op1=ALU.add).then_inc(conv_done, 1)
                for h in range(2):
                    r = slice(h * BANK, (h + 1) * BANK)
                    dve.wait_ge(dt_done, h + 1)
                    dve.tensor_scalar(decay[:, r], dt_t[:, r], -1.0, 1.0, ALU.mult, ALU.add)
                    then(dve.scalar_tensor_tensor(out=drive[:, r], in0=ps[2 + h][:, :], scalar=b_s["B"][:, :],
                                                  in1=dt_t[:, r], op0=ALU.add, op1=ALU.mult))
                    first = 0.0 if h == 0 else state[:, BANK - 1:BANK]
                    then(dve.tensor_tensor_scan(state[:, r], decay[:, r], drive[:, r], first, ALU.mult, ALU.add))
                    dve.scalar_tensor_tensor(out=y[:, r], in0=ps[4 + h][:, :], scalar=b_s["C"][:, :],
                                             in1=state[:, r], op0=ALU.add, op1=ALU.mult).then_inc(y_done, 1)
                for h in range(2):
                    dve.wait_ge(nat_ready, h + 1)
                    g = slice(h * PER * BATCH, (h + 1) * PER * BATCH)
                    dve.tensor_copy(y_nat[:, g, :], ps[6 + h][:, :].rearrange("p (t s) -> p t s", s=STATE))
                then(dve.engine_nop())
                then(dve.reduce_sum(st1[:, :], y_nat[:, :, :], AX.X))
                then(dve.tensor_scalar(mean[:, :], st1[:, :], 1.0 / STATE, None, ALU.mult))
                dve.tensor_tensor(y_c[:, :, :], y_nat[:, :, :], bcast(mean[:, :], STATE), ALU.subtract)\
                   .then_inc(centred, 1)
                dve.wait_ge(squared, 1)
                then(dve.reduce_sum(st1[:, :], y_sq[:, :, :], AX.X))
                dve.tensor_scalar(var[:, :], st1[:, :], 1.0 / STATE, EPS, ALU.mult, ALU.add).then_inc(varied, 1)
                dve.wait_ge(rooted, 1)
                then(dve.reciprocal(rstd[:, :], sd[:, :]))
                dve.tensor_tensor(y_c[:, :, :], y_c[:, :, :], bcast(rstd[:, :], STATE), ALU.mult).then_inc(normed, 1)
                for b in range(BATCH):
                    for h in range(2):
                        for c in range(KT):
                            i = (b * 2 + h) * KT + c
                            r = slice((b * 2 + h) * BANK, (b * 2 + h + 1) * BANK)
                            dve.wait_ge(si_ready, i + 1)
                            ins_ = dve.scalar_tensor_tensor(out=z[c][:, r], in0=xs[c][:, r], scalar=skip[:, c:c + 1],
                                                            in1=ps[2 + i % 4][:, :], op0=ALU.mult, op1=ALU.add)
                            ins_.then_inc(si_used, 1)
                            dve.wait_ge(si_used, i + 1)
                            dve.scalar_tensor_tensor(out=z[c][:, r], in0=z[c][:, r], scalar=b_si[:, c:c + 1],
                                                     in1=sg[c][:, r], op0=ALU.add, op1=ALU.mult).then_inc(z_done, 1)
                for n in range(GROUPS):
                    dve.wait_ge(out_ready, n + 1)
                    xv = k.x[:, n * PER:(n + 1) * PER, :]
                    dve.tensor_tensor(xv, xv, ps[(6, 7, 0, 1)[n]][:, :].rearrange("p (t d) -> p t d", t=PER), ALU.add)


class Box:
    pass


def hybrid_block_kernel(nc, ins, out, stop_after=None):
    x_view = ins["attn_a_x"].rearrange("b (t p) d -> p (b t) d", p=P)
    out_view = out.rearrange("b (t p) d -> p (b t) d", p=P)

    def pick(prefix):
        return {n[len(prefix):]: a for n, a in ins.items() if n.startswith(prefix)}

    def dump(t):
        with Scope(nc, "dump") as s:
            done = s.sem("done")
            with nc.Block() as block:
                @block.sync
                def _(sp):
                    sp.dma_start(out_view, t[:, :, :]).then_inc(done, 16)
                    sp.wait_ge(done, 16)

    with Scope(nc, "all") as s:
        k = Box()
        k.x = s.sb("x", [P, TILES, D])
        k.xhi = s.sb("xhi", [P, TOKENS], F32R)
        k.xlo = s.sb("xlo", [P, TOKENS], F32R)
        k.ident = s.sb("ident", [P, P])
        ident_made = s.sem("ident_made")
        with nc.Block() as block:
            @block.gpsimd
            def _(pool):
                pool.memset(k.ident[:, :], 0.0).then_inc(ident_made, 1)
                pool.wait_ge(ident_made, 1)
                pool.affine_select(out=k.ident[:, :], in_=k.ident[:, :], compare_op=ALU.not_equal, fill=1.0,
                                   base=0, pattern=[[-1, P]], channel_multiplier=1)

        def load_x(sp, sems):
            for n in range(GROUPS):
                sp.dma_start(k.x[:, n * PER:(n + 1) * PER, :], x_view[:, n * PER:(n + 1) * PER, :])\
                  .then_inc(sems[n], 16)

        with Scope(nc, "l1") as n1:
            k.xn = n1.sb("xn", [P, TILES, D])
            layernorm_transposed(nc, "n1", k, load=load_x)
        with Scope(nc, "a1") as a1:
            k.attn_t = a1.sb("attn_t", [P, PAIRS * BATCH * SEQ])
            attention(nc, k, ins["attn_a_W_qk"])
            project_out(nc, k, ins["attn_a_W_out"])
        if stop_after == "attention":
            return dump(k.x)
        with Scope(nc, "rest") as r:
            k.xn = r.sb("xn", [P, TILES, D])
            k.xr = r.sb("xr", [P, TILES, D])
            f = Box()
            shape = [P, EXPERTS + 2, INTER]
            f.wg_hi, f.wg_lo = r.sb("wg_hi", shape, F32R), r.sb("wg_lo", shape, F32R)
            f.wu_hi, f.wu_lo = r.sb("wu_hi", shape, F32R), r.sb("wu_lo", shape, F32R)
            f.wd = r.sb("wd", [P, STEPS, D])
            f.gate_hi, f.gate_lo = r.sb("gate_hi", [P, EXPERTS], F32R), r.sb("gate_lo", [P, EXPERTS], F32R)
            f.gate_b = r.sb("gate_b", [EXPERTS, 1])
            f.sel = r.sb("sel", [P, EXPERTS // 2, P], F32R)
            f.wt = r.sb("wt", [P, TOKENS], F32R)
            f.iota = r.sb("iota", [P, TILES, EXPERTS])
            moe_weights(nc, f, pick("ffn_"))
            mixture(nc, "m1", k, f)
            if stop_after == "moe":
                return dump(k.x)
            layernorm_transposed(nc, "n3", k)
            state_space(nc, k, pick("attn_b_"))
            if stop_after == "ssm":
                return dump(k.x)
            mixture(nc, "m2", k, f, store=out_view)


def kernel(**inputs):
    import numpy as np
    import concourse.bacc as bacc
    from concourse.bass_utils import run_bass_kernel_spmd

    nc = bacc.Bacc("TRN2", target_bir_lowering=False, num_devices=1)
    arrays, ins = {}, {}
    for name, a in inputs.items():
        a = np.ascontiguousarray(a)
        arrays[f"in_{name}"] = a
        ins[name[len("L0_"):]] = nc.dram_tensor(f"in_{name}", a.shape, mybir.dt.from_np(a.dtype),
                                                kind="ExternalInput").ap()
    out = nc.dram_tensor("out", (BATCH, SEQ, D), FP32, kind="ExternalOutput").ap()
    hybrid_block_kernel(nc, ins, out)
    result = run_bass_kernel_spmd(nc, [arrays], core_ids=[0])
    return result.results[0]["out"]
```

```python
from contextlib import ExitStack

import concourse.bass as bass
from concourse import mybir

FP32 = mybir.dt.float32
F32R = mybir.dt.float32r
BF16 = mybir.dt.bfloat16
I32 = mybir.dt.int32
ALU = mybir.AluOpType
ACT = mybir.ActivationFunctionType
AX = mybir.AxisListType

P = 128
BATCH, SEQ, D = 2, 1024, 128
TOKENS = BATCH * SEQ
TILES = TOKENS // P
BANK = 512
GROUPS = TOKENS // BANK
PER = BANK // P
EPS = 1e-5

HEADS, DH = 16, 64
PAIRS = HEADS // 2
QT = SEQ // P
BETA = DH ** -0.5
MASKED = -3.0e38

EXPERTS, INTER = 16, 64
STEPS = EXPERTS // 2 + 1

INNER, STATE, TAPS = 256, 64, 3


def wait(eng, sem, value):
    if not isinstance(value, int) or value > 0:
        eng.wait_ge(sem, value)


def bcast(ap, n):
    return ap.unsqueeze(2).to_broadcast([ap.shape[0], ap.shape[1], n])


class Scope:

    def __init__(self, nc, tag):
        self.nc, self.tag, self.stack = nc, tag, ExitStack()

    def __enter__(self):
        self.stack.__enter__()
        return self

    def __exit__(self, *a):
        return self.stack.__exit__(*a)

    def sb(self, name, shape, dt=FP32):
        return self.stack.enter_context(self.nc.sbuf_tensor(f"{self.tag}_{name}", shape, dt))

    def ps(self, name, n=1):
        banks = [self.stack.enter_context(self.nc.psum_tensor(f"{self.tag}_{name}{i}", [P, BANK], FP32))
                 for i in range(n)]
        return banks if n > 1 else banks[0]

    def sem(self, name):
        return self.stack.enter_context(self.nc.semaphore(f"{self.tag}_{name}"))


def layernorm_transposed(nc, tag, k, residual=None, load=None):
    with Scope(nc, tag) as s:
        tp = s.ps("tp", GROUPS)
        sq = s.sb("sq", [P, TILES, D])
        tot = s.sb("tot", [P, TILES])
        mean = s.sb("mean", [P, TILES])
        var = s.sb("var", [P, TILES])
        sd = s.sb("sd", [P, TILES])
        rstd = s.sb("rstd", [P, TILES])
        x_loaded = [s.sem(f"x_loaded{n}") for n in range(GROUPS)]
        summed, centred, squared = s.sem("summed"), s.sem("centred"), s.sem("squared")
        meaned, varied, rooted = s.sem("meaned"), s.sem("varied"), s.sem("rooted")
        inverted, normed = s.sem("inverted"), s.sem("normed")
        transposed, high, low = s.sem("transposed"), s.sem("high"), s.sem("low")

        def grp(t, n):
            return t[:, n * PER:(n + 1) * PER, :]

        def cols(t, n):
            return t[:, n * PER:(n + 1) * PER]

        with nc.Block() as block:
            if load:
                @block.sync
                def _(sp):
                    load(sp, x_loaded)

            @block.vector
            def _(dve):
                for n in range(GROUPS):
                    if load:
                        dve.wait_ge(x_loaded[n], 16)
                    dve.reduce_sum(cols(tot, n), grp(k.x, n), AX.X).then_inc(summed, 1)
                dve.wait_ge(summed, GROUPS)
                dve.tensor_scalar(mean[:, :], tot[:, :], 1.0 / D, None, ALU.mult).then_inc(meaned, 1)
                dve.wait_ge(meaned, 1)
                for n in range(GROUPS):
                    dve.tensor_tensor(grp(k.xn, n), grp(k.x, n), bcast(cols(mean, n), D),
                                      ALU.subtract).then_inc(centred, 1)
                for n in range(GROUPS):
                    dve.wait_ge(squared, n + 1)
                    dve.reduce_sum(cols(tot, n), grp(sq, n), AX.X).then_inc(summed, 1)
                dve.wait_ge(summed, 2 * GROUPS)
                dve.tensor_scalar(var[:, :], tot[:, :], 1.0 / D, EPS, ALU.mult, ALU.add).then_inc(varied, 1)
                dve.wait_ge(rooted, 1)
                dve.reciprocal(rstd[:, :], sd[:, :]).then_inc(inverted, 1)
                dve.wait_ge(inverted, 1)
                for n in range(GROUPS):
                    dve.tensor_tensor(grp(k.xn, n), grp(k.xn, n), bcast(cols(rstd, n), D),
                                      ALU.mult).then_inc(normed, 1)
                for n in range(GROUPS):
                    dve.wait_ge(high, n + 1)
                    c = slice(n * BANK, (n + 1) * BANK)
                    dve.tensor_tensor(k.xlo[:, c], tp[n][:, :], k.xhi[:, c].bitcast(FP32),
                                      ALU.subtract).then_inc(low, 1)
                if residual is not None:
                    dve.wait_ge(normed, GROUPS)
                    dve.tensor_tensor(residual[:, :, :], k.x[:, :, :], k.xn[:, :, :], ALU.add)

            @block.scalar
            def _(act):
                for n in range(GROUPS):
                    act.wait_ge(centred, n + 1)
                    act.activation(grp(sq, n), grp(k.xn, n), ACT.Square).then_inc(squared, 1)
                act.wait_ge(varied, 1)
                act.activation(sd[:, :], var[:, :], ACT.Sqrt).then_inc(rooted, 1)
                for n in range(GROUPS):
                    act.wait_ge(transposed, n + 1)
                    act.activation(k.xhi[:, n * BANK:(n + 1) * BANK], tp[n][:, :], ACT.Copy).then_inc(high, 1)

            @block.tensor
            def _(pe):
                for n in range(GROUPS):
                    pe.wait_ge(normed, n + 1)
                    for j in range(PER):
                        last = pe.transpose(tp[n][:, j * P:(j + 1) * P], k.xn[:, n * PER + j, :], k.ident[:, :])
                    last.then_inc(transposed, 1)


HALF = QT // 2
SCORE_CHUNKS = [(j, j, HALF) for j in range(HALF)] + [(j, max(j, HALF), QT) for j in range(QT)]
NCHUNK = len(SCORE_CHUNKS)
CHUNK_AT = [P * sum(b - a for _, a, b in SCORE_CHUNKS[:c]) for c in range(NCHUNK + 1)]
DIAGONAL = [c for c, (j, a, _) in enumerate(SCORE_CHUNKS) if a == j]
FIRST_HALF_STEPS = HALF
MAX_CHUNKS = [(i, 0, i + 1) for i in range(HALF)]
for _i in range(HALF, QT):
    MAX_CHUNKS += [(_i, 0, HALF), (_i, HALF, _i + 1)]
NMAX = len(MAX_CHUNKS)
MAX_PER_STEP = [1, 1, 1, 1, 1, 2, 2, 2, 1, 0, 0, 0]
MAX_FIRST = [sum(MAX_PER_STEP[:c]) for c in range(NCHUNK)]
PROJ_STEPS = [0, 2, 4, 6]
KNAT_STEPS = [2, 5]
MROW_STEP = 9
PROLOGUE_FILLS = 7
BODY_FILLS = [5, 3, 5, 3]


def attention(nc, k, w_qk):
    with Scope(nc, "at") as s:
        def four(name):
            return [[s.sb(f"{name}{u}{l}", [P, SEQ], F32R) for l in range(2)] for u in range(2)]
        qs, ks, q2, k2 = four("qs"), four("ks"), four("q2"), four("k2")
        probs = s.sb("probs", [P, CHUNK_AT[-1]])
        k_nat = [s.sb(f"k_nat{u}", [P, QT, 3, DH]) for u in range(2)]
        k_t = s.sb("k_t", [P, SEQ])
        w_raw = s.sb("w_raw", [P, 2, P])
        w_hi = s.sb("w_hi", [P, 2, P], F32R)
        w_lo = s.sb("w_lo", [P, 2, P], F32R)
        inv = s.sb("inv", [P, 2, BANK])
        row_max = s.sb("row_max", [P, 2, QT])
        half_max = s.sb("half_max", [P, 2, QT - HALF, 2])
        neg_block = s.sb("neg_block", [QT, QT, P])
        maskb = s.sb("maskb", [P, P], BF16)
        identb = s.sb("identb", [P, P], BF16)
        max_ps, sc_ps, out_ps, misc = s.ps("max", 2), s.ps("sc", 2), s.ps("out", 2), s.ps("misc", 2)

        consts, rows_set, pool_turns = s.sem("consts"), s.sem("rows_set"), s.sem("pool_turns")
        w_loaded, w_split = s.sem("w_loaded"), s.sem("w_split")
        proj_ready, knat_ps_ready = s.sem("proj_ready"), s.sem("knat_ps_ready")
        hi_done, lo_done, dup_done = s.sem("hi_done"), s.sem("lo_done"), s.sem("dup_done")
        kt_done, knat_done = s.sem("kt_done"), s.sem("knat_done")
        max_ready, max_taken = s.sem("max_ready"), s.sem("max_taken")
        row_max_done, row_max_t, mrow_done = s.sem("row_max_done"), s.sem("row_max_t"), s.sem("mrow_done")
        scores_ready, exp_done, masked = s.sem("scores_ready"), s.sem("exp_done"), s.sem("masked")
        av_done, ln_done = s.sem("av_done"), s.sem("ln_done")
        inv_done, out_used = s.sem("inv_done"), s.sem("out_used")

        wq_view = w_qk.rearrange("d (a c) -> d a c", a=2)

        def rows(l):
            return slice(DH * l, DH * l + DH)

        def fill_no(slot, i):
            return i if slot < 0 else PROLOGUE_FILLS + sum(BODY_FILLS[:slot]) + i

        def bank_of(slot, i):
            return fill_no(slot, i) % 2

        def fills(p):
            def unit_proj(slot, unit):
                return [(slot, i, lo_done, 8 * unit + 2 * i + 2) for i in range(4)]

            def unit_knat(slot, first, unit):
                return [(slot, first + i, knat_done, 2 * unit + i + 1) for i in range(2)]
            if p is None:
                return unit_proj(-1, 0) + unit_knat(-1, 4, 0) + [(-1, 6, mrow_done, 1)]
            found = unit_proj(0, 2 * p + 1) + [(0, 4, mrow_done, 4 * p + 2)]
            found += unit_knat(1, 0, 2 * p + 1) + [(1, 2, mrow_done, 4 * p + 3)]
            more = not is_last(p)
            found += (unit_proj(2, 2 * p + 2) if more else []) + [(2, 4, mrow_done, 4 * p + 4)]
            return found + (unit_knat(3, 0, 2 * p + 2) + [(3, 2, mrow_done, 4 * p + 5)] if more else [])

        def wait_fill_free(eng, p, slot, i):
            first = isinstance(p, int) and p == 0
            before = [] if slot < 0 else fills(None) if first else fills(p - 1)
            own = fills(None) if slot < 0 else fills(p)
            own = own[:[f[:2] for f in own].index((slot, i))]
            bank = bank_of(slot, i)
            for s_, i_, sem, value in reversed(before + own):
                if bank_of(s_, i_) == bank:
                    eng.wait_ge(sem, value)
                    break
            return bank

        def slots(emit, eng):
            for kk in range(4):
                emit(0, kk)
            with eng.Fori(1, PAIRS - 1) as p:
                for kk in range(4):
                    emit(p, kk)
            for kk in range(4):
                emit(PAIRS - 1, kk)

        def is_last(p, kk=3):
            return isinstance(p, int) and p == PAIRS - 1 and kk >= 3

        def next_unit(p, kk):
            return 2 * p + (1 if kk < 2 else 2)

        def no_prep(p, kk):
            return isinstance(p, int) and p == PAIRS - 1 and kk >= 2

        with nc.Block() as block:
            @block.sync
            def _(sp):
                def load_w(p):
                    wait(sp, w_split, 2 * p)
                    sp.dma_start(w_raw[:, :, :], wq_view[:, :, bass.ds(p * P, P)]).then_inc(w_loaded, 16)

                def duplicate(u, unit):
                    sp.wait_ge(hi_done, unit * 8 + 4)
                    for l in range(2):
                        sp.dma_start(q2[u][l][rows(l), :].bitcast(FP32),
                                     qs[u][l][rows(l), :].bitcast(FP32)).then_inc(dup_done, 16)
                    sp.wait_ge(hi_done, unit * 8 + 8)
                    for l in range(2):
                        sp.dma_start(ks[u][l][rows(1 - l), :].bitcast(FP32),
                                     ks[u][l][rows(l), :].bitcast(FP32)).then_inc(dup_done, 16)

                load_w(0)
                duplicate(0, 0)

                def body(p):
                    duplicate(1, 2 * p + 1)
                    if not is_last(p):
                        load_w(p + 1)
                        duplicate(0, 2 * p + 2)
                body(0)
                with sp.Fori(1, PAIRS - 1) as p:
                    body(p)
                body(PAIRS - 1)
                sp.wait_ge(dup_done, 64 * 2 * PAIRS)

            @block.gpsimd
            def _(pool):
                pool.memset(maskb[:, :], 0.0).then_inc(consts, 1)
                pool.memset(identb[:, :], 0.0).then_inc(consts, 1)
                pool.memset(neg_block[:, :, :], 0.0).then_inc(consts, 1)
                for u in range(2):
                    pool.memset(k_nat[u][:, :, 1, :], 1.0).then_inc(consts, 1)
                pool.wait_ge(consts, 5)
                pool.affine_select(out=maskb[:, :], in_=maskb[:, :], compare_op=ALU.is_ge, fill=MASKED,
                                   base=0, pattern=[[-1, P]], channel_multiplier=1).then_inc(consts, 1)
                pool.affine_select(out=identb[:, :], in_=identb[:, :], compare_op=ALU.not_equal, fill=1.0,
                                   base=0, pattern=[[-1, P]], channel_multiplier=1).then_inc(consts, 1)
                pool.affine_select(out=neg_block[:, :, :], in_=neg_block[:, :, :], compare_op=ALU.not_equal,
                                   fill=-1.0, base=0, pattern=[[-1, QT], [0, P]],
                                   channel_multiplier=1).then_inc(consts, 1)

                def split_w(p):
                    pool.wait_ge(w_loaded, 16 * (p + 1))
                    wait(pool, proj_ready, 8 * p)
                    pool.sem_inc(pool_turns, 1)
                    pool.tensor_copy(w_hi[:, :, :], w_raw[:, :, :]).then_inc(w_split, 1)
                    pool.wait_ge(w_split, 2 * p + 1)
                    pool.sem_inc(pool_turns, 1)
                    pool.tensor_tensor(w_lo[:, :, :], w_raw[:, :, :], w_hi[:, :, :].bitcast(FP32),
                                       ALU.subtract).then_inc(w_split, 1)

                split_w(0)

                def slot(p, kk):
                    h = 4 * p + kk
                    if kk == 1 and not is_last(p):
                        split_w(p + 1)
                    for c in DIAGONAL:
                        pool.wait_ge(exp_done, NCHUNK * h + c + 1)
                        pool.sem_inc(pool_turns, 1)
                        v = probs[:, CHUNK_AT[c]:CHUNK_AT[c] + P]
                        pool.affine_select(out=v, in_=v, compare_op=ALU.is_ge, fill=0.0, base=0,
                                           pattern=[[1, P]], channel_multiplier=-1).then_inc(masked, 1)
                slots(slot, pool)

            @block.scalar
            def _(act):
                def proj_half(p, slot_no, u, unit, i):
                    bank = bank_of(slot_no, i)
                    act.wait_ge(proj_ready, 4 * unit + i + 1)
                    c = slice((i % 2) * BANK, (i % 2 + 1) * BANK)
                    if i >= 2:
                        act.activation(k_t[:, c], misc[bank][:, :], ACT.Copy).then_inc(kt_done, 1)
                    dst = qs if i < 2 else ks
                    for l in range(2):
                        act.activation(dst[u][l][rows(l), c], misc[bank][rows(l), :], ACT.Copy)\
                           .then_inc(hi_done, 1)

                def knat_half(p, slot_no, u, unit, i):
                    bank = bank_of(slot_no, i)
                    act.wait_ge(knat_ps_ready, 2 * unit + (i % 4) + 1)
                    act.activation(k_nat[u][:, HALF * (i % 4):HALF * (i % 4 + 1), 0::2, :],
                                   misc[bank][:, :].rearrange("p (t l d) -> p t l d", t=HALF, l=2),
                                   ACT.Copy).then_inc(knat_done, 1)

                def invert(g, l, half):
                    act.wait_ge(av_done, NCHUNK * g + (NCHUNK if half else FIRST_HALF_STEPS))
                    act.activation(inv[rows(l), half, :], out_ps[half][rows(1 - l), :], ACT.Ln).then_inc(ln_done, 1)
                    act.wait_ge(ln_done, 2 * g + half + 1)
                    act.activation(inv[rows(l), half, :], inv[rows(l), half, :], ACT.Exp, scale=-1.0)\
                       .then_inc(inv_done, 1)

                act.preload_act_table_set("natural_log_exp_and_others")
                for i in range(4):
                    proj_half(0, -1, 0, 0, i)
                for i in range(2):
                    bank = bank_of(-1, 4 + i)
                    act.wait_ge(knat_ps_ready, i + 1)
                    act.activation(k_nat[0][:, HALF * i:HALF * (i + 1), 0::2, :],
                                   misc[bank][:, :].rearrange("p (t l d) -> p t l d", t=HALF, l=2),
                                   ACT.Copy).then_inc(knat_done, 1)

                def slot(p, kk):
                    h = 4 * p + kk
                    zero = isinstance(p, int) and p == 0
                    for c in range(NCHUNK):
                        act.wait_ge(scores_ready, NCHUNK * h + c + 1)
                        if not (zero and kk == 0):
                            act.wait_ge(av_done, NCHUNK * (h - 1) + c + 1)
                        a, b = CHUNK_AT[c], CHUNK_AT[c + 1]
                        bank = (NCHUNK * kk + c) % 2
                        act.activation(probs[:, a:b], sc_ps[bank][:, 0:b - a], ACT.Exp, scale=BETA)\
                           .then_inc(exp_done, 1)
                        if c == 0 and not (zero and kk < 2):
                            invert(h - 2, kk % 2, 1)
                        if c == FIRST_HALF_STEPS and not (zero and kk == 0):
                            invert(h - 1, (kk + 1) % 2, 0)
                        if not no_prep(p, kk):
                            unit, u = next_unit(p, kk), (kk // 2 + 1) % 2
                            if kk % 2 == 0 and c - 1 in PROJ_STEPS:
                                proj_half(p, kk, u, unit, PROJ_STEPS.index(c - 1))
                            if kk % 2 == 1 and c - 1 in KNAT_STEPS:
                                knat_half(p, kk, u, unit, KNAT_STEPS.index(c - 1))
                slots(slot, act)
                invert(4 * PAIRS - 2, 0, 1)
                invert(4 * PAIRS - 1, 1, 0)
                invert(4 * PAIRS - 1, 1, 1)

            @block.vector
            def _(dve):
                for u in range(2):
                    for l in range(2):
                        o = DH * (1 - l)
                        dve.memset(q2[u][l][o:o + DH, :].bitcast(FP32), 0.0).then_inc(rows_set, 1)
                        dve.memset(k2[u][l][o:o + DH, :].bitcast(FP32), 0.0).then_inc(rows_set, 1)
                dve.wait_ge(rows_set, 8)
                for u in range(2):
                    for l in range(2):
                        o = DH * (1 - l)
                        dve.memset(k2[u][l][o:o + QT, :].bitcast(FP32), 1.0).then_inc(rows_set, 1)

                def low_half(p, slot_no, u, unit, i):
                    bank = bank_of(slot_no, i)
                    c = slice((i % 2) * BANK, (i % 2 + 1) * BANK)
                    for l in range(2):
                        dve.wait_ge(hi_done, 8 * unit + 2 * i + l + 1)
                        if i < 2:
                            dst, hi = qs[u][l][rows(1 - l), c], qs[u][l][rows(l), c]
                        else:
                            dst, hi = k2[u][l][rows(l), c], ks[u][l][rows(l), c]
                        dve.tensor_tensor(dst, misc[bank][rows(l), :], hi.bitcast(FP32), ALU.subtract)\
                           .then_inc(lo_done, 1)

                def maxima(h, kk, c):
                    i, a, b = MAX_CHUNKS[c]
                    dst = row_max[:, kk % 2, i:i + 1] if i < HALF else half_max[:, kk % 2, i - HALF, (a > 0):(a > 0) + 1]
                    dve.wait_ge(max_ready, NMAX * h + c + 1)
                    dve.reduce_max(dst, max_ps[(NMAX * kk + c) % 2][:, 0:(b - a) * P], AX.X).then_inc(max_taken, 1)

                def join_maxima(h, kk):
                    dve.wait_ge(max_taken, NMAX * (h + 1))
                    dve.reduce_max(row_max[:, kk % 2, HALF:QT], half_max[:, kk % 2, :, :], AX.X)\
                       .then_inc(row_max_done, 1)

                def max_row(h, p, slot_no, i, u, l):
                    bank = bank_of(slot_no, i)
                    dve.wait_ge(row_max_t, h + 1)
                    o = DH * (1 - l)
                    mt = misc[bank][0:QT, 0:P].unsqueeze(1).to_broadcast([QT, QT, P])
                    dve.tensor_tensor(q2[u][l][o:o + QT, :].rearrange("r (i q) -> r i q", i=QT), mt,
                                      neg_block[:, :, :], ALU.mult)\
                       .then_inc(mrow_done, 1)

                def scale_out(g, p, kk, half):
                    l = kk % 2
                    dve.wait_ge(inv_done, 2 * g + half + 1)
                    at = p * (BATCH * SEQ) + (kk // 2) * SEQ + half * BANK
                    dve.tensor_tensor(k.attn_t[rows(l), bass.ds(at, BANK)], out_ps[half][rows(l), :],
                                      inv[rows(l), half, :], ALU.mult).then_inc(out_used, 1)

                for i in range(4):
                    low_half(0, -1, 0, 0, i)
                for c in range(NMAX):
                    maxima(0, 0, c)
                join_maxima(0, 0)
                dve.wait_ge(consts, 8)
                dve.wait_ge(rows_set, 12)
                max_row(0, 0, -1, 6, 0, 0)

                def slot(p, kk):
                    h = 4 * p + kk
                    zero = isinstance(p, int) and p == 0
                    nk = (kk + 1) % 4
                    for c in range(NCHUNK):
                        if not is_last(p, kk):
                            for m in range(MAX_FIRST[c], MAX_FIRST[c] + MAX_PER_STEP[c]):
                                maxima(h + 1, nk, m)
                        if c == 2 and not (zero and kk < 2):
                            scale_out(h - 2, p if kk >= 2 else p - 1, (kk + 2) % 4, 1)
                        if c == FIRST_HALF_STEPS + 1 and not (zero and kk == 0):
                            scale_out(h - 1, p if kk >= 1 else p - 1, (kk + 3) % 4, 0)
                        if kk % 2 == 0 and not no_prep(p, kk) and c - 2 in PROJ_STEPS:
                            low_half(p, kk, (kk // 2 + 1) % 2, next_unit(p, kk), PROJ_STEPS.index(c - 2))
                        if c == MROW_STEP - 1 and not is_last(p, kk):
                            join_maxima(h + 1, nk)
                    if not is_last(p, kk):
                        max_row(h + 1, p, kk, BODY_FILLS[kk] - 1, nk // 2, nk % 2)
                slots(slot, dve)
                last = PAIRS - 1
                scale_out(4 * PAIRS - 2, last, 2, 1)
                scale_out(4 * PAIRS - 1, last, 3, 0)
                scale_out(4 * PAIRS - 1, last, 3, 1)

            @block.tensor
            def _(pe):
                def project(p, slot_no, b, unit, i):
                    bank = wait_fill_free(pe, p, slot_no, i)
                    a = i // 2
                    c = slice(b * SEQ + (i % 2) * BANK, b * SEQ + (i % 2 + 1) * BANK)
                    pe.matmul(misc[bank][:, :], w_hi[:, a, :], k.xhi[:, c], start=True, stop=False)
                    pe.matmul(misc[bank][:, :], w_hi[:, a, :], k.xlo[:, c], start=False, stop=False)
                    pe.matmul(misc[bank][:, :], w_lo[:, a, :], k.xhi[:, c], start=False, stop=True)\
                      .then_inc(proj_ready, 1)

                def turn_k(p, slot_no, first, unit, i):
                    bank = wait_fill_free(pe, p, slot_no, first + i)
                    pe.wait_ge(kt_done, 2 * unit + i + 1)
                    for t in range(HALF):
                        j = HALF * i + t
                        last = pe.transpose(misc[bank][:, t * P:(t + 1) * P], k_t[:, j * P:(j + 1) * P],
                                            k.ident[:, :])
                    last.then_inc(knat_ps_ready, 1)

                def max_scores(h, kk, c):
                    i, a, b = MAX_CHUNKS[c]
                    u, l = kk // 2, kk % 2
                    n = (NMAX * kk + c) % 2
                    wait(pe, max_taken, NMAX * h + c - 1)
                    diag = b == i + 1
                    pe_last = pe.matmul(max_ps[n][:, 0:(b - a) * P], qs[u][l][:, i * P:(i + 1) * P],
                                        ks[u][l][:, a * P:b * P], start=True, stop=not diag)
                    if diag:
                        o = (i - a) * P
                        pe_last = pe.matmul(max_ps[n][:, o:o + P], identb[:, :], maskb[:, :], start=False, stop=True)
                    pe_last.then_inc(max_ready, 1)

                def wait_unit(unit):
                    pe.wait_ge(hi_done, 8 * (unit + 1))
                    pe.wait_ge(lo_done, 8 * (unit + 1))
                    pe.wait_ge(dup_done, 64 * (unit + 1))

                def turn_max(h, kk, p, slot_no, i):
                    bank = wait_fill_free(pe, p, slot_no, i)
                    pe.wait_ge(row_max_done, h + 1)
                    pe.transpose(misc[bank][0:QT, 0:P], row_max[:, kk % 2, :], k.ident[:, :])\
                      .then_inc(row_max_t, 1)

                def scores(h, kk, c):
                    j, a, b = SCORE_CHUNKS[c]
                    u, l = kk // 2, kk % 2
                    n = (NCHUNK * kk + c) % 2
                    if c == 0:
                        pe.wait_ge(mrow_done, h + 1)
                    wait(pe, exp_done, NCHUNK * h + c - 1)
                    o = sc_ps[n][:, 0:(b - a) * P]
                    pe.matmul(o, ks[u][l][:, j * P:(j + 1) * P], qs[u][l][:, a * P:b * P], start=True, stop=False)
                    pe.matmul(o, k2[u][l][:, j * P:(j + 1) * P], q2[u][l][:, a * P:b * P], start=False, stop=True)\
                      .then_inc(scores_ready, 1)

                def outputs(g, kk, c):
                    j, a, b = SCORE_CHUNKS[c]
                    u, l = kk // 2, kk % 2
                    half = int(c >= FIRST_HALF_STEPS)
                    if c == 0:
                        pe.wait_ge(masked, len(DIAGONAL) * (g + 1) - 2)
                    if c >= NCHUNK - 2:
                        pe.wait_ge(masked, len(DIAGONAL) * g + DIAGONAL.index(c) + 1)
                    if c in (0, FIRST_HALF_STEPS):
                        wait(pe, out_used, 2 * g + half - 1)
                    o = (a - half * HALF) * P
                    kn = k_nat[u][:, j, l:l + 2, :].rearrange("p l d -> p (l d)")
                    pe.matmul(out_ps[half][:, o:o + (b - a) * P], kn, probs[:, CHUNK_AT[c]:CHUNK_AT[c + 1]],
                              start=(j == 0), stop=(c in (FIRST_HALF_STEPS - 1, NCHUNK - 1)))\
                      .then_inc(av_done, 1)

                pe.wait_ge(w_split, 2)
                for i in range(4):
                    project(0, -1, 0, 0, i)
                for i in range(2):
                    turn_k(0, -1, 4, 0, i)
                wait_unit(0)
                pe.wait_ge(consts, 8)
                pe.wait_ge(rows_set, 12)
                for c in range(NMAX):
                    max_scores(0, 0, c)
                turn_max(0, 0, 0, -1, 6)

                def slot(p, kk):
                    h = 4 * p + kk
                    zero = isinstance(p, int) and p == 0
                    nk = (kk + 1) % 4
                    for c in range(NCHUNK):
                        if not (zero and kk == 0):
                            if c == 0 and kk % 2 == 1:
                                pe.wait_ge(knat_done, 2 * (2 * p + kk // 2 + 1))
                            outputs(h - 1, (kk + 3) % 4, c)
                        scores(h, kk, c)
                        if not is_last(p, kk):
                            if c == 0 and kk % 2 == 1:
                                wait_unit(next_unit(p, kk))
                            for m in range(MAX_FIRST[c], MAX_FIRST[c] + MAX_PER_STEP[c]):
                                max_scores(h + 1, nk, m)
                        if not no_prep(p, kk):
                            unit = next_unit(p, kk)
                            if kk % 2 == 0 and c in PROJ_STEPS:
                                if kk == 2 and c == PROJ_STEPS[0]:
                                    pe.wait_ge(w_split, 2 * (p + 2))
                                project(p, kk, (kk // 2 + 1) % 2, unit, PROJ_STEPS.index(c))
                            if kk % 2 == 1 and c in KNAT_STEPS:
                                turn_k(p, kk, 0, unit, KNAT_STEPS.index(c))
                        if c == MROW_STEP and not is_last(p, kk):
                            turn_max(h + 1, nk, p, kk, BODY_FILLS[kk] - 1)
                slots(slot, pe)
                for c in range(NCHUNK):
                    outputs(4 * PAIRS - 1, 3, c)


RING = 2
BUFS = 3
LAST = STEPS - 1
NSTEPS = STEPS * GROUPS
PREPARE = dict(centre=-21, square=-19, variance=-18, root=-16, norm=-16, residual=-15, turn=-14, high=-13,
               low=-13, logits=-10, sigmoid=-9, natural=-7, route1=-7, route2=-6, route3=-5, turn_w=-3,
               w_high=-2, w_low=-3)
FINISH = dict(add_up=1, centre=2, square=4, variance=5, root=6, norm=6, turn=7, high=8, low=8)
SOURCE_TILES = [[-23, -22.8, -22.6, -22.4], [-20, -19, -18, -17], [-13, -10, -9, -6.5], [-6.4, -6.3, -6.2, -2.5]]
SOURCE_ADDED = [-22, -12.5, -4.5, -1.3]
ORDER = ["source", "add_up"] + list(PREPARE)


def agenda(pieces, with_finish, tiles=False):
    found = []
    for n in range(GROUPS):
        for piece in pieces:
            if piece == "source":
                found += [(at, piece, n, t) for t, at in enumerate(SOURCE_TILES[n])] if tiles else \
                    [(SOURCE_ADDED[n], piece, n, 0)]
            if piece in PREPARE:
                found.append((PREPARE[piece] + STEPS * n, piece, n, "prepare"))
            if piece in FINISH and (with_finish or piece == "add_up"):
                found.append((FINISH[piece] + STEPS * (n + 1), piece, n, "finish"))
    return sorted(found, key=lambda f: (f[0], ORDER.index(f[1])))


class GroupNorm:

    def __init__(self, s, tag):
        self.xc, self.sq, self.xn = [s.sb(f"{tag}_{n}", [P, PER, D]) for n in ("xc", "sq", "xn")]
        self.tot, self.mean, self.tot2, self.var, self.sd, self.rstd = [
            s.sb(f"{tag}_{n}", [P, PER]) for n in ("tot", "mean", "tot2", "var", "sd", "rstd")]
        self.small, self.centred, self.squared, self.varied, self.rooted, self.normed, self.turned, \
            self.high, self.low = [s.sem(f"{tag}_{n}") for n in (
                "small", "centred", "squared", "varied", "rooted", "normed", "turned", "high", "low")]

    def centre(self, dve, n, x):
        dve.reduce_sum(self.tot[:, :], x, AX.X).then_inc(self.small, 1)
        dve.wait_ge(self.small, 4 * n + 1)
        dve.tensor_scalar(self.mean[:, :], self.tot[:, :], 1.0 / D, None, ALU.mult).then_inc(self.small, 1)
        dve.wait_ge(self.small, 4 * n + 2)
        dve.tensor_tensor(self.xc[:, :, :], x, bcast(self.mean[:, :], D), ALU.subtract).then_inc(self.centred, 1)

    def variance(self, dve, n):
        dve.wait_ge(self.squared, n + 1)
        dve.reduce_sum(self.tot2[:, :], self.sq[:, :, :], AX.X).then_inc(self.small, 1)
        dve.wait_ge(self.small, 4 * n + 3)
        dve.tensor_scalar(self.var[:, :], self.tot2[:, :], 1.0 / D, EPS, ALU.mult, ALU.add).then_inc(self.varied, 1)

    def norm(self, dve, n):
        dve.wait_ge(self.rooted, n + 1)
        dve.reciprocal(self.rstd[:, :], self.sd[:, :]).then_inc(self.small, 1)
        dve.wait_ge(self.small, 4 * n + 4)
        wait(dve, self.turned, n)
        dve.tensor_tensor(self.xn[:, :, :], self.xc[:, :, :], bcast(self.rstd[:, :], D), ALU.mult)\
           .then_inc(self.normed, 1)

    def low_part(self, dve, n, lo, hi, bank):
        dve.wait_ge(self.high, n + 1)
        dve.tensor_tensor(lo, bank[:, :], hi.bitcast(FP32), ALU.subtract).then_inc(self.low, 1)

    def square(self, act, n):
        act.wait_ge(self.centred, n + 1)
        act.activation(self.sq[:, :, :], self.xc[:, :, :], ACT.Square).then_inc(self.squared, 1)

    def root(self, act, n):
        act.wait_ge(self.varied, n + 1)
        act.activation(self.sd[:, :], self.var[:, :], ACT.Sqrt).then_inc(self.rooted, 1)

    def high_part(self, act, n, hi, bank):
        act.wait_ge(self.turned, n + 1)
        act.activation(hi, bank[:, :], ACT.Copy).then_inc(self.high, 1)

    def turn(self, pe, n, bank, ident):
        pe.wait_ge(self.normed, n + 1)
        for t in range(PER):
            last = pe.transpose(bank[:, t * P:(t + 1) * P], self.xn[:, t, :], ident[:, :])
        last.then_inc(self.turned, 1)


def mixture(nc, tag, k, f, source, source_ready=None, weights=None, next_norm=False, store=None, prefetch=None):
    with Scope(nc, tag) as s:
        g_ps, u_ps, wb_ps, acc, misc = s.ps("g", RING), s.ps("u", RING), s.ps("wb"), s.ps("acc"), s.ps("misc", 2)
        src_ps = [g_ps[0], g_ps[1], u_ps[0], u_ps[1]]
        gate = [s.sb(f"gate{r}", [P, BANK]) for r in range(BUFS)]
        prod = [s.sb(f"prod{r}", [P, BANK]) for r in range(BUFS)]
        hid = [s.sb(f"hid{r}", [P, BANK]) for r in range(BUFS)]
        wb = [s.sb(f"wb_copy{r}", [P, BANK]) for r in range(2)]
        wb_copied = s.sem("wb_copied")
        g_ready, u_ready, wb_ready = s.sem("g_ready"), s.sem("u_ready"), s.sem("wb_ready")
        gated, weighted = s.sem("gated"), s.sem("weighted")
        hid_ready, down_done, acc_used, stored = s.sem("hid_ready"), s.sem("down_done"), s.sem("acc_used"), s.sem("stored")
        sourced, added, summed = s.sem("sourced"), s.sem("added"), s.sem("summed")
        before, after = GroupNorm(s, "before"), GroupNorm(s, "after")
        score_t = s.sb("score_t", [EXPERTS, BANK])
        full = [P, PER, EXPERTS]
        sc, eq, key, one1, one2, sc2, w1, w2, w = [
            s.sb(n, full) for n in ("sc", "eq", "key", "one1", "one2", "sc2", "w1", "w2", "w")]
        v1, v2, i1, i2, den, rec, r1, r2 = [
            s.sb(n, [P, PER]) for n in ("v1", "v2", "i1", "i2", "den", "rec", "r1", "r2")]
        logit_ready, scored, nat_ready, nat_read = [s.sem(n) for n in ("logit_ready", "scored", "nat_ready", "nat_read")]
        route_step, w_ready, wt_ready, wt_high, wt_low = [
            s.sem(n) for n in ("route_step", "w_ready", "wt_ready", "wt_high", "wt_low")]
        if weights:
            raw = {n: s.sb(f"raw_{n}", [P, EXPERTS + 2, INTER]) for n in ("wg", "wu")}
            gate_raw = s.sb("gate_raw", [P, EXPERTS])
            sel = s.sb("sel", [P, EXPERTS // 2, P])
            iota_i = s.sb("iota_i", full, I32)
        loaded, split, padded = s.sem("loaded"), s.sem("split"), s.sem("padded")
        low_split, iota_made, sel_made, const_done = [s.sem(n) for n in ("low_split", "iota_made", "sel_made", "const_done")]

        def grp(t, n):
            return t[:, n * PER:(n + 1) * PER, :]

        def cols(n):
            return slice(n * BANK, (n + 1) * BANK)

        def ahead(g):
            return g < NSTEPS and g % STEPS < LAST

        def interleave(pieces, emit, step, tiles=False):
            todo = agenda(pieces, next_norm, tiles)
            for g in range(-1, NSTEPS):
                if g >= 0:
                    step(g)
                while todo and todo[0][0] <= g:
                    emit(*todo.pop(0)[1:])
                if g == -1:
                    step(None)
            step(NSTEPS)
            for item in todo:
                emit(*item[1:])

        with nc.Block() as block:
            @block.tensor
            def _(pe):
                def up(out, hi, lo, st, n):
                    wh = hi[:, 2 * st:2 * st + 2, :].rearrange("p e i -> p (e i)")
                    wl = lo[:, 2 * st:2 * st + 2, :].rearrange("p e i -> p (e i)")
                    pe.matmul(out[:, :], wh, k.xhi[:, cols(n)], start=True, stop=False)
                    pe.matmul(out[:, :], wh, k.xlo[:, cols(n)], start=False, stop=False)
                    return pe.matmul(out[:, :], wl, k.xhi[:, cols(n)], start=False, stop=True)

                def down(g):
                    n, st = divmod(g, STEPS)
                    pe.wait_ge(hid_ready, g + 1)
                    if st == 0:
                        wait(pe, acc_used, n)
                    for t in range(PER):
                        last = pe.matmul(acc[:, t * P:(t + 1) * P], hid[g % BUFS][:, t * P:(t + 1) * P],
                                         f.wd[:, st, :], start=(st == 0 and t == 0), stop=(st == LAST),
                                         skip_group_check=True)
                    last.then_inc(down_done, 1)

                def spread(g):
                    n, st = divmod(g, STEPS)
                    if st == 0:
                        pe.wait_ge(wt_low, n + 1)
                    wait(pe, wb_copied, LAST * n + st)
                    pe.matmul(wb_ps[:, :], f.sel[:, st, :], f.wt[:, cols(n)],
                              start=True, stop=True).then_inc(wb_ready, 1)

                def step(g):
                    if g is None:
                        pe.wait_ge(added, GROUPS)
                        if weights:
                            pe.wait_ge(low_split, 3)
                            pe.wait_ge(const_done, 1)
                        return
                    if g == NSTEPS:
                        down(g - 2)
                        return down(g - 1)
                    n, st = divmod(g, STEPS)
                    r = g % RING
                    if st == 0:
                        pe.wait_ge(before.low, n + 1)
                    wait(pe, gated, g - RING + 1)
                    up(g_ps[r], f.wg_hi, f.wg_lo, st, n).then_inc(g_ready, 1)
                    if g == 0:
                        spread(0)
                        spread(1)
                    elif ahead(g + 1):
                        spread(g + 1)
                    wait(pe, hid_ready, g - RING + 1)
                    up(u_ps[r], f.wu_hi, f.wu_lo, st, n).then_inc(u_ready, 1)
                    if g > 1:
                        down(g - 2)

                def emit(piece, n, kind):
                    if piece == "source":
                        if source_ready and n == 0 and kind == 0:
                            source_ready(pe)
                        last = source(pe, n * PER + kind, src_ps[n][:, kind * P:(kind + 1) * P])
                        if kind == PER - 1:
                            last.then_inc(sourced, 1)
                    elif piece == "turn" and kind == "prepare":
                        wait(pe, nat_read, n)
                        before.turn(pe, n, misc[0], k.ident)
                    elif piece == "turn":
                        if n == 0:
                            pe.wait_ge(before.low, GROUPS)
                        else:
                            pe.wait_ge(nat_read, GROUPS)
                            pe.wait_ge(after.low, n)
                        after.turn(pe, n, misc[0], k.ident)
                    elif piece == "logits":
                        if n == 0 and weights:
                            pe.wait_ge(low_split, 1)
                        pe.wait_ge(before.low, n + 1)
                        wait(pe, wt_low, n)
                        o = misc[1][0:EXPERTS, :]
                        pe.matmul(o, f.gate_hi[:, :], k.xhi[:, cols(n)], start=True, stop=False)
                        pe.matmul(o, f.gate_hi[:, :], k.xlo[:, cols(n)], start=False, stop=False)
                        pe.matmul(o, f.gate_lo[:, :], k.xhi[:, cols(n)], start=False, stop=True)\
                          .then_inc(logit_ready, 1)
                    elif piece == "natural":
                        pe.wait_ge(scored, n + 1)
                        if next_norm:
                            wait(pe, after.low, n - 2)
                        for t in range(PER):
                            last = pe.transpose(misc[0][:, t * EXPERTS:(t + 1) * EXPERTS],
                                                score_t[:, t * P:(t + 1) * P], k.ident[0:EXPERTS, 0:EXPERTS])
                        last.then_inc(nat_ready, 1)
                    elif piece == "turn_w":
                        pe.wait_ge(w_ready, n + 1)
                        for t in range(PER):
                            last = pe.transpose(misc[1][0:EXPERTS, t * P:(t + 1) * P], w[:, t, :], k.ident[:, :])
                        last.then_inc(wt_ready, 1)
                interleave(("source", "turn", "logits", "natural", "turn_w"), emit, step, tiles=True)

            @block.scalar
            def _(act):
                def copy_weights(g):
                    n, st = divmod(g, STEPS)
                    act.wait_ge(wb_ready, LAST * n + st + 1)
                    wait(act, weighted, LAST * n + st - 1)
                    act.activation(wb[(LAST * n + st) % 2][:, :], wb_ps[:, :], ACT.Copy).then_inc(wb_copied, 1)

                def step(g):
                    if g is None or g == NSTEPS:
                        return
                    if g == 0:
                        copy_weights(0)
                    act.wait_ge(g_ready, g + 1)
                    wait(act, hid_ready, g - BUFS + 1)
                    act.activation(gate[g % BUFS][:, :], g_ps[g % RING][:, :], ACT.Silu).then_inc(gated, 1)
                    if ahead(g + 1):
                        copy_weights(g + 1)

                def emit(piece, n, kind):
                    norm = before if kind == "prepare" else after
                    if piece == "square":
                        norm.square(act, n)
                        if weights and n == 0 and norm is before:
                            act.wait_ge(loaded, 16 * 8)
                            act.activation(f.gate_hi[:, :], gate_raw[:, :], ACT.Copy).then_inc(split, 1)
                            act.wait_ge(padded, 4)
                            act.activation(f.wg_hi[:, :, :], raw["wg"][:, :, :], ACT.Copy).then_inc(split, 1)
                            act.activation(f.wu_hi[:, :, :], raw["wu"][:, :, :], ACT.Copy).then_inc(split, 1)
                    elif piece == "root":
                        norm.root(act, n)
                    elif piece == "high":
                        norm.high_part(act, n, k.xhi[:, cols(n)], misc[0])
                    elif piece == "sigmoid":
                        act.wait_ge(logit_ready, n + 1)
                        wait(act, nat_ready, n)
                        act.activation(score_t[:, :], misc[1][0:EXPERTS, :], ACT.Sigmoid, bias=f.gate_b[:, :])\
                           .then_inc(scored, 1)
                        if weights and n == 0:
                            act.wait_ge(sel_made, 5)
                            act.activation(f.sel[:, :, :], sel[:, :, :], ACT.Copy).then_inc(const_done, 1)
                    elif piece == "w_high":
                        act.wait_ge(wt_ready, n + 1)
                        if weights and n == 0:
                            act.wait_ge(padded, 4)
                        act.activation(f.wt[0:EXPERTS, cols(n)], misc[1][0:EXPERTS, :], ACT.Copy)\
                           .then_inc(wt_high, 1)
                interleave(("square", "root", "high", "sigmoid", "w_high"), emit, step)

            @block.vector
            def _(dve):
                count = [0]

                def then(ins):
                    count[0] += 1
                    ins.then_inc(route_step, 1)
                    dve.wait_ge(route_step, count[0])

                def largest(x, v, i, one):
                    then(dve.reduce_max(v[:, :], x[:, :, :], AX.X))
                    then(dve.tensor_tensor(eq[:, :, :], x[:, :, :], bcast(v[:, :], EXPERTS), ALU.is_equal))
                    then(dve.scalar_tensor_tensor(out=key[:, :, :], in0=eq[:, :, :], scalar=-100.0,
                                                  in1=f.iota[:, :, :], op0=ALU.mult, op1=ALU.add))
                    then(dve.tensor_reduce(i[:, :], key[:, :, :], AX.X, ALU.min))
                    then(dve.tensor_tensor(one[:, :, :], key[:, :, :], bcast(i[:, :], EXPERTS), ALU.is_equal))

                def step(g):
                    if g is None or g == NSTEPS:
                        return
                    n, st = divmod(g, STEPS)
                    r = g % BUFS
                    if st < LAST:
                        dve.wait_ge(weighted, LAST * n + st + 1)
                    else:
                        dve.wait_ge(gated, g + 1)
                    dve.wait_ge(u_ready, g + 1)
                    wait(dve, down_done, g - BUFS + 1)
                    left = prod[r] if st < LAST else gate[r]
                    dve.tensor_tensor(hid[r][:, :], left[:, :], u_ps[g % RING][:, :], ALU.mult).then_inc(hid_ready, 1)

                def emit(piece, n, kind):
                    norm = before if kind == "prepare" else after
                    if piece == "source":
                        dve.wait_ge(sourced, n + 1)
                        dve.tensor_tensor(grp(k.x, n), grp(k.x, n),
                                          src_ps[n][:, :].rearrange("p (t d) -> p t d", t=PER), ALU.add)\
                           .then_inc(added, 1)
                    elif piece == "centre":
                        if norm is before:
                            dve.wait_ge(added, n + 1)
                        else:
                            dve.wait_ge(acc_used, n + 1)
                        norm.centre(dve, n, grp(k.x, n))
                    elif piece == "variance":
                        norm.variance(dve, n)
                    elif piece == "norm":
                        if norm is before:
                            wait(dve, summed, n)
                        norm.norm(dve, n)
                        if weights and n == 0 and norm is before:
                            for i, (lo, hi, src) in enumerate(((f.gate_lo[:, :], f.gate_hi[:, :], gate_raw[:, :]),
                                                               (f.wg_lo[:, :, :], f.wg_hi[:, :, :], raw["wg"][:, :, :]),
                                                               (f.wu_lo[:, :, :], f.wu_hi[:, :, :], raw["wu"][:, :, :]))):
                                dve.wait_ge(split, i + 1)
                                dve.tensor_tensor(lo, src, hi.bitcast(FP32), ALU.subtract).then_inc(low_split, 1)
                    elif piece == "low":
                        norm.low_part(dve, n, k.xlo[:, cols(n)], k.xhi[:, cols(n)], misc[0])
                    elif piece == "route1":
                        if weights and n == 0:
                            dve.wait_ge(iota_made, 1)
                            then(dve.tensor_copy(f.iota[:, :, :], iota_i[:, :, :]))
                        dve.wait_ge(nat_ready, n + 1)
                        dve.tensor_copy(sc[:, :, :], misc[0][:, 0:PER * EXPERTS].rearrange("p (t e) -> p t e", t=PER))\
                           .then_inc(nat_read, 1)
                        dve.wait_ge(nat_read, n + 1)
                        largest(sc, v1, i1, one1)
                        then(dve.scalar_tensor_tensor(out=sc2[:, :, :], in0=one1[:, :, :], scalar=-4.0,
                                                      in1=sc[:, :, :], op0=ALU.mult, op1=ALU.add))
                    elif piece == "route2":
                        largest(sc2, v2, i2, one2)
                    elif piece == "route3":
                        then(dve.tensor_tensor(den[:, :], v1[:, :], v2[:, :], ALU.add))
                        then(dve.reciprocal(rec[:, :], den[:, :]))
                        dve.tensor_tensor(r1[:, :], v1[:, :], rec[:, :], ALU.mult)
                        then(dve.tensor_tensor(r2[:, :], v2[:, :], rec[:, :], ALU.mult))
                        dve.tensor_tensor(w1[:, :, :], one1[:, :, :], bcast(r1[:, :], EXPERTS), ALU.mult)
                        then(dve.tensor_tensor(w2[:, :, :], one2[:, :, :], bcast(r2[:, :], EXPERTS), ALU.mult))
                        wait(dve, wt_ready, n)
                        dve.tensor_tensor(w[:, :, :], w1[:, :, :], w2[:, :, :], ALU.add).then_inc(w_ready, 1)
                    elif piece == "w_low":
                        dve.wait_ge(wt_high, n + 1)
                        dve.tensor_tensor(f.wt[32:32 + EXPERTS, cols(n)], misc[1][0:EXPERTS, :],
                                          f.wt[0:EXPERTS, cols(n)].bitcast(FP32), ALU.subtract).then_inc(wt_low, 1)
                    elif piece == "add_up":
                        dve.wait_ge(down_done, STEPS * (n + 1))
                        dve.wait_ge(summed, n + 1)
                        dve.tensor_tensor(grp(k.x, n), grp(k.xr, n),
                                          acc[:, :].rearrange("p (t d) -> p t d", t=PER), ALU.add).then_inc(acc_used, 1)

                if weights:
                    for n in ("wg", "wu"):
                        dve.memset(raw[n][:, EXPERTS + 1, :], 0.0).then_inc(padded, 1)
                    dve.memset(f.wd[INTER:P, EXPERTS // 2, :], 0.0).then_inc(padded, 1)
                    dve.memset(f.wt[:, :].bitcast(FP32), 0.0).then_inc(padded, 1)
                interleave(("source", "centre", "variance", "norm", "low", "route1", "route2", "route3", "w_low", "add_up"),
                           emit, step)

            @block.gpsimd
            def _(pool):
                if weights:
                    pool.iota(iota_i[:, :, :], pattern=[[0, PER], [1, EXPERTS]], base=0, channel_multiplier=0)\
                        .then_inc(iota_made, 1)
                    pool.memset(sel[:, :, :], 0.0).then_inc(sel_made, 1)
                    for i, (half, top) in enumerate(((0, 0), (0, 32), (1, 0), (1, 32))):
                        pool.wait_ge(sel_made, i + 1)
                        v = sel[top:top + EXPERTS, :, half * INTER:(half + 1) * INTER]
                        pool.affine_select(out=v, in_=v, compare_op=ALU.not_equal, fill=1.0, base=-half,
                                           pattern=[[-2, EXPERTS // 2], [0, INTER]], channel_multiplier=1)\
                            .then_inc(sel_made, 1)
                    pool.wait_ge(sel_made, 5)

                def step(g):
                    if g is None or g == NSTEPS:
                        return
                    n, st = divmod(g, STEPS)
                    if st < LAST:
                        pool.wait_ge(gated, g + 1)
                        pool.wait_ge(wb_copied, LAST * n + st + 1)
                        wait(pool, hid_ready, g - BUFS + 1)
                        pool.tensor_tensor(prod[g % BUFS][:, :], gate[g % BUFS][:, :],
                                           wb[(LAST * n + st) % 2][:, :], ALU.mult)\
                            .then_inc(weighted, 1)

                def emit(piece, n, kind):
                    wait(pool, summed, n)
                    pool.wait_ge(before.normed, n + 1)
                    pool.tensor_tensor(grp(k.xr, n), grp(k.x, n), before.xn[:, :, :], ALU.add).then_inc(summed, 1)
                interleave(("residual",), emit, step)

            if weights or store is not None:
                @block.sync
                def _(sp):
                    if weights:
                        sp.dma_start(gate_raw[:, :], weights["gate_w"]).then_inc(loaded, 16)
                        sp.dma_start(f.gate_b[:, :], weights["gate_b"].rearrange("(e a) -> e a", a=1)).then_inc(loaded, 16)
                        for n in ("wg", "wu"):
                            sp.dma_start(raw[n][:, 0:EXPERTS, :], weights[f"experts_{n}"].rearrange("e d i -> d e i"))\
                              .then_inc(loaded, 16)
                            sp.dma_start(raw[n][:, EXPERTS, :], weights[f"shared_{n}"]).then_inc(loaded, 16)
                        sp.dma_start(f.wd[:, 0:EXPERTS // 2, :],
                                     weights["experts_wd"].rearrange("(p e) i d -> (e i) p d", e=2)).then_inc(loaded, 16)
                        sp.dma_start(f.wd[0:INTER, EXPERTS // 2, :], weights["shared_wd"]).then_inc(loaded, 16)
                        if prefetch:
                            prefetch(sp)
                        sp.wait_ge(loaded, 16 * 8)
                    if store is not None:
                        for n in range(GROUPS):
                            sp.wait_ge(acc_used, n + 1)
                            sp.dma_start(grp(store, n), grp(k.x, n)).then_inc(stored, 16)
                        sp.wait_ge(stored, 16 * GROUPS)


class StateSpaceWeights:

    def __init__(self, s, ins):
        KT = INNER // P
        self.ins, self.loaded = ins, s.sem("ssm_loaded")
        self.w_in = s.sb("w_in", [P, 2 * INNER])
        self.b_in = s.sb("b_in", [P, 2 * KT])
        self.conv_w, self.conv_b, self.skip = s.sb("conv_w", [P, KT, TAPS]), s.sb("conv_b", [P, KT]), s.sb("skip", [P, KT])
        self.w_s = {n: s.sb(f"w_{n}", [P, KT, STATE]) for n in ("dt", "B", "C")}
        self.b_s = {n: s.sb(f"b_{n}", [P, 1]) for n in ("dt", "B", "C")}
        self.w_si, self.b_si = s.sb("w_si", [P, INNER]), s.sb("b_si", [P, KT])
        self.w_out, self.b_out = s.sb("w_out", [P, KT, D]), s.sb("b_out", [P, D])
        self.count = 0

    def load(self, sp):
        def dma(dst, src):
            slow = src.ap[-1][0] != 1
            sp.dma_start(dst, src, allow_slow_non_contiguous=slow).then_inc(self.loaded, 16)
            self.count += 16

        def col(v):
            return v.rearrange("(c p) -> p c", p=P)
        ins = self.ins
        dma(self.w_in[:, :], ins["W_in"])
        dma(self.b_in[:, :], col(ins["b_in"]))
        dma(self.conv_w[:, :, :], ins["conv_w"].rearrange("(c p) t -> p c t", p=P))
        dma(self.conv_b[:, :], col(ins["conv_b"]))
        dma(self.skip[:, :], col(ins["D"]))
        for n in ("dt", "B", "C"):
            dma(self.w_s[n][:, :, :], ins[f"W_{n}"].rearrange("(c p) n -> p c n", p=P))
            for b in range(BATCH):
                dma(self.b_s[n][b * STATE:(b + 1) * STATE, :], ins[f"b_{n}"].rearrange("(p a) -> p a", a=1))
        for b in range(BATCH):
            dma(self.w_si[b * STATE:(b + 1) * STATE, :], ins["W_si"])
        dma(self.b_si[:, :], col(ins["b_si"]))
        dma(self.w_out[:, :, :], ins["W_out"].rearrange("(c p) n -> p c n", p=P))
        dma(self.b_out[:, :], ins["b_out"].partition_broadcast(P))
        sp.wait_ge(self.loaded, self.count)


def state_space(nc, k, v, z):
    KT = INNER // P
    PAD = TAPS - 1
    with Scope(nc, "ss") as s:
        ps = s.ps("ps", 8)
        w_in, b_in, conv_w, conv_b, skip = v.w_in, v.b_in, v.conv_w, v.conv_b, v.skip
        w_s, b_s, w_si, b_si, b_out = v.w_s, v.b_s, v.w_si, v.b_si, v.b_out
        w_in_hi, w_in_lo = s.sb("w_in_hi", [P, 2 * INNER], F32R), s.sb("w_in_lo", [P, 2 * INNER], F32R)
        used = [0]

        def room(n):
            used[0] += n
            return k.attn_t[:, used[0] - n:used[0]]
        xm = [room(BATCH * (SEQ + PAD)).rearrange("p (b s) -> p b s", b=BATCH) for _ in range(KT)]
        sg = [room(TOKENS) for _ in range(KT)]
        xs = [room(TOKENS) for _ in range(KT)]
        cv = s.sb("cv", [P, 2, SEQ])
        dt_t, decay, drive, state, y = [s.sb(n, [P, SEQ]) for n in ("dt_t", "decay", "drive", "state", "y")]
        y_nat = s.sb("y_nat", [P, QT * BATCH, STATE])
        y_c, y_sq = s.sb("y_c", [P, QT * BATCH, STATE]), s.sb("y_sq", [P, QT * BATCH, STATE])
        yt = s.sb("yt", [P, SEQ])
        st1, mean, var, sd, rstd = [s.sb(n, [P, QT * BATCH]) for n in ("st1", "mean", "var", "sd", "rstd")]

        split, w_ready = s.sem("split"), s.sem("w_ready")
        in_ready, in_used = s.sem("in_ready"), s.sem("in_used")
        xm_done, conv_done, conv_used, link = s.sem("xm_done"), s.sem("conv_done"), s.sem("conv_used"), s.sem("link")
        ssm_ready, dt_done, ssm_used = s.sem("ssm_ready"), s.sem("dt_done"), s.sem("ssm_used")
        y_done, nat_ready, centred, squared = s.sem("y_done"), s.sem("nat_ready"), s.sem("centred"), s.sem("squared")
        varied, rooted, normed, yt_ready, yt_done = s.sem("varied"), s.sem("rooted"), s.sem("normed"), s.sem("yt_ready"), s.sem("yt_done")
        si_ready, si_used, z_done = s.sem("si_ready"), s.sem("si_used"), s.sem("z_done")
        padded = s.sem("padded")
        N_IN = 2 * KT * GROUPS

        with nc.Block() as block:
            @block.gpsimd
            def _(pool):
                for c in range(KT):
                    pool.memset(xm[c][:, :, 0:PAD], 0.0).then_inc(padded, 1)

            @block.tensor
            def _(pe):
                pe.wait_ge(w_ready, 1)
                for m in range(2 * KT):
                    for n in range(GROUPS):
                        i = m * GROUPS + n
                        wait(pe, in_used, i - 7)
                        o, c, r = ps[i % 8][:, :], slice(m * P, (m + 1) * P), slice(n * BANK, (n + 1) * BANK)
                        pe.matmul(o, w_in_hi[:, c], k.xhi[:, r], start=True, stop=False)
                        pe.matmul(o, w_in_hi[:, c], k.xlo[:, r], start=False, stop=False)
                        pe.matmul(o, w_in_lo[:, c], k.xhi[:, r], start=False, stop=True).then_inc(in_ready, 1)
                pe.wait_ge(in_used, N_IN)
                for b in range(BATCH):
                    pe.wait_ge(conv_used, KT * (b + 1))
                    for q, name in enumerate(("dt", "B", "C")):
                        for h in range(2):
                            o = ps[2 * q + h][b * STATE:(b + 1) * STATE, :]
                            for c in range(KT):
                                at = b * SEQ + h * BANK
                                last = pe.matmul(o, w_s[name][:, c, :], xs[c][:, at:at + BANK],
                                                 start=(c == 0), stop=(c == KT - 1))
                            last.then_inc(ssm_ready, 1)
                for h in range(2):
                    pe.wait_ge(y_done, h + 1)
                    for t in range(PER):
                        at = (h * PER + t) * P
                        last = pe.transpose(ps[6 + h][:, t * P:(t + 1) * P], y[:, at:at + P], k.ident[:, :])
                    last.then_inc(nat_ready, 1)
                pe.wait_ge(normed, 1)
                for h in range(2):
                    for t in range(PER):
                        j = h * PER + t
                        last = pe.transpose(ps[h][:, t * P:(t + 1) * P],
                                            y_c[:, 2 * j:2 * j + 2, :].rearrange("p b s -> p (b s)"), k.ident[:, :])
                    last.then_inc(yt_ready, 1)
                for b in range(BATCH):
                    for h in range(2):
                        if b == 0:
                            pe.wait_ge(yt_done, h + 1)
                        for c in range(KT):
                            i = (b * 2 + h) * KT + c
                            wait(pe, si_used, i - 3)
                            pe.matmul(ps[2 + i % 4][:, :], w_si[b * STATE:(b + 1) * STATE, c * P:(c + 1) * P],
                                      yt[b * STATE:(b + 1) * STATE, h * BANK:(h + 1) * BANK],
                                      start=True, stop=True).then_inc(si_ready, 1)

            @block.scalar
            def _(act):
                act.wait_ge(v.loaded, v.count)
                act.activation(w_in_hi[:, :], w_in[:, :], ACT.Copy).then_inc(split, 1)
                for m in range(2 * KT):
                    for n in range(GROUPS):
                        i = m * GROUPS + n
                        act.wait_ge(in_ready, i + 1)
                        b, h = n // 2, n % 2
                        if m < KT:
                            act.activation(xm[m][:, b, PAD + h * BANK:PAD + (h + 1) * BANK], ps[i % 8][:, :],
                                           ACT.Identity, bias=b_in[:, m:m + 1]).then_inc(in_used, 1)
                        else:
                            act.activation(sg[m - KT][:, n * BANK:(n + 1) * BANK], ps[i % 8][:, :],
                                           ACT.Sigmoid, bias=b_in[:, m:m + 1]).then_inc(in_used, 1)
                for b in range(BATCH):
                    for c in range(KT):
                        act.wait_ge(conv_done, b * KT + c + 1)
                        act.activation(xs[c][:, b * SEQ:(b + 1) * SEQ], cv[:, c, :], ACT.Silu, bias=conv_b[:, c:c + 1])\
                           .then_inc(conv_used, 1)
                act.wait_ge(ssm_ready, 12)
                for h in range(2):
                    act.activation(dt_t[:, h * BANK:(h + 1) * BANK], ps[h][:, :], ACT.Sigmoid, bias=b_s["dt"][:, :])\
                       .then_inc(dt_done, 1)
                act.wait_ge(centred, 1)
                act.activation(y_sq[:, :, :], y_c[:, :, :], ACT.Square).then_inc(squared, 1)
                act.wait_ge(varied, 1)
                act.activation(sd[:, :], var[:, :], ACT.Sqrt).then_inc(rooted, 1)
                for h in range(2):
                    act.wait_ge(yt_ready, h + 1)
                    act.activation(yt[:, h * BANK:(h + 1) * BANK], ps[h][:, :], ACT.Copy).then_inc(yt_done, 1)

            @block.vector
            def _(dve):
                count = [0]

                def then(ins):
                    count[0] += 1
                    ins.then_inc(link, 1)
                    dve.wait_ge(link, count[0])

                dve.wait_ge(split, 1)
                dve.tensor_tensor(w_in_lo[:, :], w_in[:, :], w_in_hi[:, :].bitcast(FP32), ALU.subtract)\
                   .then_inc(w_ready, 1)
                dve.wait_ge(v.loaded, v.count)
                each = b_out[:, :].unsqueeze(1).to_broadcast([P, TILES, D])
                then(dve.tensor_tensor(k.x[:, :, :], k.x[:, :, :], each, ALU.add))
                dve.wait_ge(padded, KT)
                for b in range(BATCH):
                    for c in range(KT):
                        dve.wait_ge(in_used, (c * GROUPS) + 2 * (b + 1))
                        wait(dve, conv_used, (b - 1) * KT + c + 1)
                        o = cv[:, c, :]
                        then(dve.tensor_scalar(o, xm[c][:, b, 0:SEQ], conv_w[:, c, 0:1], None, ALU.mult))
                        then(dve.scalar_tensor_tensor(out=o, in0=xm[c][:, b, 1:SEQ + 1], scalar=conv_w[:, c, 1:2],
                                                      in1=o, op0=ALU.mult, op1=ALU.add))
                        dve.scalar_tensor_tensor(out=o, in0=xm[c][:, b, 2:SEQ + 2], scalar=conv_w[:, c, 2:3],
                                                 in1=o, op0=ALU.mult, op1=ALU.add).then_inc(conv_done, 1)
                for h in range(2):
                    r = slice(h * BANK, (h + 1) * BANK)
                    dve.wait_ge(dt_done, h + 1)
                    dve.tensor_scalar(decay[:, r], dt_t[:, r], -1.0, 1.0, ALU.mult, ALU.add)
                    then(dve.scalar_tensor_tensor(out=drive[:, r], in0=ps[2 + h][:, :], scalar=b_s["B"][:, :],
                                                  in1=dt_t[:, r], op0=ALU.add, op1=ALU.mult))
                    first = 0.0 if h == 0 else state[:, BANK - 1:BANK]
                    then(dve.tensor_tensor_scan(state[:, r], decay[:, r], drive[:, r], first, ALU.mult, ALU.add))
                    dve.scalar_tensor_tensor(out=y[:, r], in0=ps[4 + h][:, :], scalar=b_s["C"][:, :],
                                             in1=state[:, r], op0=ALU.add, op1=ALU.mult).then_inc(y_done, 1)
                for h in range(2):
                    dve.wait_ge(nat_ready, h + 1)
                    g = slice(h * PER * BATCH, (h + 1) * PER * BATCH)
                    dve.tensor_copy(y_nat[:, g, :], ps[6 + h][:, :].rearrange("p (t s) -> p t s", s=STATE))
                then(dve.engine_nop())
                then(dve.reduce_sum(st1[:, :], y_nat[:, :, :], AX.X))
                then(dve.tensor_scalar(mean[:, :], st1[:, :], 1.0 / STATE, None, ALU.mult))
                dve.tensor_tensor(y_c[:, :, :], y_nat[:, :, :], bcast(mean[:, :], STATE), ALU.subtract)\
                   .then_inc(centred, 1)
                dve.wait_ge(squared, 1)
                then(dve.reduce_sum(st1[:, :], y_sq[:, :, :], AX.X))
                dve.tensor_scalar(var[:, :], st1[:, :], 1.0 / STATE, EPS, ALU.mult, ALU.add).then_inc(varied, 1)
                dve.wait_ge(rooted, 1)
                then(dve.reciprocal(rstd[:, :], sd[:, :]))
                dve.tensor_tensor(y_c[:, :, :], y_c[:, :, :], bcast(rstd[:, :], STATE), ALU.mult).then_inc(normed, 1)
                for b in range(BATCH):
                    for h in range(2):
                        for c in range(KT):
                            i = (b * 2 + h) * KT + c
                            r = slice((b * 2 + h) * BANK, (b * 2 + h + 1) * BANK)
                            dve.wait_ge(si_ready, i + 1)
                            ins_ = dve.scalar_tensor_tensor(out=z[c][:, r], in0=xs[c][:, r], scalar=skip[:, c:c + 1],
                                                            in1=ps[2 + i % 4][:, :], op0=ALU.mult, op1=ALU.add)
                            ins_.then_inc(si_used, 1)
                            dve.wait_ge(si_used, i + 1)
                            dve.scalar_tensor_tensor(out=z[c][:, r], in0=z[c][:, r], scalar=b_si[:, c:c + 1],
                                                     in1=sg[c][:, r], op0=ALU.add, op1=ALU.mult).then_inc(z_done, 1)


class Box:
    pass


def hybrid_block_kernel(nc, ins, out, stop_after=None):
    x_view = ins["attn_a_x"].rearrange("b (t p) d -> p (b t) d", p=P)
    out_view = out.rearrange("b (t p) d -> p (b t) d", p=P)

    def pick(prefix):
        return {n[len(prefix):]: a for n, a in ins.items() if n.startswith(prefix)}

    def dump(t):
        with Scope(nc, "dump") as s:
            done = s.sem("done")
            with nc.Block() as block:
                @block.sync
                def _(sp):
                    sp.dma_start(out_view, t[:, :, :]).then_inc(done, 16)
                    sp.wait_ge(done, 16)

    with Scope(nc, "all") as s:
        k = Box()
        k.x = s.sb("x", [P, TILES, D])
        k.xhi = s.sb("xhi", [P, TOKENS], F32R)
        k.xlo = s.sb("xlo", [P, TOKENS], F32R)
        k.ident = s.sb("ident", [P, P])
        ident_made = s.sem("ident_made")
        with nc.Block() as block:
            @block.gpsimd
            def _(pool):
                pool.memset(k.ident[:, :], 0.0).then_inc(ident_made, 1)
                pool.wait_ge(ident_made, 1)
                pool.affine_select(out=k.ident[:, :], in_=k.ident[:, :], compare_op=ALU.not_equal, fill=1.0,
                                   base=0, pattern=[[-1, P]], channel_multiplier=1)

        def load_x(sp, sems):
            for n in range(GROUPS):
                sp.dma_start(k.x[:, n * PER:(n + 1) * PER, :], x_view[:, n * PER:(n + 1) * PER, :])\
                  .then_inc(sems[n], 16)

        with Scope(nc, "l1") as n1:
            k.xn = n1.sb("xn", [P, TILES, D])
            layernorm_transposed(nc, "n1", k, load=load_x)
        with Scope(nc, "a1") as a1:
            k.attn_t = a1.sb("attn_t", [P, PAIRS * BATCH * SEQ])
            attention(nc, k, ins["attn_a_W_qk"])
            with Scope(nc, "rest") as r:
                rest(nc, k, r, ins, pick, out_view, dump, stop_after)


def rest(nc, k, r, ins, pick, out_view, dump, stop_after):
    KT = INNER // P
    k.xr = r.sb("xr", [P, TILES, D])
    f = Box()
    shape = [P, EXPERTS + 2, INTER]
    f.wg_hi, f.wg_lo = r.sb("wg_hi", shape, F32R), r.sb("wg_lo", shape, F32R)
    f.wu_hi, f.wu_lo = r.sb("wu_hi", shape, F32R), r.sb("wu_lo", shape, F32R)
    f.wd = r.sb("wd", [P, STEPS, D])
    f.gate_hi, f.gate_lo = r.sb("gate_hi", [P, EXPERTS], F32R), r.sb("gate_lo", [P, EXPERTS], F32R)
    f.gate_b = r.sb("gate_b", [EXPERTS, 1])
    f.sel = r.sb("sel", [P, EXPERTS // 2, P], F32R)
    f.wt = r.sb("wt", [P, TOKENS], F32R)
    f.iota = r.sb("iota", [P, PER, EXPERTS])
    ssm = StateSpaceWeights(r, pick("attn_b_"))

    with Scope(nc, "m1w") as w:
        w_out, w_loaded = w.sb("w_out", [P, PAIRS, D]), w.sem("w_loaded")

        def load(sp):
            ssm.load(sp)

        def attention_out(pe, tile, out):
            for p in range(PAIRS):
                last = pe.matmul(out, k.attn_t[:, p * TOKENS + tile * P:p * TOKENS + (tile + 1) * P], w_out[:, p, :],
                                 start=(p == 0), stop=(p == PAIRS - 1))
            return last
        with nc.Block() as block:
            @block.sync
            def _(sp):
                sp.dma_start(w_out[:, :, :], ins["attn_a_W_out"].rearrange("(p r) n -> r p n", r=P)).then_inc(w_loaded, 16)
        mixture(nc, "m1", k, f, attention_out, source_ready=lambda pe: pe.wait_ge(w_loaded, 16),
                weights=pick("ffn_"), next_norm=True, prefetch=load)
    if stop_after == "moe":
        return dump(k.x)
    with Scope(nc, "m2w") as w:
        z = [w.sb(f"z{c}", [P, TOKENS]) for c in range(KT)]
        state_space(nc, k, ssm, z)

        def ssm_out(pe, tile, out):
            for c in range(KT):
                last = pe.matmul(out, z[c][:, tile * P:(tile + 1) * P], ssm.w_out[:, c, :],
                                 start=(c == 0), stop=(c == KT - 1))
            return last
        mixture(nc, "m2", k, f, ssm_out, store=out_view)


def kernel(**inputs):
    import numpy as np
    import concourse.bacc as bacc
    from concourse.bass_utils import run_bass_kernel_spmd

    nc = bacc.Bacc("TRN2", target_bir_lowering=False, num_devices=1)
    arrays, ins = {}, {}
    for name, a in inputs.items():
        a = np.ascontiguousarray(a)
        arrays[f"in_{name}"] = a
        ins[name[len("L0_"):]] = nc.dram_tensor(f"in_{name}", a.shape, mybir.dt.from_np(a.dtype),
                                                kind="ExternalInput").ap()
    out = nc.dram_tensor("out", (BATCH, SEQ, D), FP32, kind="ExternalOutput").ap()
    hybrid_block_kernel(nc, ins, out)
    result = run_bass_kernel_spmd(nc, [arrays], core_ids=[0])
    return result.results[0]["out"]
```

```python
from contextlib import ExitStack

import concourse.bass as bass
from concourse import mybir

FP32 = mybir.dt.float32
F32R = mybir.dt.float32r
BF16 = mybir.dt.bfloat16
I32 = mybir.dt.int32
ALU = mybir.AluOpType
ACT = mybir.ActivationFunctionType
AX = mybir.AxisListType

P = 128
BATCH, SEQ, D = 2, 1024, 128
TOKENS = BATCH * SEQ
TILES = TOKENS // P
BANK = 512
GROUPS = TOKENS // BANK
PER = BANK // P
EPS = 1e-5

HEADS, DH = 16, 64
PAIRS = HEADS // 2
QT = SEQ // P
BETA = DH ** -0.5
MASKED = -3.0e38

EXPERTS, INTER = 16, 64
STEPS = EXPERTS // 2 + 1

INNER, STATE, TAPS = 256, 64, 3


def wait(eng, sem, value):
    if not isinstance(value, int) or value > 0:
        eng.wait_ge(sem, value)


def bcast(ap, n):
    return ap.unsqueeze(2).to_broadcast([ap.shape[0], ap.shape[1], n])


class Scope:

    def __init__(self, nc, tag):
        self.nc, self.tag, self.stack = nc, tag, ExitStack()

    def __enter__(self):
        self.stack.__enter__()
        return self

    def __exit__(self, *a):
        return self.stack.__exit__(*a)

    def sb(self, name, shape, dt=FP32):
        return self.stack.enter_context(self.nc.sbuf_tensor(f"{self.tag}_{name}", shape, dt))

    def ps(self, name, n=1):
        banks = [self.stack.enter_context(self.nc.psum_tensor(f"{self.tag}_{name}{i}", [P, BANK], FP32))
                 for i in range(n)]
        return banks if n > 1 else banks[0]

    def sem(self, name):
        return self.stack.enter_context(self.nc.semaphore(f"{self.tag}_{name}"))


def layernorm_transposed(nc, s, k, load, banks, xn, sq, sync_first, vector_first, gpsimd_work):
    EARLY = GROUPS // BATCH
    tp = banks
    tot = s.sb("tot", [P, TILES])
    mean = s.sb("mean", [P, TILES])
    var = s.sb("var", [P, TILES])
    sd = s.sb("sd", [P, TILES])
    rstd = s.sb("rstd", [P, TILES])
    x_loaded = [s.sem(f"x_loaded{n}") for n in range(GROUPS)]
    summed, centred, squared = s.sem("summed"), s.sem("centred"), s.sem("squared")
    meaned, varied, rooted = s.sem("meaned"), s.sem("varied"), s.sem("rooted")
    inverted, normed = s.sem("inverted"), s.sem("normed")
    transposed, high, low = s.sem("transposed"), s.sem("high"), s.sem("low")

    def grp(t, n):
        return t[:, n * PER:(n + 1) * PER, :]

    def cols(t, n):
        return t[:, n * PER:(n + 1) * PER]

    def turn(pe, n):
        pe.wait_ge(normed, n + 1)
        for j in range(PER):
            last = pe.transpose(tp[n][:, j * P:(j + 1) * P], xn[:, n * PER + j, :], k.ident[:, :])
        last.then_inc(transposed, 1)

    def high_part(act, n):
        act.wait_ge(transposed, n + 1)
        act.activation(k.xhi[:, n * BANK:(n + 1) * BANK], tp[n][:, :], ACT.Copy).then_inc(high, 1)

    def low_part(dve, n):
        dve.wait_ge(high, n + 1)
        c = slice(n * BANK, (n + 1) * BANK)
        dve.tensor_tensor(k.xlo[:, c], tp[n][:, :], k.xhi[:, c].bitcast(FP32), ALU.subtract).then_inc(low, 1)

    with nc.Block() as block:
        @block.sync
        def _(sp):
            load(sp, x_loaded)
            sync_first(sp)

        @block.gpsimd
        def _(pool):
            gpsimd_work(pool)

        @block.vector
        def _(dve):
            vector_first(dve)
            for n in range(GROUPS):
                dve.wait_ge(x_loaded[n], 16)
                dve.reduce_sum(cols(tot, n), grp(k.x, n), AX.X).then_inc(summed, 1)
            dve.wait_ge(summed, GROUPS)
            dve.tensor_scalar(mean[:, :], tot[:, :], 1.0 / D, None, ALU.mult).then_inc(meaned, 1)
            dve.wait_ge(meaned, 1)
            for n in range(GROUPS):
                dve.tensor_tensor(grp(xn, n), grp(k.x, n), bcast(cols(mean, n), D),
                                  ALU.subtract).then_inc(centred, 1)
            for n in range(GROUPS):
                dve.wait_ge(squared, n + 1)
                dve.reduce_sum(cols(tot, n), grp(sq, n), AX.X).then_inc(summed, 1)
            dve.wait_ge(summed, 2 * GROUPS)
            dve.tensor_scalar(var[:, :], tot[:, :], 1.0 / D, EPS, ALU.mult, ALU.add).then_inc(varied, 1)
            dve.wait_ge(rooted, 1)
            dve.reciprocal(rstd[:, :], sd[:, :]).then_inc(inverted, 1)
            dve.wait_ge(inverted, 1)
            for n in range(GROUPS):
                dve.tensor_tensor(grp(xn, n), grp(xn, n), bcast(cols(rstd, n), D),
                                  ALU.mult).then_inc(normed, 1)
            for n in range(EARLY):
                low_part(dve, n)

        @block.scalar
        def _(act):
            for n in range(GROUPS):
                act.wait_ge(centred, n + 1)
                act.activation(grp(sq, n), grp(xn, n), ACT.Square).then_inc(squared, 1)
            act.wait_ge(varied, 1)
            act.activation(sd[:, :], var[:, :], ACT.Sqrt).then_inc(rooted, 1)
            for n in range(EARLY):
                high_part(act, n)

        @block.tensor
        def _(pe):
            for n in range(EARLY):
                turn(pe, n)

    def later(piece):
        def issue(eng):
            for n in range(EARLY, GROUPS):
                piece(eng, n)
        return issue
    return later(turn), later(high_part), later(low_part), low


HALF = QT // 2
SCORE_CHUNKS = [(j, j, HALF) for j in range(HALF)] + [(j, max(j, HALF), QT) for j in range(QT)]
NCHUNK = len(SCORE_CHUNKS)
DIAGONAL = [c for c, (j, a, _) in enumerate(SCORE_CHUNKS) if a == j]
SPLIT_TILES = 3
SPLIT = [c for c in range(NCHUNK) if c not in DIAGONAL and SCORE_CHUNKS[c][0] < SPLIT_TILES]
WHOLE = [c for c in range(NCHUNK) if c not in SPLIT]
FIRST_HALF_STEPS = HALF
MAX_CHUNKS = [(i, 0, i + 1) for i in range(HALF)]
for _i in range(HALF, QT):
    MAX_CHUNKS += [(_i, 0, HALF), (_i, HALF, _i + 1)]
NMAX = len(MAX_CHUNKS)
MAX_PER_STEP = [1, 1, 1, 1, 1, 2, 2, 2, 1, 0, 0, 0]
MAX_FIRST = [sum(MAX_PER_STEP[:c]) for c in range(NCHUNK)]
PROJ_STEPS = [0, 2, 4, 5]
KNAT_STEPS = [2, 8]
MROW_STEP = 9
PROLOGUE_FILLS = 7
BODY_FILLS = [5, 3, 5, 3]


def chunk_columns(kind, c):
    return P * sum(b - a for i, (_, a, b) in enumerate(SCORE_CHUNKS) if i in kind and i < c)


def attention(nc, k, w_qk, load_x, load_w_out):
    with Scope(nc, "at") as s:
        def four(name):
            return [[s.sb(f"{name}{u}{l}", [P, SEQ], F32R) for l in range(2)] for u in range(2)]
        qs, ks, q2, k2 = four("qs"), four("ks"), four("q2"), four("k2")
        probs = s.sb("probs", [P, chunk_columns(WHOLE, NCHUNK)])
        probs_hi = s.sb("probs_hi", [P, chunk_columns(SPLIT, NCHUNK)], F32R)
        probs_lo = s.sb("probs_lo", [P, chunk_columns(SPLIT, NCHUNK)], F32R)
        probs_raw = k.x[:, :, :].rearrange("p t d -> p (t d)")
        assert chunk_columns(SPLIT, NCHUNK) <= TOKENS
        k_nat = [s.sb(f"k_nat{u}", [P, QT, 3, DH]) for u in range(2)]
        k_nat_hi = [s.sb(f"k_nat_hi{u}", [P, SPLIT_TILES, 3, DH], F32R) for u in range(2)]
        k_nat_lo = [s.sb(f"k_nat_lo{u}", [P, SPLIT_TILES, 3, DH], F32R) for u in range(2)]
        k_t = k.room[:, 0:SEQ]
        w_raw = s.sb("w_raw", [P, 2, P])
        w_hi = s.sb("w_hi", [P, 2, P], F32R)
        w_lo = s.sb("w_lo", [P, 2, P], F32R)
        inv = s.sb("inv", [P, BANK])
        row_max = s.sb("row_max", [P, 2, QT])
        half_max = s.sb("half_max", [P, 2, QT - HALF, 2])
        neg_eye = s.sb("neg_eye", [QT, QT])
        maskb = s.sb("maskb", [P, P], BF16)
        identb = s.sb("identb", [P, P], BF16)
        max_ps, sc_ps, out_ps, misc = s.ps("max", 2), s.ps("sc", 2), s.ps("out", 2), s.ps("misc", 2)

        consts, pool_turns = s.sem("consts"), s.sem("pool_turns")
        rows_set, rows_set1 = s.sem("rows_set"), s.sem("rows_set1")
        w_loaded, w_split = s.sem("w_loaded"), s.sem("w_split")
        proj_ready, knat_ps_ready = s.sem("proj_ready"), s.sem("knat_ps_ready")
        hi_done, lo_done, dup_done = s.sem("hi_done"), s.sem("lo_done"), s.sem("dup_done")
        kt_done, knat_done, k_low = s.sem("kt_done"), s.sem("knat_done"), s.sem("k_low")
        knat_high, knat_low, probs_split = s.sem("knat_high"), s.sem("knat_low"), s.sem("probs_split")
        max_ready, max_taken = s.sem("max_ready"), s.sem("max_taken")
        row_max_done, row_max_t, mrow_done = s.sem("row_max_done"), s.sem("row_max_t"), s.sem("mrow_done")
        scores_ready, exp_done, masked = s.sem("scores_ready"), s.sem("exp_done"), s.sem("masked")
        av_done, ln_done = s.sem("av_done"), s.sem("ln_done")
        inv_done, out_used = s.sem("inv_done"), s.sem("out_used")

        wq_view = w_qk.rearrange("d (a c) -> d a c", a=2)

        def rows(l):
            return slice(DH * l, DH * l + DH)

        def whole(c):
            return probs[:, chunk_columns(WHOLE, c):chunk_columns(WHOLE, c + 1)]

        def part(t, c):
            return t[:, chunk_columns(SPLIT, c):chunk_columns(SPLIT, c + 1)]

        def fill_no(slot, i):
            return i if slot < 0 else PROLOGUE_FILLS + sum(BODY_FILLS[:slot]) + i

        def bank_of(slot, i):
            return fill_no(slot, i) % 2

        def fills(p):
            def unit_proj(slot, unit):
                return [(slot, i, lo_done, 4 * unit + 2 * i + 2) for i in range(2)] + \
                    [(slot, i, hi_done, 8 * unit + 2 * i + 2) for i in (2, 3)]

            def unit_knat(slot, first, unit):
                return [(slot, first, knat_low, unit + 1), (slot, first + 1, knat_done, 2 * unit + 2)]
            if p is None:
                return unit_proj(-1, 0) + unit_knat(-1, 4, 0) + [(-1, 6, mrow_done, 1)]
            found = unit_proj(0, 2 * p + 1) + [(0, 4, mrow_done, 4 * p + 2)]
            found += unit_knat(1, 0, 2 * p + 1) + [(1, 2, mrow_done, 4 * p + 3)]
            more = not is_last(p)
            found += (unit_proj(2, 2 * p + 2) if more else []) + [(2, 4, mrow_done, 4 * p + 4)]
            return found + (unit_knat(3, 0, 2 * p + 2) + [(3, 2, mrow_done, 4 * p + 5)] if more else [])

        def wait_fill_free(eng, p, slot, i):
            first = isinstance(p, int) and p == 0
            before = [] if slot < 0 else fills(None) if first else fills(p - 1)
            own = fills(None) if slot < 0 else fills(p)
            own = own[:[f[:2] for f in own].index((slot, i))]
            bank = bank_of(slot, i)
            for s_, i_, sem, value in reversed(before + own):
                if bank_of(s_, i_) == bank:
                    eng.wait_ge(sem, value)
                    break
            return bank

        def slots(emit, eng):
            for kk in range(4):
                emit(0, kk)
            with eng.Fori(1, PAIRS - 1) as p:
                for kk in range(4):
                    emit(p, kk)
            for kk in range(4):
                emit(PAIRS - 1, kk)

        def is_last(p, kk=3):
            return isinstance(p, int) and p == PAIRS - 1 and kk >= 3

        def next_unit(p, kk):
            return 2 * p + (1 if kk < 2 else 2)

        def no_prep(p, kk):
            return isinstance(p, int) and p == PAIRS - 1 and kk >= 2

        def load_w(sp, p):
            wait(sp, w_split, 2 * p)
            sp.dma_start(w_raw[:, :, :], wq_view[:, :, bass.ds(p * P, P)]).then_inc(w_loaded, 16)

        def split_w(pool, p):
            pool.wait_ge(w_loaded, 16 * (p + 1))
            wait(pool, proj_ready, 8 * p)
            pool.sem_inc(pool_turns, 1)
            pool.tensor_copy(w_hi[:, :, :], w_raw[:, :, :]).then_inc(w_split, 1)
            pool.wait_ge(w_split, 2 * p + 1)
            pool.sem_inc(pool_turns, 1)
            pool.tensor_tensor(w_lo[:, :, :], w_raw[:, :, :], w_hi[:, :, :].bitcast(FP32),
                               ALU.subtract).then_inc(w_split, 1)

        def set_up(pool):
            pool.memset(maskb[:, :], 0.0).then_inc(consts, 1)
            pool.memset(identb[:, :], 0.0).then_inc(consts, 1)
            pool.memset(neg_eye[:, :], 0.0).then_inc(consts, 1)
            for u in range(2):
                pool.memset(k_nat[u][:, :, 1, :], 1.0).then_inc(consts, 1)
                pool.memset(k_nat_hi[u][:, :, 1, :].bitcast(FP32), 1.0).then_inc(consts, 1)
                pool.memset(k_nat_lo[u][:, :, 1, :].bitcast(FP32), 0.0).then_inc(consts, 1)
            pool.wait_ge(consts, 9)
            pool.affine_select(out=maskb[:, :], in_=maskb[:, :], compare_op=ALU.is_ge, fill=MASKED,
                               base=0, pattern=[[-1, P]], channel_multiplier=1).then_inc(consts, 1)
            pool.affine_select(out=identb[:, :], in_=identb[:, :], compare_op=ALU.not_equal, fill=1.0,
                               base=0, pattern=[[-1, P]], channel_multiplier=1).then_inc(consts, 1)
            pool.affine_select(out=neg_eye[:, :], in_=neg_eye[:, :], compare_op=ALU.not_equal, fill=-1.0,
                               base=0, pattern=[[-1, QT]], channel_multiplier=1).then_inc(consts, 1)

            split_w(pool, 0)
            pool.wait_ge(w_split, 2)
            set_rows(pool, [(0, 1), (1, 0), (1, 1)], rows_set1)

        def set_rows(eng, heads, done):
            for n, (u, l) in enumerate(heads):
                o = DH * (1 - l)
                if n and eng is nc.gpsimd:
                    eng.wait_ge(done, 2 * n)
                eng.memset(q2[u][l][o:o + DH, :].bitcast(FP32), 0.0).then_inc(done, 1)
                eng.memset(k2[u][l][o:o + DH, :].bitcast(FP32), 0.0).then_inc(done, 1)
            eng.wait_ge(done, 2 * len(heads))
            for u, l in heads:
                o = DH * (1 - l)
                eng.memset(k2[u][l][o:o + QT, :].bitcast(FP32), 1.0).then_inc(done, 1)

        room = [k.attn_t[:, i * TOKENS:(i + 1) * TOKENS].rearrange("p (t d) -> p t d", t=TILES) for i in range(2)]
        turn_rest, high_rest, low_rest, x_low = layernorm_transposed(
            nc, s, k, load_x, max_ps + sc_ps, room[0], room[1], lambda sp: load_w(sp, 0),
            lambda dve: set_rows(dve, [(0, 0)], rows_set), set_up)

        with nc.Block() as block:
            @block.sync
            def _(sp):
                def duplicate(u, unit):
                    sp.wait_ge(hi_done, unit * 8 + 4)
                    for l in range(2):
                        sp.dma_start(q2[u][l][rows(l), :].bitcast(FP32),
                                     qs[u][l][rows(l), :].bitcast(FP32)).then_inc(dup_done, 16)
                    sp.wait_ge(hi_done, unit * 8 + 8)
                    for l in range(2):
                        sp.dma_start(ks[u][l][rows(1 - l), :].bitcast(FP32),
                                     ks[u][l][rows(l), :].bitcast(FP32)).then_inc(dup_done, 16)

                duplicate(0, 0)

                def body(p):
                    duplicate(1, 2 * p + 1)
                    if not is_last(p):
                        load_w(sp, p + 1)
                        duplicate(0, 2 * p + 2)
                body(0)
                with sp.Fori(1, PAIRS - 1) as p:
                    body(p)
                body(PAIRS - 1)
                sp.wait_ge(dup_done, 64 * 2 * PAIRS)
                sp.wait_ge(knat_ps_ready, 2 * 2 * PAIRS)
                sp.wait_ge(k_low, 4 * 2 * PAIRS)
                load_w_out(sp)

            @block.gpsimd
            def _(pool):
                def k_low_half(u, unit, i, before=None):
                    c = slice((i % 2) * BANK, (i % 2 + 1) * BANK)
                    pool.wait_ge(hi_done, 8 * unit + 2 * i + 2)
                    pool.sem_inc(pool_turns, 1)
                    pool.wait_ge(kt_done, 2 * unit + i - 1)
                    pool.sem_inc(pool_turns, 1)
                    for l in range(2):
                        if l == 1 or before is not None:
                            pool.wait_ge(*((k_low, 4 * unit + 2 * (i - 2) + 1) if l else before))
                            pool.sem_inc(pool_turns, 1)
                        pool.tensor_tensor(k2[u][l][rows(l), c], k_t[rows(l), c], ks[u][l][rows(l), c].bitcast(FP32),
                                           ALU.subtract).then_inc(k_low, 1)

                k_low_half(0, 0, 2)
                k_low_half(0, 0, 3, (k_low, 2))
                pool.wait_ge(k_low, 4)

                def slot(p, kk):
                    h = 4 * p + kk
                    if kk == 1 and not is_last(p):
                        split_w(pool, p + 1)
                    prepare = kk % 2 == 0 and not no_prep(p, kk)

                    def between(i, before):
                        unit = next_unit(p, kk)
                        k_low_half((kk // 2 + 1) % 2, unit, i, before)
                        pool.wait_ge(k_low, 4 * unit + 2 * (i - 1))
                        pool.sem_inc(pool_turns, 1)
                    for c in DIAGONAL:
                        if prepare and c == NCHUNK - QT // 2:
                            between(2, (masked, len(DIAGONAL) * h + DIAGONAL.index(c)))
                        pool.wait_ge(exp_done, NCHUNK * h + c + 1)
                        pool.sem_inc(pool_turns, 1)
                        v = whole(c)[:, 0:P]
                        pool.affine_select(out=v, in_=v, compare_op=ALU.is_ge, fill=0.0, base=0,
                                           pattern=[[1, P]], channel_multiplier=-1).then_inc(masked, 1)
                    if prepare:
                        between(3, (masked, len(DIAGONAL) * (h + 1)))
                slots(slot, pool)

            @block.scalar
            def _(act):
                def proj_half(p, slot_no, u, unit, i):
                    bank = bank_of(slot_no, i)
                    act.wait_ge(proj_ready, 4 * unit + i + 1)
                    c = slice((i % 2) * BANK, (i % 2 + 1) * BANK)
                    if i >= 2:
                        if i == 2:
                            wait(act, k_low, 4 * unit)
                        act.activation(k_t[:, c], misc[bank][:, :], ACT.Copy).then_inc(kt_done, 1)
                    dst = qs if i < 2 else ks
                    for l in range(2):
                        act.activation(dst[u][l][rows(l), c], misc[bank][rows(l), :], ACT.Copy)\
                           .then_inc(hi_done, 1)

                def knat_half(bank, u, unit, i):
                    act.wait_ge(knat_ps_ready, 2 * unit + i + 1)
                    src = misc[bank][:, :].rearrange("p (t l d) -> p t l d", t=HALF, l=2)
                    act.activation(k_nat[u][:, HALF * i:HALF * (i + 1), 0::2, :], src, ACT.Copy).then_inc(knat_done, 1)
                    if i == 0:
                        act.activation(k_nat_hi[u][:, :, 0::2, :], src[:, 0:SPLIT_TILES, :, :], ACT.Copy)\
                           .then_inc(knat_high, 1)

                def invert(g, l, half):
                    act.wait_ge(av_done, NCHUNK * g + (NCHUNK if half else FIRST_HALF_STEPS))
                    if half:
                        act.wait_ge(out_used, 2 * g + 1)
                    act.activation(inv[rows(l), :], out_ps[half][rows(1 - l), :], ACT.Ln).then_inc(ln_done, 1)
                    act.wait_ge(ln_done, 2 * g + half + 1)
                    act.activation(inv[rows(l), :], inv[rows(l), :], ACT.Exp, scale=-1.0)\
                       .then_inc(inv_done, 1)

                act.preload_act_table_set("natural_log_exp_and_others")
                for i in range(4):
                    proj_half(0, -1, 0, 0, i)
                high_rest(act)
                for i in range(2):
                    knat_half(bank_of(-1, 4 + i), 0, 0, i)

                def slot(p, kk):
                    h = 4 * p + kk
                    zero = isinstance(p, int) and p == 0
                    for c in range(NCHUNK):
                        act.wait_ge(scores_ready, NCHUNK * h + c + 1)
                        if not (zero and kk == 0):
                            act.wait_ge(av_done, NCHUNK * (h - 1) + c + 1)
                        _, a, b = SCORE_CHUNKS[c]
                        src = sc_ps[(NCHUNK * kk + c) % 2][:, 0:(b - a) * P]
                        if c in SPLIT:
                            act.activation(part(probs_raw, c), src, ACT.Exp, scale=BETA)
                            act.activation(part(probs_hi, c), src, ACT.Exp, scale=BETA).then_inc(exp_done, 1)
                        else:
                            act.activation(whole(c), src, ACT.Exp, scale=BETA).then_inc(exp_done, 1)
                        if c == 0 and not (zero and kk < 2):
                            invert(h - 2, kk % 2, 1)
                        if c == FIRST_HALF_STEPS and not (zero and kk == 0):
                            invert(h - 1, (kk + 1) % 2, 0)
                        if not no_prep(p, kk):
                            unit, u = next_unit(p, kk), (kk // 2 + 1) % 2
                            if kk % 2 == 0 and c - 1 in PROJ_STEPS:
                                proj_half(p, kk, u, unit, PROJ_STEPS.index(c - 1))
                            if kk % 2 == 1 and c - 1 in KNAT_STEPS:
                                i = KNAT_STEPS.index(c - 1)
                                knat_half(bank_of(kk, i), u, unit, i)
                slots(slot, act)
                invert(4 * PAIRS - 2, 0, 1)
                invert(4 * PAIRS - 1, 1, 0)
                invert(4 * PAIRS - 1, 1, 1)

            @block.vector
            def _(dve):
                def low_half(p, slot_no, u, unit, i):
                    bank = bank_of(slot_no, i)
                    c = slice(i * BANK, (i + 1) * BANK)
                    for l in range(2):
                        dve.wait_ge(hi_done, 8 * unit + 2 * i + l + 1)
                        dve.tensor_tensor(qs[u][l][rows(1 - l), c], misc[bank][rows(l), :],
                                          qs[u][l][rows(l), c].bitcast(FP32), ALU.subtract).then_inc(lo_done, 1)

                def maxima(h, kk, c):
                    i, a, b = MAX_CHUNKS[c]
                    dst = row_max[:, kk % 2, i:i + 1] if i < HALF else half_max[:, kk % 2, i - HALF, (a > 0):(a > 0) + 1]
                    dve.wait_ge(max_ready, NMAX * h + c + 1)
                    dve.reduce_max(dst, max_ps[(NMAX * kk + c) % 2][:, 0:(b - a) * P], AX.X).then_inc(max_taken, 1)

                def join_maxima(h, kk):
                    dve.wait_ge(max_taken, NMAX * (h + 1))
                    dve.reduce_max(row_max[:, kk % 2, HALF:QT], half_max[:, kk % 2, :, :], AX.X)\
                       .then_inc(row_max_done, 1)

                def max_row(h, p, slot_no, i, u, l):
                    bank = bank_of(slot_no, i)
                    dve.wait_ge(row_max_t, h + 1)
                    o = DH * (1 - l)
                    mt = misc[bank][0:QT, 0:P].unsqueeze(1).to_broadcast([QT, QT, P])
                    dve.tensor_tensor(q2[u][l][o:o + QT, :].rearrange("r (i q) -> r i q", i=QT), mt,
                                      bcast(neg_eye[:, :], P), ALU.mult)\
                       .then_inc(mrow_done, 1)

                def scale_out(g, p, kk, half):
                    l = kk % 2
                    dve.wait_ge(inv_done, 2 * g + half + 1)
                    at = p * (BATCH * SEQ) + (kk // 2) * SEQ + half * BANK
                    dve.tensor_tensor(k.attn_t[rows(l), bass.ds(at, BANK)], out_ps[half][rows(l), :],
                                      inv[rows(l), :], ALU.mult).then_inc(out_used, 1)

                def knat_low_parts(bank, u, unit):
                    dve.wait_ge(knat_high, unit + 1)
                    src = misc[bank][:, :].rearrange("p (t l d) -> p t l d", t=HALF, l=2)[:, 0:SPLIT_TILES, :, :]
                    dve.tensor_tensor(k_nat_lo[u][:, :, 0::2, :], src, k_nat_hi[u][:, :, 0::2, :].bitcast(FP32),
                                      ALU.subtract).then_inc(knat_low, 1)

                def split_probs(h, c):
                    dve.wait_ge(exp_done, NCHUNK * h + c + 1)
                    dve.tensor_tensor(part(probs_lo, c), part(probs_raw, c),
                                      part(probs_hi, c).bitcast(FP32), ALU.subtract).then_inc(probs_split, 1)

                for i in range(2):
                    low_half(0, -1, 0, 0, i)
                low_rest(dve)
                for c in range(NMAX):
                    maxima(0, 0, c)
                    if c == HALF:
                        knat_low_parts(bank_of(-1, 4), 0, 0)
                join_maxima(0, 0)
                dve.wait_ge(consts, 12)
                dve.wait_ge(rows_set, 3)
                max_row(0, 0, -1, 6, 0, 0)

                def slot(p, kk):
                    h = 4 * p + kk
                    zero = isinstance(p, int) and p == 0
                    nk = (kk + 1) % 4
                    for c in range(NCHUNK):
                        if not is_last(p, kk):
                            for m in range(MAX_FIRST[c], MAX_FIRST[c] + MAX_PER_STEP[c]):
                                maxima(h + 1, nk, m)
                        if c == 1 and not (zero and kk < 2):
                            scale_out(h - 2, p if kk >= 2 else p - 1, (kk + 2) % 4, 1)
                        if c == FIRST_HALF_STEPS + 1 and not (zero and kk == 0):
                            scale_out(h - 1, p if kk >= 1 else p - 1, (kk + 3) % 4, 0)
                        if kk % 2 == 1 and not no_prep(p, kk) and c - 2 == KNAT_STEPS[0]:
                            knat_low_parts(bank_of(kk, 0), (kk // 2 + 1) % 2, next_unit(p, kk))
                        if kk % 2 == 0 and not no_prep(p, kk) and c - 2 in PROJ_STEPS[:2]:
                            low_half(p, kk, (kk // 2 + 1) % 2, next_unit(p, kk), PROJ_STEPS.index(c - 2))
                        if c == MROW_STEP - 1 and not is_last(p, kk):
                            join_maxima(h + 1, nk)
                    if not is_last(p, kk):
                        max_row(h + 1, p, kk, BODY_FILLS[kk] - 1, nk // 2, nk % 2)
                    for c in SPLIT:
                        split_probs(h, c)
                slots(slot, dve)
                last = PAIRS - 1
                scale_out(4 * PAIRS - 2, last, 2, 1)
                scale_out(4 * PAIRS - 1, last, 3, 0)
                scale_out(4 * PAIRS - 1, last, 3, 1)

            @block.tensor
            def _(pe):
                def project(p, slot_no, b, unit, i):
                    bank = wait_fill_free(pe, p, slot_no, i)
                    a = i // 2
                    c = slice(b * SEQ + (i % 2) * BANK, b * SEQ + (i % 2 + 1) * BANK)
                    pe.matmul(misc[bank][:, :], w_hi[:, a, :], k.xhi[:, c], start=True, stop=False)
                    pe.matmul(misc[bank][:, :], w_hi[:, a, :], k.xlo[:, c], start=False, stop=False)
                    pe.matmul(misc[bank][:, :], w_lo[:, a, :], k.xhi[:, c], start=False, stop=True)\
                      .then_inc(proj_ready, 1)

                def turn_k(p, slot_no, first, unit, i):
                    bank = wait_fill_free(pe, p, slot_no, first + i)
                    pe.wait_ge(kt_done, 2 * unit + i + 1)
                    for t in range(HALF):
                        j = HALF * i + t
                        last = pe.transpose(misc[bank][:, t * P:(t + 1) * P], k_t[:, j * P:(j + 1) * P],
                                            k.ident[:, :])
                    last.then_inc(knat_ps_ready, 1)

                def max_scores(h, kk, c):
                    i, a, b = MAX_CHUNKS[c]
                    u, l = kk // 2, kk % 2
                    n = (NMAX * kk + c) % 2
                    wait(pe, max_taken, NMAX * h + c - 1)
                    diag = b == i + 1
                    pe_last = pe.matmul(max_ps[n][:, 0:(b - a) * P], qs[u][l][:, i * P:(i + 1) * P],
                                        ks[u][l][:, a * P:b * P], start=True, stop=not diag)
                    if diag:
                        o = (i - a) * P
                        pe_last = pe.matmul(max_ps[n][:, o:o + P], identb[:, :], maskb[:, :], start=False, stop=True)
                    pe_last.then_inc(max_ready, 1)

                def wait_unit(unit):
                    pe.wait_ge(hi_done, 8 * (unit + 1))
                    pe.wait_ge(lo_done, 4 * (unit + 1))
                    pe.wait_ge(dup_done, 64 * (unit + 1))

                def turn_max(h, kk, p, slot_no, i):
                    bank = wait_fill_free(pe, p, slot_no, i)
                    pe.wait_ge(row_max_done, h + 1)
                    pe.transpose(misc[bank][0:QT, 0:P], row_max[:, kk % 2, :], k.ident[:, :])\
                      .then_inc(row_max_t, 1)

                def scores(h, kk, c):
                    j, a, b = SCORE_CHUNKS[c]
                    u, l = kk // 2, kk % 2
                    n = (NCHUNK * kk + c) % 2
                    if c == 0:
                        pe.wait_ge(mrow_done, h + 1)
                        if kk % 2 == 0:
                            pe.wait_ge(k_low, 2 * (h + 2))
                    wait(pe, exp_done, NCHUNK * h + c - 1)
                    o = sc_ps[n][:, 0:(b - a) * P]
                    pe.matmul(o, ks[u][l][:, j * P:(j + 1) * P], qs[u][l][:, a * P:b * P], start=True, stop=False)
                    pe.matmul(o, k2[u][l][:, j * P:(j + 1) * P], q2[u][l][:, a * P:b * P], start=False, stop=True)\
                      .then_inc(scores_ready, 1)

                def outputs(g, kk, c):
                    j, a, b = SCORE_CHUNKS[c]
                    u, l = kk // 2, kk % 2
                    half = int(c >= FIRST_HALF_STEPS)
                    if c == 0:
                        pe.wait_ge(masked, len(DIAGONAL) * (g + 1) - 2)
                    if c >= NCHUNK - 2:
                        pe.wait_ge(masked, len(DIAGONAL) * g + DIAGONAL.index(c) + 1)
                    if c in (0, FIRST_HALF_STEPS):
                        wait(pe, out_used, 2 * g + half - 1)
                    o = (a - half * HALF) * P
                    out = out_ps[half][:, o:o + (b - a) * P]

                    def stationary(t):
                        return t[u][:, j, l:l + 2, :].rearrange("p l d -> p (l d)")
                    last = c in (FIRST_HALF_STEPS - 1, NCHUNK - 1)
                    if c in SPLIT:
                        pe.wait_ge(probs_split, len(SPLIT) * g + SPLIT.index(c) + 1)
                        pe.matmul(out, stationary(k_nat_hi), part(probs_hi, c), start=(j == 0), stop=False)
                        pe.matmul(out, stationary(k_nat_hi), part(probs_lo, c), start=False, stop=False)
                        pe.matmul(out, stationary(k_nat_lo), part(probs_hi, c), start=False, stop=last)\
                          .then_inc(av_done, 1)
                    else:
                        pe.matmul(out, stationary(k_nat), whole(c), start=(j == 0), stop=last).then_inc(av_done, 1)

                pe.wait_ge(w_split, 2)
                for i in range(4):
                    project(0, -1, 0, 0, i)
                turn_rest(pe)
                for i in range(2):
                    turn_k(0, -1, 4, 0, i)
                wait_unit(0)
                pe.wait_ge(consts, 12)
                pe.wait_ge(rows_set, 3)
                for c in range(NMAX):
                    max_scores(0, 0, c)
                turn_max(0, 0, 0, -1, 6)
                pe.wait_ge(x_low, GROUPS)

                def slot(p, kk):
                    h = 4 * p + kk
                    zero = isinstance(p, int) and p == 0
                    nk = (kk + 1) % 4
                    for c in range(NCHUNK):
                        if not (zero and kk == 0):
                            if c == 0 and kk % 2 == 1:
                                pe.wait_ge(knat_done, 2 * (2 * p + kk // 2 + 1))
                                pe.wait_ge(knat_low, 2 * p + kk // 2 + 1)
                            outputs(h - 1, (kk + 3) % 4, c)
                        scores(h, kk, c)
                        if not is_last(p, kk):
                            if c == 0 and kk % 2 == 1:
                                wait_unit(next_unit(p, kk))
                            for m in range(MAX_FIRST[c], MAX_FIRST[c] + MAX_PER_STEP[c]):
                                max_scores(h + 1, nk, m)
                        if not no_prep(p, kk):
                            unit = next_unit(p, kk)
                            if kk % 2 == 0 and c in PROJ_STEPS:
                                if kk == 2 and c == PROJ_STEPS[0]:
                                    pe.wait_ge(w_split, 2 * (p + 2))
                                project(p, kk, (kk // 2 + 1) % 2, unit, PROJ_STEPS.index(c))
                            if kk % 2 == 1 and c in KNAT_STEPS:
                                turn_k(p, kk, 0, unit, KNAT_STEPS.index(c))
                        if c == MROW_STEP and not is_last(p, kk):
                            turn_max(h + 1, nk, p, kk, BODY_FILLS[kk] - 1)
                slots(slot, pe)
                for c in range(NCHUNK):
                    outputs(4 * PAIRS - 1, 3, c)


RING = 2
BUFS = 3
LAST = STEPS - 1
NSTEPS = STEPS * GROUPS
PREPARE = dict(centre=-21, square=-19, variance=-18, root=-16, norm=-16, residual=-15, turn=-14, high=-13,
               low=-13, logits=-10, sigmoid=-9, natural=-8, route1=-8, route2=-7, route3=-6, turn_w=-3,
               w_high=-2, w_low=-3)
FINISH = dict(add_up=0, centre=2, square=4, variance=5, root=6, norm=6, turn=7, high=8, low=8)
SOURCE_TILES = [[-23, -22.8, -22.6, -22.4], [-20, -19, -18, -17], [-13, -10, -9, -8.7], [-6.4, -6.3, -6.2, -2.5]]
SOURCE_ADDED = [-22, -12.5, -8.5, -1.3]
ORDER = ["source", "add_up", "sigmoid"] + [p for p in PREPARE if p != "sigmoid"]


def agenda(pieces, with_finish, tiles=False):
    found = []
    for n in range(GROUPS):
        for piece in pieces:
            if piece == "source":
                found += [(at, piece, n, t) for t, at in enumerate(SOURCE_TILES[n])] if tiles else \
                    [(SOURCE_ADDED[n], piece, n, 0)]
            if piece in PREPARE:
                at = PREPARE[piece] + STEPS * n
                if piece == "square" and n == 1:
                    at = PREPARE["sigmoid"]
                found.append((at, piece, n, "prepare"))
            if piece in FINISH and (with_finish or piece == "add_up"):
                found.append((FINISH[piece] + STEPS * (n + 1), piece, n, "finish"))
    return sorted(found, key=lambda f: (f[0], ORDER.index(f[1])))


class GroupNorm:

    def __init__(self, s, tag):
        self.xc, self.sq, self.xn = [s.sb(f"{tag}_{n}", [P, PER, D]) for n in ("xc", "sq", "xn")]
        self.tot, self.mean, self.tot2, self.var, self.sd, self.rstd = [
            s.sb(f"{tag}_{n}", [P, PER]) for n in ("tot", "mean", "tot2", "var", "sd", "rstd")]
        self.small, self.centred, self.squared, self.varied, self.rooted, self.normed, self.turned, \
            self.high, self.low = [s.sem(f"{tag}_{n}") for n in (
                "small", "centred", "squared", "varied", "rooted", "normed", "turned", "high", "low")]

    def centre(self, dve, n, x):
        dve.reduce_sum(self.tot[:, :], x, AX.X).then_inc(self.small, 1)
        dve.wait_ge(self.small, 4 * n + 1)
        dve.tensor_scalar(self.mean[:, :], self.tot[:, :], 1.0 / D, None, ALU.mult).then_inc(self.small, 1)
        dve.wait_ge(self.small, 4 * n + 2)
        dve.tensor_tensor(self.xc[:, :, :], x, bcast(self.mean[:, :], D), ALU.subtract).then_inc(self.centred, 1)

    def variance(self, dve, n):
        dve.wait_ge(self.squared, n + 1)
        dve.reduce_sum(self.tot2[:, :], self.sq[:, :, :], AX.X).then_inc(self.small, 1)
        dve.wait_ge(self.small, 4 * n + 3)
        dve.tensor_scalar(self.var[:, :], self.tot2[:, :], 1.0 / D, EPS, ALU.mult, ALU.add).then_inc(self.varied, 1)

    def norm(self, dve, n):
        dve.wait_ge(self.rooted, n + 1)
        dve.reciprocal(self.rstd[:, :], self.sd[:, :]).then_inc(self.small, 1)
        dve.wait_ge(self.small, 4 * n + 4)
        wait(dve, self.turned, n)
        dve.tensor_tensor(self.xn[:, :, :], self.xc[:, :, :], bcast(self.rstd[:, :], D), ALU.mult)\
           .then_inc(self.normed, 1)

    def low_part(self, dve, n, lo, hi, bank):
        dve.wait_ge(self.high, n + 1)
        dve.tensor_tensor(lo, bank[:, :], hi.bitcast(FP32), ALU.subtract).then_inc(self.low, 1)

    def square(self, act, n):
        act.wait_ge(self.centred, n + 1)
        act.activation(self.sq[:, :, :], self.xc[:, :, :], ACT.Square).then_inc(self.squared, 1)

    def root(self, act, n):
        act.wait_ge(self.varied, n + 1)
        act.activation(self.sd[:, :], self.var[:, :], ACT.Sqrt).then_inc(self.rooted, 1)

    def high_part(self, act, n, hi, bank):
        act.wait_ge(self.turned, n + 1)
        act.activation(hi, bank[:, :], ACT.Copy).then_inc(self.high, 1)

    def turn(self, pe, n, bank, ident):
        pe.wait_ge(self.normed, n + 1)
        for t in range(PER):
            last = pe.transpose(bank[:, t * P:(t + 1) * P], self.xn[:, t, :], ident[:, :])
        last.then_inc(self.turned, 1)


def mixture(nc, tag, k, f, source, source_ready=None, load_x=None, weights=None, next_norm=False, store=None, ahead_of=None):
    with Scope(nc, tag) as s:
        g_ps, u_ps, wb_ps, acc, misc = s.ps("g", RING), s.ps("u", RING), s.ps("wb"), s.ps("acc"), s.ps("misc", 2)
        src_ps = [g_ps[0], g_ps[1], u_ps[0], u_ps[1]]
        gate = [s.sb(f"gate{r}", [P, BANK]) for r in range(BUFS)]
        prod = [s.sb(f"prod{r}", [P, BANK]) for r in range(BUFS)]
        hid = [s.sb(f"hid{r}", [P, BANK]) for r in range(BUFS)]
        wb = [s.sb(f"wb_copy{r}", [P, BANK]) for r in range(2)]
        wb_copied = s.sem("wb_copied")
        g_ready, u_ready, wb_ready = s.sem("g_ready"), s.sem("u_ready"), s.sem("wb_ready")
        gated, weighted = s.sem("gated"), s.sem("weighted")
        hid_ready, down_done, acc_used, stored = s.sem("hid_ready"), s.sem("down_done"), s.sem("acc_used"), s.sem("stored")
        x_loaded = [s.sem(f"x_loaded{n}") for n in range(GROUPS if load_x else 0)]
        sourced, added, summed = s.sem("sourced"), s.sem("added"), s.sem("summed")
        before, after = GroupNorm(s, "before"), GroupNorm(s, "after") if next_norm else None
        score_t = s.sb("score_t", [EXPERTS, BANK])
        full = [P, PER, EXPERTS]
        sc, eq, key, one1, one2, sc2, w1, w2, w = [
            s.sb(n, full) for n in ("sc", "eq", "key", "one1", "one2", "sc2", "w1", "w2", "w")]
        v1, v2, i1, i2, den, rec, r1, r2 = [
            s.sb(n, [P, PER]) for n in ("v1", "v2", "i1", "i2", "den", "rec", "r1", "r2")]
        logit_ready, scored, nat_ready, nat_read = [s.sem(n) for n in ("logit_ready", "scored", "nat_ready", "nat_read")]
        route_step, w_ready, wt_ready, wt_high, wt_low = [
            s.sem(n) for n in ("route_step", "w_ready", "wt_ready", "wt_high", "wt_low")]
        if weights:
            raw = {n: s.sb(f"raw_{n}", [P, EXPERTS + 2, INTER]) for n in ("wg", "wu")}
            gate_raw = s.sb("gate_raw", [P, EXPERTS])
            sel = s.sb("sel", [P, EXPERTS // 2, P])
            iota_i = s.sb("iota_i", full, I32)
            loaded, split, padded, low_split, iota_made, sel_made, const_done = [
                s.sem(n) for n in ("loaded", "split", "padded", "low_split", "iota_made", "sel_made", "const_done")]

        def grp(t, n):
            return t[:, n * PER:(n + 1) * PER, :]

        def cols(n):
            return slice(n * BANK, (n + 1) * BANK)

        def ahead(g):
            return g < NSTEPS and g % STEPS < LAST

        def interleave(pieces, emit, step, tiles=False):
            todo = agenda(pieces, next_norm, tiles)
            for g in range(-1, NSTEPS):
                if g >= 0:
                    step(g)
                while todo and todo[0][0] <= g:
                    emit(*todo.pop(0)[1:])
                if g == -1:
                    step(None)
            step(NSTEPS)
            for item in todo:
                emit(*item[1:])

        with nc.Block() as block:
            @block.tensor
            def _(pe):
                def up(out, hi, lo, st, n):
                    wh = hi[:, 2 * st:2 * st + 2, :].rearrange("p e i -> p (e i)")
                    wl = lo[:, 2 * st:2 * st + 2, :].rearrange("p e i -> p (e i)")
                    pe.matmul(out[:, :], wh, k.xhi[:, cols(n)], start=True, stop=False)
                    pe.matmul(out[:, :], wh, k.xlo[:, cols(n)], start=False, stop=False)
                    return pe.matmul(out[:, :], wl, k.xhi[:, cols(n)], start=False, stop=True)

                def down(g):
                    n, st = divmod(g, STEPS)
                    pe.wait_ge(hid_ready, g + 1)
                    if st == 0:
                        wait(pe, acc_used, n)
                    for t in range(PER):
                        last = pe.matmul(acc[:, t * P:(t + 1) * P], hid[g % BUFS][:, t * P:(t + 1) * P],
                                         f.wd[:, st, :], start=(st == 0 and t == 0), stop=(st == LAST),
                                         skip_group_check=True)
                    last.then_inc(down_done, 1)

                def spread(g):
                    n, st = divmod(g, STEPS)
                    if st == 0:
                        pe.wait_ge(wt_low, n + 1)
                    wait(pe, wb_copied, LAST * n + st)
                    pe.matmul(wb_ps[:, :], f.sel[:, st, :], f.wt[:, cols(n)],
                              start=True, stop=True).then_inc(wb_ready, 1)

                def step(g):
                    if g is None:
                        pe.wait_ge(added, 3)
                        if weights:
                            pe.wait_ge(low_split, 3)
                            pe.wait_ge(const_done, 1)
                        return
                    if g == NSTEPS:
                        down(g - 2)
                        return down(g - 1)
                    n, st = divmod(g, STEPS)
                    r = g % RING
                    if st == 0:
                        pe.wait_ge(before.low, n + 1)
                    if g == 1:
                        pe.wait_ge(added, GROUPS)
                    wait(pe, gated, g - RING + 1)
                    up(g_ps[r], f.wg_hi, f.wg_lo, st, n).then_inc(g_ready, 1)
                    if g > 0 and ahead(g + 1):
                        spread(g + 1)
                    wait(pe, hid_ready, g - RING + 1)
                    up(u_ps[r], f.wu_hi, f.wu_lo, st, n).then_inc(u_ready, 1)
                    if g == 0:
                        emit("turn_w", 0, "first")
                        spread(0)
                        spread(1)
                        emit("logits", 1, "first")
                    if g > 1:
                        down(g - 2)

                def emit(piece, n, kind):
                    if piece == "source":
                        if source_ready and n == 0 and kind == 0:
                            source_ready(pe)
                        last = source(pe, n * PER + kind, src_ps[n][:, kind * P:(kind + 1) * P])
                        if kind == PER - 1:
                            last.then_inc(sourced, 1)
                    elif piece == "turn" and kind == "prepare":
                        wait(pe, nat_read, n)
                        before.turn(pe, n, misc[0], k.ident)
                    elif piece == "turn":
                        if n == 0:
                            pe.wait_ge(before.low, GROUPS)
                        else:
                            pe.wait_ge(nat_read, GROUPS)
                            pe.wait_ge(after.low, n)
                        after.turn(pe, n, misc[0], k.ident)
                    elif piece == "logits" and (n != 1 or kind == "first"):
                        if n == 0 and weights:
                            pe.wait_ge(low_split, 1)
                        pe.wait_ge(before.low, n + 1)
                        wait(pe, wt_low, n)
                        o = misc[1][0:EXPERTS, :]
                        pe.matmul(o, f.gate_hi[:, :], k.xhi[:, cols(n)], start=True, stop=False)
                        pe.matmul(o, f.gate_hi[:, :], k.xlo[:, cols(n)], start=False, stop=False)
                        pe.matmul(o, f.gate_lo[:, :], k.xhi[:, cols(n)], start=False, stop=True)\
                          .then_inc(logit_ready, 1)
                    elif piece == "natural":
                        pe.wait_ge(scored, n + 1)
                        if next_norm:
                            wait(pe, after.low, n - 2)
                        for t in range(PER):
                            last = pe.transpose(misc[0][:, t * EXPERTS:(t + 1) * EXPERTS],
                                                score_t[:, t * P:(t + 1) * P], k.ident[0:EXPERTS, 0:EXPERTS])
                        last.then_inc(nat_ready, 1)
                    elif piece == "turn_w" and (n > 0 or kind == "first"):
                        pe.wait_ge(w_ready, n + 1)
                        for t in range(PER):
                            last = pe.transpose(misc[1][0:EXPERTS, t * P:(t + 1) * P], w[:, t, :], k.ident[:, :])
                        last.then_inc(wt_ready, 1)
                interleave(("source", "turn", "logits", "natural", "turn_w"), emit, step, tiles=True)

            @block.scalar
            def _(act):
                def copy_weights(g):
                    n, st = divmod(g, STEPS)
                    act.wait_ge(wb_ready, LAST * n + st + 1)
                    wait(act, weighted, LAST * n + st - 1)
                    act.activation(wb[(LAST * n + st) % 2][:, :], wb_ps[:, :], ACT.Copy).then_inc(wb_copied, 1)

                def step(g):
                    if g is None or g == NSTEPS:
                        return
                    if g == 0:
                        copy_weights(0)
                    act.wait_ge(g_ready, g + 1)
                    wait(act, hid_ready, g - BUFS + 1)
                    act.activation(gate[g % BUFS][:, :], g_ps[g % RING][:, :], ACT.Silu).then_inc(gated, 1)
                    if ahead(g + 1):
                        copy_weights(g + 1)

                def emit(piece, n, kind):
                    norm = before if kind == "prepare" else after
                    if piece == "square":
                        norm.square(act, n)
                        if ahead_of and n == 1 and norm is after:
                            ahead_of.split_high(act)
                    elif piece == "root":
                        norm.root(act, n)
                        if n == 0 and norm is before:
                            act.preload_act_table_set("sigmoid_and_others")
                    elif piece == "high":
                        norm.high_part(act, n, k.xhi[:, cols(n)], misc[0])
                        if weights and n == 0 and norm is before:
                            act.wait_ge(loaded, 16 * 8)
                            act.wait_ge(padded, 4)
                            act.activation(f.gate_hi[:, :], gate_raw[:, :], ACT.Copy).then_inc(split, 1)
                            act.activation(f.wg_hi[:, :, :], raw["wg"][:, :, :], ACT.Copy).then_inc(split, 1)
                            act.activation(f.wu_hi[:, :, :], raw["wu"][:, :, :], ACT.Copy).then_inc(split, 1)
                        if n == 1 and norm is before:
                            act.preload_act_table_set("silu_and_others")
                    elif piece == "sigmoid":
                        act.wait_ge(logit_ready, n + 1)
                        wait(act, nat_ready, n)
                        act.activation(score_t[:, :], misc[1][0:EXPERTS, :], ACT.Sigmoid, bias=f.gate_b[:, :])\
                           .then_inc(scored, 1)
                        if weights and n == 0:
                            act.wait_ge(sel_made, 5)
                            act.activation(f.sel[:, :, :], sel[:, :, :], ACT.Copy).then_inc(const_done, 1)
                    elif piece == "w_high":
                        act.wait_ge(wt_ready, n + 1)
                        if weights and n == 0:
                            act.wait_ge(padded, 4)
                        act.activation(f.wt[0:EXPERTS, cols(n)], misc[1][0:EXPERTS, :], ACT.Copy)\
                           .then_inc(wt_high, 1)
                interleave(("square", "root", "high", "sigmoid", "w_high"), emit, step)

            @block.vector
            def _(dve):
                count = [0]

                def then(ins):
                    count[0] += 1
                    ins.then_inc(route_step, 1)
                    dve.wait_ge(route_step, count[0])

                def largest(x, v, i, one):
                    then(dve.reduce_max(v[:, :], x[:, :, :], AX.X))
                    then(dve.tensor_tensor(eq[:, :, :], x[:, :, :], bcast(v[:, :], EXPERTS), ALU.is_equal))
                    then(dve.scalar_tensor_tensor(out=key[:, :, :], in0=eq[:, :, :], scalar=-100.0,
                                                  in1=f.iota[:, :, :], op0=ALU.mult, op1=ALU.add))
                    then(dve.tensor_reduce(i[:, :], key[:, :, :], AX.X, ALU.min))
                    then(dve.tensor_tensor(one[:, :, :], key[:, :, :], bcast(i[:, :], EXPERTS), ALU.is_equal))

                def step(g):
                    if g is None or g == NSTEPS:
                        return
                    n, st = divmod(g, STEPS)
                    r = g % BUFS
                    if st < LAST:
                        dve.wait_ge(weighted, LAST * n + st + 1)
                    else:
                        dve.wait_ge(gated, g + 1)
                    dve.wait_ge(u_ready, g + 1)
                    wait(dve, down_done, g - BUFS + 1)
                    left = prod[r] if st < LAST else gate[r]
                    dve.tensor_tensor(hid[r][:, :], left[:, :], u_ps[g % RING][:, :], ALU.mult).then_inc(hid_ready, 1)

                def emit(piece, n, kind):
                    norm = before if kind == "prepare" else after
                    if piece == "source":
                        dve.wait_ge(sourced, n + 1)
                        if load_x:
                            dve.wait_ge(x_loaded[n], 16)
                        dve.tensor_tensor(grp(k.x, n), grp(k.x, n),
                                          src_ps[n][:, :].rearrange("p (t d) -> p t d", t=PER), ALU.add)\
                           .then_inc(added, 1)
                    elif piece == "centre":
                        if norm is before:
                            dve.wait_ge(added, n + 1)
                        else:
                            dve.wait_ge(acc_used, n + 1)
                        norm.centre(dve, n, grp(k.x, n))
                    elif piece == "variance":
                        norm.variance(dve, n)
                        if ahead_of and n == 1 and norm is after:
                            ahead_of.split_low(dve)
                    elif piece == "norm":
                        if norm is before:
                            wait(dve, summed, n)
                        norm.norm(dve, n)
                    elif piece == "low":
                        norm.low_part(dve, n, k.xlo[:, cols(n)], k.xhi[:, cols(n)], misc[0])
                        if weights and n == 0 and norm is before:
                            for i, (lo, hi, src) in enumerate(((f.gate_lo[:, :], f.gate_hi[:, :], gate_raw[:, :]),
                                                               (f.wg_lo[:, :, :], f.wg_hi[:, :, :], raw["wg"][:, :, :]),
                                                               (f.wu_lo[:, :, :], f.wu_hi[:, :, :], raw["wu"][:, :, :]))):
                                dve.wait_ge(split, i + 1)
                                dve.tensor_tensor(lo, src, hi.bitcast(FP32), ALU.subtract).then_inc(low_split, 1)
                    elif piece == "route1":
                        if weights and n == 0:
                            dve.wait_ge(iota_made, 1)
                            then(dve.tensor_copy(f.iota[:, :, :], iota_i[:, :, :]))
                        dve.wait_ge(nat_ready, n + 1)
                        dve.tensor_copy(sc[:, :, :], misc[0][:, 0:PER * EXPERTS].rearrange("p (t e) -> p t e", t=PER))\
                           .then_inc(nat_read, 1)
                        dve.wait_ge(nat_read, n + 1)
                        largest(sc, v1, i1, one1)
                        then(dve.scalar_tensor_tensor(out=sc2[:, :, :], in0=one1[:, :, :], scalar=-4.0,
                                                      in1=sc[:, :, :], op0=ALU.mult, op1=ALU.add))
                    elif piece == "route2":
                        largest(sc2, v2, i2, one2)
                    elif piece == "route3":
                        then(dve.tensor_tensor(den[:, :], v1[:, :], v2[:, :], ALU.add))
                        then(dve.reciprocal(rec[:, :], den[:, :]))
                        dve.tensor_tensor(r1[:, :], v1[:, :], rec[:, :], ALU.mult)
                        then(dve.tensor_tensor(r2[:, :], v2[:, :], rec[:, :], ALU.mult))
                        dve.tensor_tensor(w1[:, :, :], one1[:, :, :], bcast(r1[:, :], EXPERTS), ALU.mult)
                        then(dve.tensor_tensor(w2[:, :, :], one2[:, :, :], bcast(r2[:, :], EXPERTS), ALU.mult))
                        wait(dve, wt_ready, n)
                        dve.tensor_tensor(w[:, :, :], w1[:, :, :], w2[:, :, :], ALU.add).then_inc(w_ready, 1)
                    elif piece == "w_low":
                        dve.wait_ge(wt_high, n + 1)
                        dve.tensor_tensor(f.wt[32:32 + EXPERTS, cols(n)], misc[1][0:EXPERTS, :],
                                          f.wt[0:EXPERTS, cols(n)].bitcast(FP32), ALU.subtract).then_inc(wt_low, 1)
                    elif piece == "add_up":
                        dve.wait_ge(down_done, STEPS * (n + 1))
                        dve.wait_ge(summed, n + 1)
                        dve.tensor_tensor(grp(k.x, n), grp(k.xr, n),
                                          acc[:, :].rearrange("p (t d) -> p t d", t=PER), ALU.add).then_inc(acc_used, 1)

                interleave(("source", "centre", "variance", "norm", "low", "route1", "route2", "route3", "w_low", "add_up"),
                           emit, step)

            @block.gpsimd
            def _(pool):
                if weights:
                    for n in ("wg", "wu"):
                        pool.memset(raw[n][:, EXPERTS + 1, :], 0.0).then_inc(padded, 1)
                    pool.memset(f.wt[:, :].bitcast(FP32), 0.0).then_inc(padded, 1)
                    pool.wait_ge(padded, 3)
                    pool.memset(f.wd[INTER:P, EXPERTS // 2, :], 0.0).then_inc(padded, 1)
                    pool.wait_ge(padded, 4)
                    pool.iota(iota_i[:, :, :], pattern=[[0, PER], [1, EXPERTS]], base=0, channel_multiplier=0)\
                        .then_inc(iota_made, 1)
                    pool.memset(sel[:, :, :], 0.0).then_inc(sel_made, 1)
                    for i, (half, top) in enumerate(((0, 0), (0, 32), (1, 0), (1, 32))):
                        pool.wait_ge(sel_made, i + 1)
                        v = sel[top:top + EXPERTS, :, half * INTER:(half + 1) * INTER]
                        pool.affine_select(out=v, in_=v, compare_op=ALU.not_equal, fill=1.0, base=-half,
                                           pattern=[[-2, EXPERTS // 2], [0, INTER]], channel_multiplier=1)\
                            .then_inc(sel_made, 1)
                    pool.wait_ge(sel_made, 5)

                def step(g):
                    if g is None or g == NSTEPS:
                        return
                    n, st = divmod(g, STEPS)
                    if st < LAST:
                        pool.wait_ge(gated, g + 1)
                        pool.wait_ge(wb_copied, LAST * n + st + 1)
                        wait(pool, hid_ready, g - BUFS + 1)
                        pool.tensor_tensor(prod[g % BUFS][:, :], gate[g % BUFS][:, :],
                                           wb[(LAST * n + st) % 2][:, :], ALU.mult)\
                            .then_inc(weighted, 1)

                def emit(piece, n, kind):
                    wait(pool, summed, n)
                    pool.wait_ge(before.normed, n + 1)
                    pool.tensor_tensor(grp(k.xr, n), grp(k.x, n), before.xn[:, :, :], ALU.add).then_inc(summed, 1)
                interleave(("residual",), emit, step)

            if weights or store is not None:
                @block.sync
                def _(sp):
                    if load_x:
                        load_x(sp, x_loaded)
                    if weights:
                        sp.dma_start(gate_raw[:, :], weights["gate_w"]).then_inc(loaded, 16)
                        sp.dma_start(f.gate_b[:, :], weights["gate_b"].rearrange("(e a) -> e a", a=1)).then_inc(loaded, 16)
                        for n in ("wg", "wu"):
                            sp.dma_start(raw[n][:, 0:EXPERTS, :], weights[f"experts_{n}"].rearrange("e d i -> d e i"))\
                              .then_inc(loaded, 16)
                            sp.dma_start(raw[n][:, EXPERTS, :], weights[f"shared_{n}"]).then_inc(loaded, 16)
                        sp.dma_start(f.wd[:, 0:EXPERTS // 2, :],
                                     weights["experts_wd"].rearrange("(p e) i d -> (e i) p d", e=2)).then_inc(loaded, 16)
                        sp.dma_start(f.wd[0:INTER, EXPERTS // 2, :], weights["shared_wd"]).then_inc(loaded, 16)
                        if ahead_of:
                            ahead_of.load(sp)
                        sp.wait_ge(loaded, 16 * 8)
                    if store is not None:
                        for n in range(GROUPS):
                            sp.wait_ge(acc_used, n + 1)
                            sp.dma_start(grp(store, n), grp(k.x, n)).then_inc(stored, 16)
                        sp.wait_ge(stored, 16 * GROUPS)


class StateSpaceWeights:

    def __init__(self, s, ins):
        KT = INNER // P
        self.ins, self.loaded, self.w_in_loaded = ins, s.sem("ssm_loaded"), s.sem("ssm_w_in_loaded")
        self.split = s.sem("ssm_split")
        self.w_in = s.sb("w_in", [P, 2 * INNER])
        self.w_in_hi, self.w_in_lo = s.sb("w_in_hi", [P, 2 * INNER], F32R), s.sb("w_in_lo", [P, 2 * INNER], F32R)
        self.b_in = s.sb("b_in", [P, 2 * KT])
        self.conv_w, self.conv_b, self.skip = s.sb("conv_w", [P, KT, TAPS]), s.sb("conv_b", [P, KT]), s.sb("skip", [P, KT])
        self.w_s = {n: s.sb(f"w_{n}", [P, KT, STATE]) for n in ("dt", "B", "C")}
        self.b_s = {n: s.sb(f"b_{n}", [P, 1]) for n in ("dt", "B", "C")}
        self.w_si, self.b_si = s.sb("w_si", [P, INNER]), s.sb("b_si", [P, KT])
        self.w_out, self.b_out = s.sb("w_out", [P, KT, D]), s.sb("b_out", [P, D])
        self.count = 0

    def load(self, sp):
        def dma(dst, src):
            slow = src.ap[-1][0] != 1
            sp.dma_start(dst, src, allow_slow_non_contiguous=slow).then_inc(self.loaded, 16)
            self.count += 16

        def col(v):
            return v.rearrange("(c p) -> p c", p=P)
        ins = self.ins
        sp.dma_start(self.w_in[:, :], ins["W_in"]).then_inc(self.w_in_loaded, 16)
        dma(self.b_in[:, :], col(ins["b_in"]))
        dma(self.conv_w[:, :, :], ins["conv_w"].rearrange("(c p) t -> p c t", p=P))
        dma(self.conv_b[:, :], col(ins["conv_b"]))
        dma(self.skip[:, :], col(ins["D"]))
        for n in ("dt", "B", "C"):
            dma(self.w_s[n][:, :, :], ins[f"W_{n}"].rearrange("(c p) n -> p c n", p=P))
            for b in range(BATCH):
                dma(self.b_s[n][b * STATE:(b + 1) * STATE, :], ins[f"b_{n}"].rearrange("(p a) -> p a", a=1))
        for b in range(BATCH):
            dma(self.w_si[b * STATE:(b + 1) * STATE, :], ins["W_si"])
        dma(self.b_si[:, :], col(ins["b_si"]))
        dma(self.w_out[:, :, :], ins["W_out"].rearrange("(c p) n -> p c n", p=P))
        dma(self.b_out[:, :], ins["b_out"].partition_broadcast(P))
        sp.wait_ge(self.loaded, self.count)

    def split_high(self, act):
        act.wait_ge(self.w_in_loaded, 16)
        act.activation(self.w_in_hi[:, :], self.w_in[:, :], ACT.Copy).then_inc(self.split, 1)

    def split_low(self, dve):
        dve.wait_ge(self.split, 1)
        dve.tensor_tensor(self.w_in_lo[:, :], self.w_in[:, :], self.w_in_hi[:, :].bitcast(FP32), ALU.subtract)


def state_space(nc, k, v, z):
    KT = INNER // P
    PAD = TAPS - 1
    SETS = BATCH * KT
    MAIN = 2 * SETS
    GATE_BANKS = 5
    with Scope(nc, "ss") as s:
        ps = s.ps("ps", 8)
        b_in, conv_w, conv_b, skip = v.b_in, v.conv_w, v.conv_b, v.skip
        w_s, b_s, w_si, b_si, b_out = v.w_s, v.b_s, v.w_si, v.b_si, v.b_out
        used = [0]

        def room(n):
            used[0] += n
            return k.attn_t[:, used[0] - n:used[0]]
        xm = [room(BATCH * (SEQ + PAD)).rearrange("p (b s) -> p b s", b=BATCH) for _ in range(KT)]
        sg = [room(TOKENS) for _ in range(KT)]
        xs = [room(TOKENS) for _ in range(KT)]
        cv = [room(SETS * BANK).rearrange("p (i s) -> p i s", i=SETS), s.sb("cv", [P, SETS, BANK])]
        dt_t, decay, drive, state, y = [s.sb(n, [P, SEQ]) for n in ("dt_t", "decay", "drive", "state", "y")]
        rows = PER * BATCH
        y_nat, y_c, y_sq = [s.sb(n, [P, 2, rows, STATE]) for n in ("y_nat", "y_c", "y_sq")]
        yt = s.sb("yt", [P, SEQ])
        st1, mean, st2, var, sd, rstd = [s.sb(n, [P, 2, rows]) for n in ("st1", "mean", "st2", "var", "sd", "rstd")]

        in_ready, in_used = s.sem("in_ready"), s.sem("in_used")
        conv_done, conv_used, link, padded = s.sem("conv_done"), s.sem("conv_used"), s.sem("link"), s.sem("padded")
        tapped = s.sem("tapped")
        ssm_ready, dt_done, skipped, biased = s.sem("ssm_ready"), s.sem("dt_done"), s.sem("skipped"), s.sem("biased")
        y_done, nat_ready, centred, squared = s.sem("y_done"), s.sem("nat_ready"), s.sem("centred"), s.sem("squared")
        varied, rooted, normed, yt_ready, yt_done = [
            s.sem(n) for n in ("varied", "rooted", "normed", "yt_ready", "yt_done")]
        si_ready, si_used = s.sem("si_ready"), s.sem("si_used")

        def fill(i):
            gate, i = divmod(i, MAIN)
            h, i = divmod(i, SETS)
            b, c = divmod(i, KT)
            return gate * KT + c, b, h

        def bank(i):
            return i if i < MAIN else 8 - GATE_BANKS + (i - MAIN) % GATE_BANKS

        def tokens(b, h):
            return slice(b * SEQ + h * BANK, b * SEQ + (h + 1) * BANK)

        def on_gpsimd(h, i):
            return h == 0 or i % 2 == 0

        def half(h):
            return slice(h * BANK, (h + 1) * BANK)

        with nc.Block() as block:
            @block.gpsimd
            def _(pool):
                for c in range(KT):
                    pool.memset(xm[c][:, :, 0:PAD], 0.0).then_inc(padded, 1)
                pool.wait_ge(v.loaded, v.count)
                for i in range(SETS):
                    b, c = divmod(i, KT)
                    pool.wait_ge(in_used, SETS + i + 1)
                    pool.tensor_scalar(cv[1][:, i, :], xm[c][:, b, BANK:2 * BANK], conv_w[:, c, 0:1], None, ALU.mult)\
                        .then_inc(tapped, 1)
                each = b_out[:, :].unsqueeze(1).to_broadcast([P, TILES, D])
                pool.tensor_tensor(k.x[:, :, :], k.x[:, :, :], each, ALU.add).then_inc(biased, 1)
                for h in range(2):
                    for i in range(SETS):
                        b, c = divmod(i, KT)
                        pool.wait_ge(conv_used, SETS * h + i + 1)
                        pool.tensor_scalar(z[c][:, tokens(b, h)], xs[c][:, tokens(b, h)], skip[:, c:c + 1],
                                           b_si[:, c:c + 1], ALU.mult, ALU.add).then_inc(skipped, 1)
                for i in range(2 * SETS):
                    h, j = divmod(i, SETS)
                    b, c = divmod(j, KT)
                    if on_gpsimd(h, j):
                        pool.wait_ge(si_used, i + 1)
                        pool.tensor_tensor(z[c][:, tokens(b, h)], z[c][:, tokens(b, h)], sg[c][:, tokens(b, h)], ALU.mult)

            @block.tensor
            def _(pe):
                def project_in(i):
                    m, b, h = fill(i)
                    if i >= MAIN:
                        pe.wait_ge(in_used, bank(i) + 1 if i < MAIN + GATE_BANKS else i - GATE_BANKS + 1)
                    o, c, r = ps[bank(i)][:, :], slice(m * P, (m + 1) * P), tokens(b, h)
                    pe.matmul(o, v.w_in_hi[:, c], k.xhi[:, r], start=True, stop=False)
                    pe.matmul(o, v.w_in_hi[:, c], k.xlo[:, r], start=False, stop=False)
                    pe.matmul(o, v.w_in_lo[:, c], k.xhi[:, r], start=False, stop=True).then_inc(in_ready, 1)

                def states(h):
                    for q, name in enumerate(("dt", "B", "C")):
                        for b in range(BATCH):
                            if q == 0:
                                pe.wait_ge(conv_used, SETS * h + KT * (b + 1))
                            for c in range(KT):
                                last = pe.matmul(ps[3 * h + q][b * STATE:(b + 1) * STATE, :], w_s[name][:, c, :],
                                                 xs[c][:, tokens(b, h)], start=(c == 0), stop=(c == KT - 1))
                        last.then_inc(ssm_ready, 1)

                def turn_y(h):
                    pe.wait_ge(y_done, h + 1)
                    for t in range(PER):
                        at = (h * PER + t) * P
                        last = pe.transpose(ps[6 + h][:, t * P:(t + 1) * P], y[:, at:at + P], k.ident[:, :])
                    last.then_inc(nat_ready, 1)

                def turn_back(h):
                    pe.wait_ge(normed, h + 1)
                    for t in range(PER):
                        last = pe.transpose(ps[6 + h][:, t * P:(t + 1) * P],
                                            y_c[:, h, 2 * t:2 * t + 2, :].rearrange("p b s -> p (b s)"), k.ident[:, :])
                    last.then_inc(yt_ready, 1)

                def project(h, sets):
                    if sets[0] == 0:
                        pe.wait_ge(yt_done, h + 1)
                    for i in sets:
                        b, c = divmod(i, KT)
                        if i >= 3:
                            pe.wait_ge(si_used, SETS * h + i - 2)
                        r = slice(b * STATE, (b + 1) * STATE)
                        pe.matmul(ps[3 * h + i % 3][:, :], w_si[r, c * P:(c + 1) * P], yt[r, half(h)],
                                  start=True, stop=True).then_inc(si_ready, 1)

                for i in range(MAIN + GATE_BANKS):
                    project_in(i)
                states(0)
                for i in range(MAIN + GATE_BANKS, 2 * MAIN):
                    project_in(i)
                pe.wait_ge(in_used, 2 * MAIN)
                turn_y(0)
                states(1)
                turn_back(0)
                project(0, range(3))
                turn_y(1)
                project(0, range(3, SETS))
                turn_back(1)
                project(1, range(SETS))

            @block.scalar
            def _(act):
                def use(i):
                    m, b, h = fill(i)
                    act.wait_ge(in_ready, i + 1)
                    dst = xm[m][:, b, PAD + h * BANK:PAD + (h + 1) * BANK] if m < KT else sg[m - KT][:, tokens(b, h)]
                    act.activation(dst, ps[bank(i)][:, :], ACT.Identity if m < KT else ACT.Sigmoid,
                                   bias=b_in[:, m:m + 1]).then_inc(in_used, 1)

                def silu(h):
                    for i in range(SETS):
                        b, c = divmod(i, KT)
                        act.wait_ge(conv_done, SETS * h + i + 1)
                        act.activation(xs[c][:, tokens(b, h)], cv[h][:, i, :], ACT.Silu, bias=conv_b[:, c:c + 1])\
                           .then_inc(conv_used, 1)

                def gates(h):
                    act.wait_ge(ssm_ready, 3 * h + 1)
                    act.activation(dt_t[:, half(h)], ps[3 * h][:, :], ACT.Sigmoid, bias=b_s["dt"][:, :])\
                       .then_inc(dt_done, 1)

                def square(h):
                    act.wait_ge(centred, h + 1)
                    act.activation(y_sq[:, h, :, :], y_c[:, h, :, :], ACT.Square).then_inc(squared, 1)

                def root(h):
                    act.wait_ge(varied, h + 1)
                    act.activation(sd[:, h, :], var[:, h, :], ACT.Sqrt).then_inc(rooted, 1)

                def copy(h):
                    act.wait_ge(yt_ready, h + 1)
                    act.activation(yt[:, half(h)], ps[6 + h][:, :], ACT.Copy).then_inc(yt_done, 1)

                act.wait_ge(v.loaded, v.count)
                for i in range(MAIN):
                    use(i)
                silu(0)
                for i in range(MAIN, 2 * MAIN):
                    use(i)
                    if i == MAIN + 1:
                        gates(0)
                silu(1)
                square(0)
                gates(1)
                root(0)
                copy(0)
                square(1)
                root(1)
                copy(1)

            @block.vector
            def _(dve):
                count = [0]

                def then(ins):
                    count[0] += 1
                    ins.then_inc(link, 1)
                    dve.wait_ge(link, count[0])

                def convolve(h):
                    for i in range(SETS):
                        b, c = divmod(i, KT)
                        dve.wait_ge(in_used, SETS * h + i + 1)
                        if h:
                            dve.wait_ge(tapped, i + 1)
                        o, at = cv[h][:, i, :], h * BANK
                        if h == 0:
                            then(dve.tensor_scalar(o, xm[c][:, b, at:at + BANK], conv_w[:, c, 0:1], None, ALU.mult))
                        then(dve.scalar_tensor_tensor(out=o, in0=xm[c][:, b, at + 1:at + 1 + BANK],
                                                      scalar=conv_w[:, c, 1:2], in1=o, op0=ALU.mult, op1=ALU.add))
                        dve.scalar_tensor_tensor(out=o, in0=xm[c][:, b, at + 2:at + 2 + BANK],
                                                 scalar=conv_w[:, c, 2:3], in1=o, op0=ALU.mult, op1=ALU.add)\
                           .then_inc(conv_done, 1)

                def scan(h):
                    r = half(h)
                    dve.wait_ge(dt_done, h + 1)
                    dve.tensor_scalar(decay[:, r], dt_t[:, r], -1.0, 1.0, ALU.mult, ALU.add)
                    dve.wait_ge(ssm_ready, 3 * h + 2)
                    then(dve.scalar_tensor_tensor(out=drive[:, r], in0=ps[3 * h + 1][:, :], scalar=b_s["B"][:, :],
                                                  in1=dt_t[:, r], op0=ALU.add, op1=ALU.mult))
                    first = 0.0 if h == 0 else state[:, BANK - 1:BANK]
                    then(dve.tensor_tensor_scan(state[:, r], decay[:, r], drive[:, r], first, ALU.mult, ALU.add))
                    dve.wait_ge(ssm_ready, 3 * h + 3)
                    dve.scalar_tensor_tensor(out=y[:, r], in0=ps[3 * h + 2][:, :], scalar=b_s["C"][:, :],
                                             in1=state[:, r], op0=ALU.add, op1=ALU.mult).then_inc(y_done, 1)

                def centre(h):
                    dve.wait_ge(nat_ready, h + 1)
                    then(dve.tensor_copy(y_nat[:, h, :, :], ps[6 + h][:, :].rearrange("p (t s) -> p t s", s=STATE)))
                    then(dve.reduce_sum(st1[:, h, :], y_nat[:, h, :, :], AX.X))
                    then(dve.tensor_scalar(mean[:, h, :], st1[:, h, :], 1.0 / STATE, None, ALU.mult))
                    dve.tensor_tensor(y_c[:, h, :, :], y_nat[:, h, :, :], bcast(mean[:, h, :], STATE), ALU.subtract)\
                       .then_inc(centred, 1)

                def variance(h):
                    dve.wait_ge(squared, h + 1)
                    then(dve.reduce_sum(st2[:, h, :], y_sq[:, h, :, :], AX.X))
                    dve.tensor_scalar(var[:, h, :], st2[:, h, :], 1.0 / STATE, EPS, ALU.mult, ALU.add)\
                       .then_inc(varied, 1)

                def norm(h):
                    dve.wait_ge(rooted, h + 1)
                    then(dve.reciprocal(rstd[:, h, :], sd[:, h, :]))
                    dve.tensor_tensor(y_c[:, h, :, :], y_c[:, h, :, :], bcast(rstd[:, h, :], STATE), ALU.mult)\
                       .then_inc(normed, 1)

                def close(h, i):
                    b, c = divmod(i, KT)
                    r = tokens(b, h)
                    dve.wait_ge(si_ready, SETS * h + i + 1)
                    dve.wait_ge(skipped, SETS * h + i + 1)
                    dve.tensor_tensor(z[c][:, r], z[c][:, r], ps[3 * h + i % 3][:, :], ALU.add).then_inc(si_used, 1)
                    if not on_gpsimd(h, i):
                        dve.wait_ge(si_used, SETS * h + i + 1)
                        dve.tensor_tensor(z[c][:, r], z[c][:, r], sg[c][:, r], ALU.mult)

                dve.wait_ge(padded, KT)
                dve.wait_ge(v.loaded, v.count)
                convolve(0)
                convolve(1)
                scan(0)
                centre(0)
                variance(0)
                scan(1)
                norm(0)
                close(0, 0)
                close(0, 1)
                centre(1)
                close(0, 2)
                variance(1)
                close(0, 3)
                norm(1)
                for i in range(SETS):
                    close(1, i)


class Box:
    pass


def hybrid_block_kernel(nc, ins, out):
    x_view = ins["attn_a_x"].rearrange("b (t p) d -> p (b t) d", p=P)
    out_view = out.rearrange("b (t p) d -> p (b t) d", p=P)

    def pick(prefix):
        return {n[len(prefix):]: a for n, a in ins.items() if n.startswith(prefix)}

    with Scope(nc, "all") as s:
        k = Box()
        k.x = s.sb("x", [P, TILES, D])
        k.xhi = s.sb("xhi", [P, TOKENS], F32R)
        k.xlo = s.sb("xlo", [P, TOKENS], F32R)
        k.ident = s.sb("ident", [P, P])
        ident_made = s.sem("ident_made")
        with nc.Block() as block:
            @block.gpsimd
            def _(pool):
                pool.memset(k.ident[:, :], 0.0).then_inc(ident_made, 1)
                pool.wait_ge(ident_made, 1)
                pool.affine_select(out=k.ident[:, :], in_=k.ident[:, :], compare_op=ALU.not_equal, fill=1.0,
                                   base=0, pattern=[[-1, P]], channel_multiplier=1)

        def load_x(sp, sems):
            for n in range(GROUPS):
                sp.dma_start(k.x[:, n * PER:(n + 1) * PER, :], x_view[:, n * PER:(n + 1) * PER, :])\
                  .then_inc(sems[n], 16)

        with Scope(nc, "a1") as a1:
            k.attn_t = a1.sb("attn_t", [P, PAIRS * BATCH * SEQ])
            k.room = a1.sb("room", [P, PAIRS * D])
            w_out_loaded = a1.sem("w_out_loaded")

            def load_w_out(sp):
                sp.dma_start(k.room[:, :].rearrange("r (p n) -> r p n", p=PAIRS),
                             ins["attn_a_W_out"].rearrange("(p r) n -> r p n", r=P)).then_inc(w_out_loaded, 16)
            attention(nc, k, ins["attn_a_W_qk"], load_x, load_w_out)
            with Scope(nc, "rest") as r:
                rest(nc, k, r, ins, pick, load_x, w_out_loaded, out_view)


def rest(nc, k, r, ins, pick, load_x, w_out_loaded, out_view):
    KT = INNER // P
    k.xr = r.sb("xr", [P, TILES, D])
    f = Box()
    shape = [P, EXPERTS + 2, INTER]
    f.wg_hi, f.wg_lo = r.sb("wg_hi", shape, F32R), r.sb("wg_lo", shape, F32R)
    f.wu_hi, f.wu_lo = r.sb("wu_hi", shape, F32R), r.sb("wu_lo", shape, F32R)
    f.wd = r.sb("wd", [P, STEPS, D])
    f.gate_hi, f.gate_lo = r.sb("gate_hi", [P, EXPERTS], F32R), r.sb("gate_lo", [P, EXPERTS], F32R)
    f.gate_b = r.sb("gate_b", [EXPERTS, 1])
    f.sel = r.sb("sel", [P, EXPERTS // 2, P], F32R)
    f.wt = r.sb("wt", [P, TOKENS], F32R)
    f.iota = r.sb("iota", [P, PER, EXPERTS])
    ssm = StateSpaceWeights(r, pick("attn_b_"))

    with Scope(nc, "m1w"):
        w_out = k.room[:, :].rearrange("r (p n) -> r p n", p=PAIRS)

        def attention_out(pe, tile, out):
            for p in range(PAIRS):
                last = pe.matmul(out, k.attn_t[:, p * TOKENS + tile * P:p * TOKENS + (tile + 1) * P], w_out[:, p, :],
                                 start=(p == 0), stop=(p == PAIRS - 1))
            return last
        mixture(nc, "m1", k, f, attention_out, source_ready=lambda pe: pe.wait_ge(w_out_loaded, 16), load_x=load_x,
                weights=pick("ffn_"), next_norm=True, ahead_of=ssm)
    with Scope(nc, "m2w") as w:
        z = [w.sb(f"z{c}", [P, TOKENS]) for c in range(KT)]
        state_space(nc, k, ssm, z)

        def ssm_out(pe, tile, out):
            for c in range(KT):
                last = pe.matmul(out, z[c][:, tile * P:(tile + 1) * P], ssm.w_out[:, c, :],
                                 start=(c == 0), stop=(c == KT - 1))
            return last
        mixture(nc, "m2", k, f, ssm_out, store=out_view)


def kernel(**inputs):
    import numpy as np
    import concourse.bacc as bacc
    from concourse.bass_utils import run_bass_kernel_spmd

    nc = bacc.Bacc("TRN2", target_bir_lowering=False, num_devices=1)
    arrays, ins = {}, {}
    for name, a in inputs.items():
        a = np.ascontiguousarray(a)
        arrays[f"in_{name}"] = a
        ins[name[len("L0_"):]] = nc.dram_tensor(f"in_{name}", a.shape, mybir.dt.from_np(a.dtype),
                                                kind="ExternalInput").ap()
    out = nc.dram_tensor("out", (BATCH, SEQ, D), FP32, kind="ExternalOutput").ap()
    hybrid_block_kernel(nc, ins, out)
    result = run_bass_kernel_spmd(nc, [arrays], core_ids=[0])
    return result.results[0]["out"]
```
